# Optimizing a Trainium2 kernel written in Bass

```python
import numpy as np
import jax
import jax.numpy as jnp

def _softmax(x, axis=-1):
    return jax.nn.softmax(x, axis=axis)

def _gelu(x):
    return jax.nn.gelu(x, approximate=True)

def _silu(x):
    return jax.nn.silu(x)

def _sigmoid(x):
    return jax.nn.sigmoid(x)

def _layernorm(x, axis=-1, eps=1e-05):
    m = jnp.mean(x, axis=axis, keepdims=True)
    v = jnp.var(x, axis=axis, keepdims=True)
    return (x - m) / jnp.sqrt(v + eps)

def _scatter_add(tgt, idx, src, axis=0):
    return tgt.at[idx].add(src)

def _segment_sum(src, seg, n):
    return jax.ops.segment_sum(src, seg, n)
kernel_name = 'mk_decoder_postln_d1_seqx_r8_197fe4'

def setup_inputs(seed: int=0):
    np.random.seed(seed)
    _w = jnp.asarray

    def _rec_inputs():
        import jax
        import jax.numpy as jnp
        _rk = jax.random.key(seed)
        x = -0.0003929 + 0.9999 * jax.random.normal(jax.random.fold_in(_rk, 1), (16, 56, 256), jnp.float32)
        _lenS = 56 - jax.random.randint(jax.random.fold_in(_rk, 7), (16,), 0, max(1, 56 // 4) + 1, jnp.int32)
        _lenS2 = 1500 - jax.random.randint(jax.random.fold_in(_rk, 8), (16,), 0, max(1, 1500 // 4) + 1, jnp.int32)
        _ctx_1024P = jax.random.normal(jax.random.fold_in(_rk, 11), (16, 16, 128), jnp.float32)
        _ctx_1024c = jax.random.dirichlet(jax.random.fold_in(_rk, 511), 0.3 * jnp.ones((16,), jnp.float32), (16, 1500))
        _ctx_1024t = jnp.einsum('bsk,bkd->bsd', _ctx_1024c, _ctx_1024P)
        _ctx_1024t = _ctx_1024t * jax.lax.rsqrt(jnp.mean(jnp.square(_ctx_1024t)) + 1e-12) * 0.953939
        ctx_1024 = 0.000227908 + 0.99994 * (_ctx_1024t + 0.3 * jax.random.normal(jax.random.fold_in(_rk, 611), (16, 1500, 128), jnp.float32))
        return (x, ctx_1024)
    x, ctx_1024 = _rec_inputs()

    def _L0_attn_setup():
        import jax, jax.numpy as jnp
        import numpy as np
        D_MODEL = 256
        N_HEADS = 16
        HEAD_DIM = D_MODEL // N_HEADS
        B, T = (2, 256)
        key = jax.random.key(seed)
        ks = jax.random.split(key, 9)
        s = 0.02
        x = jax.random.normal(ks[0], (B, T, D_MODEL), dtype=jnp.float32)
        Wq = jax.random.normal(ks[1], (N_HEADS, D_MODEL, HEAD_DIM), dtype=jnp.float32) * s
        bq = jax.random.normal(ks[2], (N_HEADS, HEAD_DIM), dtype=jnp.float32) * s
        Wk = jax.random.normal(ks[3], (N_HEADS, D_MODEL, HEAD_DIM), dtype=jnp.float32) * s
        bk = jax.random.normal(ks[4], (N_HEADS, HEAD_DIM), dtype=jnp.float32) * s
        Wv = jax.random.normal(ks[5], (N_HEADS, D_MODEL, HEAD_DIM), dtype=jnp.float32) * s
        bv = jax.random.normal(ks[6], (N_HEADS, HEAD_DIM), dtype=jnp.float32) * s
        Wo = jax.random.normal(ks[7], (D_MODEL, D_MODEL), dtype=jnp.float32) * s
        bo = jax.random.normal(ks[8], (D_MODEL,), dtype=jnp.float32) * s
        return {'x': x, 'Wq': Wq, 'bq': bq, 'Wk': Wk, 'bk': bk, 'Wv': Wv, 'bv': bv, 'Wo': Wo, 'bo': bo}
    _L0_attn_all = _L0_attn_setup()
    _L0_attn_in = {k: v for k, v in _L0_attn_all.items() if k in ('Wq', 'bq', 'Wk', 'bk', 'Wv', 'bv', 'Wo', 'bo')}
    del _L0_attn_all

    def _L0_xattn_setup():
        import jax, jax.numpy as jnp
        import numpy as np
        EPS = 1e-05

        def rmsnorm(x, g, eps=EPS):
            var = jnp.mean(jnp.square(x), axis=-1, keepdims=True)
            return x * jax.lax.rsqrt(var + eps) * g
        key = jax.random.key(seed)
        ks = jax.random.split(key, 8)
        B, Sq, Skv = (2, 512, 64)
        dim, cdim, H, D = (256, 128, 16, 128)
        inner = H * D
        s = lambda f: 1.0 / np.sqrt(f)
        return {'hidden_states': jax.random.normal(ks[0], (B, Sq, dim), jnp.float32), 'encoder_hidden_states': jax.random.normal(ks[1], (B, Skv, cdim), jnp.float32), 'Wq': jax.random.normal(ks[2], (dim, inner), jnp.float32) * s(dim), 'Wk': jax.random.normal(ks[3], (cdim, inner), jnp.float32) * s(cdim), 'Wv': jax.random.normal(ks[4], (cdim, inner), jnp.float32) * s(cdim), 'Wo': jax.random.normal(ks[5], (inner, dim), jnp.float32) * s(inner), 'gq': jnp.ones((D,), jnp.float32), 'gk': jnp.ones((D,), jnp.float32)}
    _L0_xattn_all = _L0_xattn_setup()
    _L0_xattn_in = {k: v for k, v in _L0_xattn_all.items() if k in ('Wq', 'Wk', 'Wv', 'Wo', 'gq', 'gk')}
    del _L0_xattn_all

    def _L0_ffn_setup():
        import jax, jax.numpy as jnp
        import numpy as np
        L, N, E, H, K = (256, 8, 256, 1024, 8)
        key = jax.random.key(seed)
        ks = jax.random.split(key, 6)
        return {'x': jax.random.normal(ks[0], (L, N, E), dtype=jnp.float32), 'proj1': jax.random.normal(ks[1], (H, E), dtype=jnp.float32) * 0.02, 'proj1_bias': jax.random.normal(ks[2], (H,), dtype=jnp.float32) * 0.02, 'proj2': jax.random.normal(ks[3], (E, H), dtype=jnp.float32) * 0.02, 'proj2_bias': jax.random.normal(ks[4], (E,), dtype=jnp.float32) * 0.02, 'gate_w': jax.random.normal(ks[5], (E, K), dtype=jnp.float32)}
    _L0_ffn_all = _L0_ffn_setup()
    _L0_ffn_in = {k: v for k, v in _L0_ffn_all.items() if k in ('proj1', 'proj1_bias', 'proj2', 'proj2_bias', 'gate_w')}
    del _L0_ffn_all
    return {'x': x, 'ctx_1024': ctx_1024, 'L0_attn_Wq': _L0_attn_in['Wq'], 'L0_attn_bq': _L0_attn_in['bq'], 'L0_attn_Wk': _L0_attn_in['Wk'], 'L0_attn_bk': _L0_attn_in['bk'], 'L0_attn_Wv': _L0_attn_in['Wv'], 'L0_attn_bv': _L0_attn_in['bv'], 'L0_attn_Wo': _L0_attn_in['Wo'], 'L0_attn_bo': _L0_attn_in['bo'], 'L0_xattn_Wq': _L0_xattn_in['Wq'], 'L0_xattn_Wk': _L0_xattn_in['Wk'], 'L0_xattn_Wv': _L0_xattn_in['Wv'], 'L0_xattn_Wo': _L0_xattn_in['Wo'], 'L0_xattn_gq': _L0_xattn_in['gq'], 'L0_xattn_gk': _L0_xattn_in['gk'], 'L0_ffn_proj1': _L0_ffn_in['proj1'], 'L0_ffn_proj1_bias': _L0_ffn_in['proj1_bias'], 'L0_ffn_proj2': _L0_ffn_in['proj2'], 'L0_ffn_proj2_bias': _L0_ffn_in['proj2_bias'], 'L0_ffn_gate_w': _L0_ffn_in['gate_w']}

def reference(x, ctx_1024, L0_attn_Wq, L0_attn_bq, L0_attn_Wk, L0_attn_bk, L0_attn_Wv, L0_attn_bv, L0_attn_Wo, L0_attn_bo, L0_xattn_Wq, L0_xattn_Wk, L0_xattn_Wv, L0_xattn_Wo, L0_xattn_gq, L0_xattn_gk, L0_ffn_proj1, L0_ffn_proj1_bias, L0_ffn_proj2, L0_ffn_proj2_bias, L0_ffn_gate_w):
    import jax
    import jax.numpy as jnp

    def _L0_attn_ref(x, Wq, bq, Wk, bk, Wv, bv, Wo, bo):
        import jax, jax.numpy as jnp
        import numpy as np
        D_MODEL = 256
        N_HEADS = 16
        HEAD_DIM = D_MODEL // N_HEADS
        B, T = (2, 256)
        Bn, Tn, C = x.shape
        H, _, D = Wq.shape
        scale = D ** (-0.5)
        q = jnp.einsum('btc,hcd->bhtd', x, Wq) + bq[None, :, None, :]
        k = jnp.einsum('btc,hcd->bhtd', x, Wk) + bk[None, :, None, :]
        v = jnp.einsum('btc,hcd->bhtd', x, Wv) + bv[None, :, None, :]
        scores = jnp.einsum('bhtd,bhsd->bhts', q, k) * scale
        neg = jnp.finfo(scores.dtype).min
        causal = jnp.triu(jnp.full((Tn, Tn), neg, dtype=scores.dtype), k=1)
        probs = jax.nn.softmax(scores + causal, axis=-1)
        y = jnp.einsum('bhts,bhsd->bhtd', probs, v)
        y = y.transpose(0, 2, 1, 3).reshape(Bn, Tn, H * D)
        return y @ Wo + bo

    def _L0_xattn_ref(hidden_states, encoder_hidden_states, Wq, Wk, Wv, Wo, gq, gk):
        import jax, jax.numpy as jnp
        import numpy as np
        EPS = 1e-05

        def rmsnorm(x, g, eps=EPS):
            var = jnp.mean(jnp.square(x), axis=-1, keepdims=True)
            return x * jax.lax.rsqrt(var + eps) * g
        B, Sq, _ = hidden_states.shape
        Skv = encoder_hidden_states.shape[1]
        D = gq.shape[0]
        H = Wq.shape[1] // D
        scale = 1.0 / np.sqrt(D)
        q = (hidden_states @ Wq).reshape(B, Sq, H, D)
        k = (encoder_hidden_states @ Wk).reshape(B, Skv, H, D)
        v = (encoder_hidden_states @ Wv).reshape(B, Skv, H, D)
        q = rmsnorm(q, gq)
        k = rmsnorm(k, gk)
        scores = jnp.einsum('bqhd,bkhd->bhqk', q, k) * scale
        attn = jax.nn.softmax(scores, axis=-1)
        out = jnp.einsum('bhqk,bkhd->bqhd', attn, v)
        out = out.reshape(B, Sq, H * D)
        return out @ Wo

    def _L0_ffn_ref(x, proj1, proj1_bias, proj2, proj2_bias, gate_w):
        import jax, jax.numpy as jnp
        import numpy as np
        L, N, E, H, K = (256, 8, 256, 1024, 8)
        dst = jnp.argmax(jnp.einsum('lne,ek->lnk', x, gate_w), axis=-1)
        h = jax.nn.gelu(jnp.einsum('lne,he->lnh', x, proj1) + proj1_bias, approximate=False)
        out = jnp.einsum('lnh,eh->lne', h, proj2) + proj2_bias
        del dst
        return out
    x = _layernorm(x + _L0_attn_ref(x, L0_attn_Wq, L0_attn_bq, L0_attn_Wk, L0_attn_bk, L0_attn_Wv, L0_attn_bv, L0_attn_Wo, L0_attn_bo), axis=-1)
    x = _layernorm(x + _L0_xattn_ref(x, ctx_1024, L0_xattn_Wq, L0_xattn_Wk, L0_xattn_Wv, L0_xattn_Wo, L0_xattn_gq, L0_xattn_gk), axis=-1)
    x = _layernorm(x + _L0_ffn_ref(x, L0_ffn_proj1, L0_ffn_proj1_bias, L0_ffn_proj2, L0_ffn_proj2_bias, L0_ffn_gate_w), axis=-1)
    return x

_drawn_inputs = setup_inputs


def setup_inputs(seed=0):
    import zlib

    import numpy as np

    out = dict(_drawn_inputs(seed))
    spreads = {'L0_xattn_gq': (1.0, 0.2), 'L0_xattn_gk': (1.0, 0.2)}
    factors = {'L0_attn_Wq': 8.0,
     'L0_attn_bq': 46.926,
     'L0_attn_Wk': 8.0,
     'L0_attn_bk': 64.0,
     'L0_attn_bv': 8.0,
     'L0_attn_bo': 3.269,
     'L0_ffn_proj1_bias': 8.0,
     'L0_ffn_proj2_bias': 2.942}
    for name, (base, spread) in spreads.items():
        noise = np.random.default_rng([zlib.crc32(name.encode()), seed]).standard_normal(out[name].shape)
        drawn = base * np.exp(spread * noise) if base else spread * noise
        out[name] = jnp.asarray(drawn.astype(out[name].dtype))
    for name, factor in factors.items():
        out[name] = (out[name] * factor).astype(out[name].dtype)
    return out
```

```python
import concourse.bass as bass
from concourse import mybir
from contextlib import ExitStack

F32 = mybir.dt.float32
F32R = mybir.dt.float32r
ALU = mybir.AluOpType
ACT = mybir.ActivationFunctionType
AX = mybir.AxisListType

B, T, E = 16, 56, 256
C, SK = 128, 1500
NH, HD = 16, 16
XH, XD = 16, 128
FF = 1024
P = 128
TOK = B * T
NT = TOK // P
EC = E // P
KT = 12
KP = SK // KT
UH = 8
UW = UH * T
LN_EPS = 1e-5
RMS_EPS = 1e-5
bass_max = bass.bass_isa.ReduceOp.max
TABLES = "natural_log_exp_and_others"


def rsqrt_refine(dve, link, y, a, t, gain=1.0):
    link(dve.tensor_tensor(t, y, y, ALU.mult))
    link(dve.tensor_tensor(t, t, a, ALU.mult))
    link(dve.tensor_scalar(t, t, -0.5, 1.5, ALU.mult, ALU.add))
    return dve.scalar_tensor_tensor(y, y, gain, t, ALU.mult, ALU.mult)


def linker(dve, sem):
    n = [0]

    def link(ins):
        n[0] += 1
        ins.then_inc(sem, 1)
        dve.wait_ge(sem, n[0])
    return link


def self_attention(nc, a, x1T):
    ctx = ExitStack()
    with ctx:
        def sb(name, shape, dt=F32):
            return ctx.enter_context(nc.sbuf_tensor(name, shape, dt))

        def sem(name):
            return ctx.enter_context(nc.semaphore(name))

        xT = sb("sa_xT", [P, EC, TOK])
        x_nat = sb("sa_x", [P, NT, E])
        wq = sb("sa_wq", [P, EC, E])
        wk = sb("sa_wk", [P, EC, E])
        wv = sb("sa_wv", [P, EC, E])
        wo = sb("sa_wo", [P, EC, E])
        bias = sb("sa_bias", [P, 3, EC])
        bo = sb("sa_bo", [P, E])
        ident = sb("sa_ident", [P, P])
        causal = sb("sa_causal", [P, T])
        parity = sb("sa_parity", [P, 2])
        qT = sb("sa_qT", [P, EC, TOK + 8])
        kT2 = sb("sa_kT2", [P, EC, 2, TOK])
        vbd = sb("sa_vbd", [P, B, NH // 2, 2 * HD])
        NP = 4
        probs = sb("sa_probs", [P, NP, NH, 64])
        pT = sb("sa_pT", [P, 2, NH // 2, P])
        yT = sb("sa_yT", [P, EC, TOK])
        z = sb("sa_z", [P, NT, E])
        stat = sb("sa_stat", [P, NT, 6])
        mv = sb("sa_mv", [P, NT, 2])
        rmax = sb("sa_rmax", [P, NP, NH])
        rsum = sb("sa_rsum", [P, 2, NH])
        lna = sb("sa_lna", [P, NT])
        lnl = sb("sa_lnl", [P, NT])
        lny = sb("sa_lny", [P, NT])
        lnt = sb("sa_lnt", [P, NT])
        ps = ctx.enter_context(nc.psum_tensor("sa_ps", [P, 8, 512], F32))

        qk_loaded, v_loaded, bias_loaded, x_loaded, o_loaded = (
            sem("sa_qk_loaded"), sem("sa_v_loaded"), sem("sa_bias_loaded"), sem("sa_x_loaded"), sem("sa_o_loaded"))
        cleared, xb_ready = sem("sa_cleared"), sem("sa_xb_ready")
        qT_mm, kT_mm, v_mm, qT_ready, kT_ready, v_low, v_high = (
            sem("sa_qT_mm"), sem("sa_kT_mm"), sem("sa_v_mm"), sem("sa_qT_ready"), sem("sa_kT_ready"),
            sem("sa_v_low"), sem("sa_v_high"))
        s_mm, s_masked, max_ready, shifted, exped, sum_ready, normed = (
            sem("sa_s_mm"), sem("sa_s_masked"), sem("sa_max_ready"), sem("sa_shifted"), sem("sa_exped"),
            sem("sa_sum_ready"), sem("sa_normed"))
        pT_mm, pT_ready, y_mm, yT_ready = sem("sa_pT_mm"), sem("sa_pT_ready"), sem("sa_y_mm"), sem("sa_yT_ready")
        o_mm, z_ready, stat_ready, ln_table, x1_ready, x1T_mm, x1T_ready, stored, dve_chain, act_chain = (
            sem("sa_o_mm"), sem("sa_z_ready"), sem("sa_stat_ready"), sem("sa_ln_table"), sem("sa_x1_ready"),
            sem("sa_x1T_mm"), sem("sa_x1T_ready"), sem("sa_stored"), sem("sa_dve_chain"), sem("sa_act_chain"))
        PAIRS = B // 2
        block = ctx.enter_context(nc.Block())

        @block.sync
        def _(sp):
            sp.dma_start(xT[:, :, :], a.xT.rearrange("(k p) t -> p k t", p=P)).then_inc(qk_loaded, 16)
            sp.dma_start(wq[:, :, :], a.sa_wq.rearrange("(k p) n -> p k n", p=P)).then_inc(qk_loaded, 16)
            sp.dma_start(wk[:, :, :], a.sa_wk.rearrange("(k p) n -> p k n", p=P)).then_inc(qk_loaded, 16)
            sp.dma_start(wv[:, :, :], a.sa_wv.rearrange("(k p) n -> p k n", p=P)).then_inc(v_loaded, 16)
            sp.dma_start(x_nat[:, :, :], a.x.rearrange("(n p) e -> p n e", p=P)).then_inc(x_loaded, 16)
            sp.dma_start(bo[:, :], a.sa_bo.partition_broadcast(P)).then_inc(x_loaded, 16)
            sp.dma_start(wo[:, :, :], a.sa_wo.rearrange("(k p) n -> p k n", p=P)).then_inc(o_loaded, 16)
            sp.wait_ge(x1_ready, NT)
            sp.dma_start(a.x1.rearrange("(n p) e -> p n e", p=P), z[:, :, :]).then_inc(stored, 16)
            sp.wait_ge(stored, 16)

        @block.gpsimd
        def _(pool):
            pool.memset(qT[:, :, TOK:TOK + 8], 0.0).then_inc(cleared, 1)
            pool.memset(vbd[:, :, :, :], 0.0).then_inc(cleared, 1)
            pool.memset(probs[:, :, :, :], 0.0).then_inc(cleared, 1)
            pool.wait_ge(x_loaded, 32)
            for n in range(NT):
                pool.tensor_tensor(x_nat[:, n, :], x_nat[:, n, :], bo[:, :], ALU.add).then_inc(xb_ready, 1)
            for p in range(PAIRS):
                pr = probs[:, p % NP, :, 0:T]
                pool.wait_ge(max_ready, p + 1)
                pool.tensor_tensor(pr, pr, rmax[:, p % NP, :].unsqueeze(2).broadcast_to([P, NH, T]),
                                   ALU.subtract).then_inc(shifted, 1)
                if p >= 1:
                    q = p - 1
                    pq = probs[:, q % NP, :, 0:T]
                    pool.wait_ge(sum_ready, q + 1)
                    pool.tensor_tensor(pq, pq, rsum[:, q % 2, :].unsqueeze(2).broadcast_to([P, NH, T]),
                                       ALU.mult).then_inc(normed, 1)
            q = PAIRS - 1
            pq = probs[:, q % NP, :, 0:T]
            pool.wait_ge(sum_ready, q + 1)
            pool.tensor_tensor(pq, pq, rsum[:, q % 2, :].unsqueeze(2).broadcast_to([P, NH, T]),
                               ALU.mult).then_inc(normed, 1)

        @block.scalar
        def _(act):
            act.dma_start(bias[:, :, :], a.sa_bias).then_inc(bias_loaded, 16)
            act.dma_start(parity[:, :], a.parity).then_inc(bias_loaded, 16)
            act.dma_start(causal[:, :], a.causal).then_inc(bias_loaded, 16)
            act.dma_start(ident[:, :], a.ident).then_inc(bias_loaded, 16)
            act.preload_act_table_set(TABLES)
            act.wait_ge(bias_loaded, 64)
            for m in range(4):
                i, n = divmod(m, 2)
                act.wait_ge(qT_mm, m + 1)
                act.activation(qT[:, i, n * UW:(n + 1) * UW], ps[:, m, 0:UW], ACT.Identity,
                               bias=bias[:, 0, i:i + 1]).then_inc(qT_ready, 1)
            act.wait_ge(cleared, 2)
            for m in range(4):
                act.wait_ge(v_mm, m + 1)
                act.activation(vbd[0:T, 4 * m:4 * m + 4, :, 0:HD],
                               ps[0:T, m, :].rearrange("p (b g d) -> p b g d", b=4, d=HD),
                               ACT.Copy).then_inc(v_low, 1)

            def tail(p):
                act.wait_ge(pT_mm, p + 1)
                if p >= 2:
                    act.wait_ge(y_mm, p - 1)
                act.activation(pT[:, p % 2, :, :], ps[:, 0:2, :].rearrange("p k (g q) -> p (k g) q", q=P),
                               ACT.Copy).then_inc(pT_ready, 1)

            def take_y(p):
                act.wait_ge(y_mm, p + 1)
                for i in range(EC):
                    act.activation(yT[:, i, 2 * p * T:2 * (p + 1) * T], ps[:, 2 + p % 2, i * 128:i * 128 + 2 * T],
                                   ACT.Identity, bias=bias[:, 2, i:i + 1]).then_inc(yT_ready, 1)

            for p in range(PAIRS):
                pr = probs[:, p % NP, :, 0:T]
                act.wait_ge(shifted, p + 1)
                act.activation(pr, pr, ACT.Exp).then_inc(exped, 1)
                if p >= 1:
                    tail(p - 1)
                if p >= 2:
                    take_y(p - 2)
            tail(PAIRS - 1)
            take_y(PAIRS - 2)
            take_y(PAIRS - 1)
            act.wait_ge(ln_table, 1)
            act.activation(lnl[:, :], lna[:, :], ACT.Ln).then_inc(act_chain, 1)
            act.wait_ge(act_chain, 1)
            act.activation(lny[:, :], lnl[:, :], ACT.Exp, scale=-0.5).then_inc(act_chain, 1)
            for n in range(NT):
                act.wait_ge(x1T_mm, n + 1)
                act.activation(x1T[:, :, n * P:(n + 1) * P],
                               ps[:, n % 2, 0:EC * P].rearrange("p (k t) -> p k t", k=EC),
                               ACT.Copy).then_inc(x1T_ready, 1)

        @block.vector
        def _(dve):
            link = linker(dve, dve_chain)
            dve.wait_ge(bias_loaded, 64)
            for m in range(4):
                i, n = divmod(m, 2)
                dve.wait_ge(kT_mm, m + 1)
                for par in range(2):
                    dve.tensor_scalar(kT2[:, i, par, n * UW:(n + 1) * UW], ps[:, 4 + m, 0:UW],
                                      bias[:, 1, i:i + 1], parity[:, par:par + 1],
                                      ALU.add, ALU.mult).then_inc(kT_ready, 1)
            dve.wait_ge(cleared, 2)
            for m in range(4):
                dve.wait_ge(v_mm, m + 1)
                dve.tensor_copy(vbd[64:64 + T, 4 * m:4 * m + 4, :, HD:2 * HD],
                                ps[64:64 + T, m, :].rearrange("p (b g d) -> p b g d", b=4, d=HD)
                                ).then_inc(v_high, 1)

            def head_rows(p):
                dve.wait_ge(s_mm, p + 1)
                if p == 0:
                    dve.wait_ge(cleared, 3)
                if p >= NP:
                    dve.wait_ge(pT_mm, p - NP + 1)
                for i in range(EC):
                    for o in range(2):
                        col = 2 * T * i + T * o
                        dve.scalar_tensor_tensor(
                            probs[:, p % NP, 8 * i + o:8 * i + 8:2, 0:T], ps[:, 4:8, col:col + T], HD ** -0.5,
                            causal[:, :].unsqueeze(1).broadcast_to([P, 4, T]), ALU.mult, ALU.add
                        ).then_inc(s_masked, 1)
                dve.wait_ge(s_masked, 4 * (p + 1))
                dve.tensor_reduce(rmax[:, p % NP, :], probs[:, p % NP, :, 0:T], AX.X, ALU.max).then_inc(max_ready, 1)

            def row_sums(p):
                dve.wait_ge(exped, p + 1)
                if p >= 2:
                    dve.wait_ge(normed, p - 1)
                link(dve.tensor_reduce(rsum[:, p % 2, :], probs[:, p % NP, :, 0:T], AX.X, ALU.add))
                dve.reciprocal(rsum[:, p % 2, :], rsum[:, p % 2, :]).then_inc(sum_ready, 1)

            head_rows(0)
            head_rows(1)
            for p in range(PAIRS):
                if p + 2 < PAIRS:
                    head_rows(p + 2)
                row_sums(p)
            for n in range(NT):
                dve.wait_ge(o_mm, n + 1)
                dve.wait_ge(xb_ready, n + 1)
                link(dve.tensor_tensor(z[:, n, :], ps[:, 4 + n % 4, 0:E], x_nat[:, n, :], ALU.add))
                link(dve.bn_stats(stat[:, n, :], z[:, n, :]))
                dve.bn_aggr(mv[:, n, :], stat[:, n, :]).then_inc(stat_ready, 1)
            dve.wait_ge(stat_ready, NT)
            dve.tensor_scalar(lna[:, :], mv[:, :, 1], LN_EPS, None, ALU.add).then_inc(ln_table, 1)
            dve.wait_ge(ln_table, 1)
            dve.wait_ge(act_chain, 2)
            link(rsqrt_refine(dve, link, lny[:, :], lna[:, :], lnt[:, :]))
            for n in range(NT):
                dve.tensor_scalar(z[:, n, :], z[:, n, :], mv[:, n, 0:1], lny[:, n:n + 1],
                                  ALU.subtract, ALU.mult).then_inc(x1_ready, 1)

        @block.tensor
        def _(pe):
            pe.wait_ge(qk_loaded, 48)
            for w, base, done in ((wq, 0, qT_mm), (wk, 4, kT_mm)):
                for m in range(4):
                    i, n = divmod(m, 2)
                    for k in range(EC):
                        mm = pe.matmul(ps[:, base + m, 0:UW], w[:, k, i * P:(i + 1) * P],
                                       xT[:, k, n * UW:(n + 1) * UW], start=(k == 0), stop=(k == EC - 1))
                    mm.then_inc(done, 1)
            pe.wait_ge(v_loaded, 16)
            for b in range(B):
                if b % 4 == 0:
                    pe.wait_ge(qT_ready, b // 4 + 1)
                for par in range(2):
                    for k in range(EC):
                        mm = pe.matmul(ps[64 * par:64 * par + T, b // 4, (b % 4) * P:(b % 4 + 1) * P],
                                       xT[:, k, b * T:(b + 1) * T],
                                       wv[:, k, :].rearrange("p (g q d) -> p q g d", q=2, d=HD)[:, par],
                                       start=(k == 0), stop=(k == EC - 1))
                if b % 4 == 3:
                    mm.then_inc(v_mm, 1)

            def scores(p):
                if p >= 1:
                    pe.wait_ge(s_masked, 4 * p)
                else:
                    pe.wait_ge(kT_ready, 8)
                    pe.wait_ge(qT_ready, 4)
                    pe.wait_ge(cleared, 1)
                for e in range(2):
                    b = 2 * p + e
                    for i in range(EC):
                        for r in range(4):
                            rows = slice(32 * r, 32 * r + 32)
                            col = 2 * T * i
                            mm = pe.matmul(ps[64 * e:64 * e + 64, 4 + r, col:col + 2 * T],
                                           qT[rows, i, b * T:b * T + 64], kT2[rows, i, :, b * T:(b + 1) * T],
                                           start=True, stop=True)
                mm.then_inc(s_mm, 1)

            def turn(p):
                pe.wait_ge(normed, p + 1)
                if p >= 1:
                    pe.wait_ge(pT_ready, p)
                else:
                    pe.wait_ge(v_low, 4)
                    pe.wait_ge(v_high, 4)
                    pe.wait_ge(bias_loaded, 64)
                for g in range(NH // 2):
                    mm = pe.transpose(ps[:, g // 4, (g % 4) * P:(g % 4 + 1) * P],
                                      probs[:, p % NP, 2 * g:2 * g + 2, :], ident[:, :])
                mm.then_inc(pT_mm, 1)

            def weigh(p):
                pe.wait_ge(pT_ready, p + 1)
                if p >= 2:
                    pe.wait_ge(yT_ready, 2 * (p - 1))
                for e in range(2):
                    for g in range(NH // 2):
                        r = 32 * (g % 4)
                        mm = pe.matmul(ps[r:r + 32, 2 + p % 2, (g // 4) * P + e * T:(g // 4) * P + (e + 1) * T],
                                       vbd[:, 2 * p + e, g, :], pT[:, p % 2, g, 64 * e:64 * e + T],
                                       start=True, stop=True)
                mm.then_inc(y_mm, 1)

            scores(0)
            scores(1)
            for p in range(PAIRS):
                if p + 2 < PAIRS:
                    scores(p + 2)
                turn(p)
                weigh(p)
            pe.wait_ge(o_loaded, 16)
            pe.wait_ge(s_masked, 4 * PAIRS)
            for n in range(NT):
                pe.wait_ge(yT_ready, 2 * ((n * P + P - 1) // (2 * T) + 1))
                if n >= 4:
                    pe.wait_ge(stat_ready, n - 3)
                for k in range(EC):
                    mm = pe.matmul(ps[:, 4 + n % 4, 0:E], yT[:, k, n * P:(n + 1) * P], wo[:, k, :],
                                   start=(k == 0), stop=(k == EC - 1))
                mm.then_inc(o_mm, 1)
            for n in range(NT):
                pe.wait_ge(x1_ready, n + 1)
                if n >= 2:
                    pe.wait_ge(x1T_ready, n - 1)
                for k in range(EC):
                    mm = pe.transpose(ps[:, n % 2, k * P:(k + 1) * P], z[:, n, k * P:(k + 1) * P], ident[:, :])
                mm.then_inc(x1T_mm, 1)


def query_path(nc, a, x1T, qo):
    ctx = ExitStack()
    with ctx:
        def sb(name, shape, dt=F32):
            return ctx.enter_context(nc.sbuf_tensor(name, shape, dt))

        def sem(name):
            return ctx.enter_context(nc.semaphore(name))

        wq = sb("xq_wq", [P, EC, XH * XD])
        wkT = sb("xq_wkT", [P, XH, C])
        ident = sb("xq_ident", [P, P])
        gains = sb("xq_gains", [P, 2])
        gqk = sb("xq_gqk", [P, 1])
        sq = sb("xq_sq", [P, 2, UH * XD])
        qn = sb("xq_qn", [P, 2, UH, XD])
        qhT = sb("xq_qhT", [P, 2, 4, P])
        ss = sb("xq_ss", [P, 2, UH])
        lg = sb("xq_lg", [P, 2, UH])
        rs = sb("xq_rs", [P, 2, UH])
        rt = sb("xq_rt", [P, 2, UH])
        ps = ctx.enter_context(nc.psum_tensor("xq_ps", [P, 8, 512], F32))
        wq_loaded, rest_loaded, gains_ready = sem("xq_wq_loaded"), sem("xq_rest_loaded"), sem("xq_gains_ready")
        q_mm, squared, mean_ready, table_ready, qn_ready, dve_chain, act_chain = (
            sem("xq_q_mm"), sem("xq_squared"), sem("xq_mean_ready"), sem("xq_table_ready"), sem("xq_qn_ready"),
            sem("xq_dve_chain"), sem("xq_act_chain"))
        qT_mm, qhT_ready, qp_mm, qp_ready = (
            sem("xq_qT_mm"), sem("xq_qhT_ready"), sem("xq_qp_mm"), sem("xq_qp_ready"))
        V = 2 * NT
        block = ctx.enter_context(nc.Block())

        @block.sync
        def _(sp):
            sp.dma_start(wq[:, :, :], a.xq_w.rearrange("(k p) n -> p k n", p=P)).then_inc(wq_loaded, 16)
            sp.dma_start(wkT[:, :, :], a.xk_wT.rearrange("(h d) c -> d h c", d=XD)).then_inc(rest_loaded, 16)
            sp.dma_start(ident[:, :], a.ident).then_inc(rest_loaded, 16)
            sp.dma_start(gains[:, :], a.gains).then_inc(rest_loaded, 16)

        @block.tensor
        def _(pe):
            pe.wait_ge(wq_loaded, 16)
            for v in range(V + 1):
                if v < V:
                    n, half = divmod(v, 2)
                    if v >= 2:
                        pe.wait_ge(qn_ready, v - 1)
                    for c in range(2):
                        col = (2 * half + c) * 512
                        for k in range(EC):
                            mm = pe.matmul(ps[:, 2 * (v % 2) + c, :], x1T[:, k, n * P:(n + 1) * P],
                                           wq[:, k, col:col + 512], start=(k == 0), stop=(k == EC - 1))
                    mm.then_inc(q_mm, 1)
                if v >= 1:
                    w = v - 1
                    pe.wait_ge(qn_ready, w + 1)
                    if w == 0:
                        pe.wait_ge(rest_loaded, 48)
                    for s in range(2):
                        m = 2 * w + s
                        if m >= 2:
                            pe.wait_ge(qhT_ready, m - 1)
                        for g in range(4):
                            mm = pe.transpose(ps[:, 4 + s, g * P:(g + 1) * P], qn[:, w % 2, 4 * s + g, :],
                                              ident[:, :])
                        mm.then_inc(qT_mm, 1)
                    for s in range(2):
                        m = 2 * w + s
                        pe.wait_ge(qhT_ready, m + 1)
                        if m >= 2:
                            pe.wait_ge(qp_ready, m - 1)
                        for g in range(4):
                            mm = pe.matmul(ps[:, 6 + s, g * P:(g + 1) * P], wkT[:, 8 * (w % 2) + 4 * s + g, :],
                                           qhT[:, s, g, :], start=True, stop=True)
                        mm.then_inc(qp_mm, 1)

        @block.scalar
        def _(act):
            def turn_out(w):
                for s in range(2):
                    m = 2 * w + s
                    act.wait_ge(qT_mm, m + 1)
                    if m >= 2:
                        act.wait_ge(qp_mm, m - 1)
                    act.activation(qhT[:, s, :, :], ps[:, 4 + s, :].rearrange("p (g t) -> p g t", g=4), ACT.Copy,
                                   scale=gqk[:, 0:1]).then_inc(qhT_ready, 1)

            act.wait_ge(gains_ready, 1)
            for v in range(V + 1):
                if v < V:
                    act.wait_ge(q_mm, v + 1)
                    if v >= 2:
                        act.wait_ge(mean_ready, v - 1)
                    act.activation(sq[:, v % 2, :], ps[:, 2 * (v % 2):2 * (v % 2) + 2, :].rearrange("p k n -> p (k n)"),
                                   ACT.Square).then_inc(squared, 1)
                if v >= 1:
                    turn_out(v - 1)
                if v < V:
                    act.wait_ge(mean_ready, v + 1)
                    act.activation(lg[:, v % 2, :], ss[:, v % 2, :], ACT.Ln).then_inc(act_chain, 1)
                    act.wait_ge(act_chain, v + 1)
                    act.activation(rs[:, v % 2, :], lg[:, v % 2, :], ACT.Exp, scale=-0.5).then_inc(table_ready, 1)

        @block.vector
        def _(dve):
            link = linker(dve, dve_chain)
            dve.wait_ge(rest_loaded, 48)
            dve.tensor_tensor(gqk[:, :], gains[:, 0:1], gains[:, 1:2], ALU.mult).then_inc(gains_ready, 1)
            for v in range(V + 1):
                if v < V:
                    i = v % 2
                    dve.wait_ge(squared, v + 1)
                    link(dve.tensor_reduce(ss[:, i, :], sq[:, i, :].rearrange("p (h d) -> p h d", d=XD), AX.X, ALU.add))
                    dve.tensor_scalar(ss[:, i, :], ss[:, i, :], 1.0 / XD, RMS_EPS, ALU.mult, ALU.add
                                      ).then_inc(mean_ready, 1)
                if v >= 1:
                    w = v - 1
                    n, half = divmod(w, 2)
                    for s in range(2):
                        m = 2 * w + s
                        dve.wait_ge(qp_mm, m + 1)
                        dve.tensor_copy(qo[:, 8 * half + 4 * s:8 * half + 4 * s + 4, n * P:(n + 1) * P],
                                        ps[:, 6 + s, :].rearrange("p (g t) -> p g t", g=4)).then_inc(qp_ready, 1)
                if v < V:
                    dve.wait_ge(table_ready, v + 1)
                    link(rsqrt_refine(dve, link, rs[:, i, :], ss[:, i, :], rt[:, i, :]))
                    if v >= 2:
                        dve.wait_ge(qT_mm, 2 * (v - 1))
                    dve.tensor_tensor(qn[:, i, :, :],
                                      ps[:, 2 * i:2 * i + 2, :].rearrange("p k (h d) -> p (k h) d", d=XD),
                                      rs[:, i, :].unsqueeze(2).broadcast_to([P, UH, XD]), ALU.mult
                                      ).then_inc(qn_ready, 1)


class Phase:

    def __init__(self, b=None, pair=None, i=0):
        self.b, self.pair, self.i = b, pair, i

    def shift(self, n):
        return Phase(self.b + n) if self.pair is None else Phase(None, self.pair, self.i + n)

    def at(self, per_phase, const):
        if self.pair is None:
            return per_phase * self.b + const
        return self.pair * (2 * per_phase) + (per_phase * self.i + const)

    def parity(self):
        return (self.i if self.b is None else self.b) % 2

    def within(self, first, last):
        return self.b is None or first <= self.b <= last

    def tokens(self):
        start = self.at(T, 0)
        return slice(start, start + T) if self.pair is None else bass.ds(start, T)


def each_phase(eng, body, loop_end):
    for b in (-1, 0, 1):
        body(Phase(b))
    with eng.Fori(1, loop_end // 2) as pair:
        for i in range(2):
            body(Phase(None, pair, i))
    for b in range(loop_end, B + 1):
        body(Phase(b))


def wait(eng, s, value):
    if not isinstance(value, int) or value > 0:
        eng.wait_ge(s, value)


STEPS = 2 * KT
SHIFT_LAG = KT + 2
DEN_LAG = SHIFT_LAG + 1
PV_LAG = SHIFT_LAG + 3
TD = 5
NPR = 6
WH = 6


def pos_s(ph, j):
    h, t = divmod(j, KT)
    if ph.b is not None:
        u = 2 * ph.b + h
        return KT * u + t + (u - 2 + (t > TD) if u >= 2 else 0)
    return ph.at(2 * (KT + 1), (KT + 1) * h + t - 2 + (t > TD))


def pos_d(ph, h):
    if ph.b is not None:
        u = 2 * ph.b + h
        return min(KT * u + TD + 1, STEPS * B) + u - 2
    return ph.at(2 * (KT + 1), (KT + 1) * h + TD - 1)


def bank_s(ph, j):
    h, t = divmod(j, KT)
    return pos_s(ph, j) % 2 if ph.b is not None else (h + t + (t > TD)) % 2


def bank_d(ph, h):
    return pos_d(ph, h) % 2 if ph.b is not None else (h + TD + 1) % 2


def closes(ph, j):
    return j % KT == TD and (ph.b is None or 2 <= 2 * ph.b + j // KT <= 2 * B + 1)


def lagged(ph, j, lag):
    y = j - lag
    return y if ph.b is None or 0 <= STEPS * ph.b + y < STEPS * B else None


def vector_shifts(ph):
    return ph.b is not None and ph.b >= B - 1


def split_at(ph, j):
    if j % 4 or not ph.within(-1, 14):
        return None
    if j == 20:
        return (2, 0) if ph.within(-1, 13) else None
    return (1, j // 4 + 1)


def cross_attention(nc, a, qo):
    ctx = ExitStack()
    with ctx:
        def sb(name, shape, dt=F32):
            return ctx.enter_context(nc.sbuf_tensor(name, shape, dt))

        def sem(name):
            return ctx.enter_context(nc.semaphore(name))

        wk_hi = sb("xa_wk_hi", [P, XH * XD], F32R)
        wk_lo = sb("xa_wk_lo", [P, XH * XD], F32R)
        ctxT_hi = sb("xa_ctxT_hi", [P, 2, KT, KP], F32R)
        ctxT_lo = sb("xa_ctxT_lo", [P, 2, KT, KP], F32R)
        ctxT_in = sb("xa_ctxT_in", [P, 2, KT, KP])
        ctx_nat = sb("xa_ctx_nat", [KP, 2, KT, C])
        q_hi = sb("xa_q_hi", [P, 2, UH, T], F32R)
        q_lo = sb("xa_q_lo", [P, 2, UH, T], F32R)
        scores = sb("xa_scores", [P, STEPS, UH, T])
        shifted = sb("xa_shifted", [KP, 2, UW])
        probs = sb("xa_probs", [KP, NPR, UW])
        sq = sb("xa_sq", [KP, 2, WH * XD])
        cmax = sb("xa_cmax", [KP, 2, UW])
        gmax = sb("xa_gmax", [KP, 2, UW])
        den = sb("xa_den", [KP, 2, UW])
        rden = sb("xa_rden", [P, UW])
        lden = sb("xa_lden", [P, UW])
        ss = sb("xa_ss", [KP, KT, XH])
        lg = sb("xa_lg", [KP, KT, XH])
        nt = sb("xa_nt", [KP, KT, XH])
        rk = sb("xa_rk", [KP, 2, KT, XH])
        ones = sb("xa_ones", [KP, P])
        spare = sb("xa_spare", [KP, 1])
        k_ps = ctx.enter_context(nc.psum_tensor("xa_k_ps", [P, 2, 2, 512], F32))
        s_ps = ctx.enter_context(nc.psum_tensor("xa_s_ps", [P, 2, 512], F32))
        o_ps = ctx.enter_context(nc.psum_tensor("xa_o_ps", [P, 2, 512], F32))
        wk_in = scores[:, 0:5, :, :].rearrange("p s h q -> p (s h q)")[:, 0:XH * XD]

        def score_slot(j):
            return scores[0:KP, j % STEPS, :, :].rearrange("p h q -> p (h q)")

        wk_loaded, wk_hi_ready, wk_lo_ready, ones_set = (
            sem("xa_wk_loaded"), sem("xa_wk_hi_ready"), sem("xa_wk_lo_ready"), sem("xa_ones_set"))
        ctxT_loaded = [sem(f"xa_ctxT_loaded{i}") for i in range(2)]
        nat_loaded = [sem(f"xa_nat_loaded{i}") for i in range(2)]
        hi_ready, lo_ready = sem("xa_hi_ready"), sem("xa_lo_ready")
        qhi_ready, qlo_ready = sem("xa_qhi_ready"), sem("xa_qlo_ready")
        k_done, squared, summed = sem("xa_k_done"), sem("xa_squared"), sem("xa_summed")
        mean_ready, ln_ready, table_ready, rk_ready = (
            sem("xa_mean_ready"), sem("xa_ln_ready"), sem("xa_table_ready"), sem("xa_rk_ready"))
        den_ln, den_table, den_step = (
            sem("xa_den_ln"), sem("xa_den_table"), sem("xa_den_step"))
        newton = sem("xa_newton")
        s_done, s_taken = sem("xa_s_done"), sem("xa_s_taken")
        max_done, gmax_ready = sem("xa_max_done"), sem("xa_gmax_ready")
        shift_done, exp_done, den_done, pv_done = (
            sem("xa_shift_done"), sem("xa_exp_done"), sem("xa_den_done"), sem("xa_pv_done"))
        o_taken = sem("xa_o_taken")
        block = ctx.enter_context(nc.Block())

        @block.sync
        def _(sp):
            def load_ctxT(ph):
                src = a.ctxT[ph.b] if ph.b is not None else a.ctxT[bass.ds(ph.at(1, 0), 1)].rearrange("o c k -> (o c) k")
                sp.dma_start(ctxT_in[:, ph.parity(), :, :].rearrange("c t p -> c (t p)"), src
                             ).then_inc(ctxT_loaded[ph.parity()], 16)

            def load_nat(ph):
                src = a.ctx[ph.b].rearrange("(p t) c -> p (t c)", t=KT) if ph.b is not None else \
                    a.ctx[bass.ds(ph.at(1, 0), 1)].rearrange("o (p t) c -> (o p) (t c)", t=KT)
                sp.dma_start(ctx_nat[:, ph.parity(), :, :].rearrange("p t c -> p (t c)"), src
                             ).then_inc(nat_loaded[ph.parity()], 16)

            sp.dma_start(wk_in, a.xk_w).then_inc(wk_loaded, 16)
            load_ctxT(Phase(0))
            load_ctxT(Phase(1))

            def body(ph):
                if ph.within(-1, 14):
                    wait(sp, pv_done, ph.at(STEPS, 0))
                    load_nat(ph.shift(1))
                if ph.within(-1, 12):
                    wait(sp, hi_ready, ph.at(KT // 2, KT))
                    wait(sp, lo_ready, ph.at(KT // 2, KT))
                    load_ctxT(ph.shift(3))

            each_phase(sp, body, 12)

        @block.gpsimd
        def _(pool):
            pool.memset(ones[:, :], 1.0).then_inc(ones_set, 1)
            pool.wait_ge(ones_set, 1)

            def q_low(ph, h):
                pool.wait_ge(qhi_ready, ph.at(2, h + 1))
                pool.tensor_tensor(q_lo[:, h, :, :], qo[:, UH * h:UH * h + UH, ph.tokens()],
                                   q_hi[:, h, :, :].bitcast(F32), ALU.subtract).then_inc(qlo_ready, 1)

            def body(ph):
                if ph.b == -1:
                    q_low(Phase(0), 0)
                    return
                for j in range(STEPS):
                    h, t = divmod(j, KT)
                    y = lagged(ph, j, SHIFT_LAG)
                    if y is not None and not vector_shifts(ph):
                        if y % KT == 0:
                            pool.wait_ge(gmax_ready, ph.at(2, y // KT + 1))
                        wait(pool, exp_done, ph.at(STEPS, y - 1))
                        pool.tensor_tensor(shifted[:, y % 2, :], score_slot(y), gmax[:, (y // KT) % 2, :],
                                           ALU.subtract).then_inc(shift_done, 1)
                    y = lagged(ph, j, DEN_LAG)
                    if y is not None and y % KT:
                        hy = (y // KT) % 2
                        wait(pool, exp_done, ph.at(STEPS, y + 1))
                        if y % KT == 1:
                            closing = ph if y > 0 else ph.shift(-1)
                            if closing.b is None or 2 * closing.b + hy >= 2:
                                wait(pool, s_done, pos_d(closing, hy) + 1)
                            pool.tensor_tensor(den[:, hy, :], probs[:, y % NPR, :], probs[:, (y - 1) % NPR, :], ALU.add
                                               ).then_inc(den_done, 2)
                        else:
                            wait(pool, den_done, ph.at(STEPS, y))
                            pool.tensor_tensor(den[:, hy, :], probs[:, y % NPR, :], den[:, hy, :], ALU.add
                                               ).then_inc(den_done, 1)
                    if ph.within(0, 15) and t == KT - 1:
                        wait(pool, max_done, ph.at(2 * (KT - 1), (KT - 1) * (h + 1)))
                        wait(pool, shift_done, ph.at(STEPS, KT * (h - 1)))
                        pool.tensor_tensor(spare[:, :], ones[:, 0:1], ones[:, 1:2], ALU.mult)
                        pool.partition_all_reduce(gmax[:, h, :], cmax[:, h, :], KP, bass_max
                                                  ).then_inc(gmax_ready, 1)
                    if t == 6 and ph.within(0, 15) and not (ph.b == 15 and h == 1):
                        q_low(ph.shift(h), 1 - h)

            each_phase(pool, body, 14)

        @block.scalar
        def _(act):
            act.preload_act_table_set(TABLES)

            def q_high(ph, h):
                act.activation(q_hi[:, h, :, :], qo[:, UH * h:UH * h + UH, ph.tokens()], ACT.Copy
                               ).then_inc(qhi_ready, 1)

            def split_high(ph, c):
                i = ph.parity()
                act.wait_ge(ctxT_loaded[i], 16 * (ph.b // 2 + 1) if ph.b is not None else
                            ph.pair * 16 + 16 * (ph.i // 2 + 1))
                if ph.within(2, B):
                    act.wait_ge(s_done, pos_s(ph.shift(-2), KT + 2 * c + 1) + 1)
                act.activation(ctxT_hi[:, i, 2 * c:2 * c + 2, :], ctxT_in[:, i, 2 * c:2 * c + 2, :],
                               ACT.Copy).then_inc(hi_ready, 1)

            def body(ph):
                for j in range(STEPS):
                    h, t = divmod(j, KT)
                    if ph.within(-1, 14):
                        wait(act, k_done, ph.at(STEPS, STEPS + j + 1))
                        wait(act, summed, ph.at(STEPS, STEPS + j - 1))
                        k_cols = k_ps[0:KP, j % 2, :, :].rearrange("p k n -> p (k n)")
                        for g in range(WH, UH):
                            head = UH * (j % 2) + g
                            own = k_cols[:, g * XD:(g + 1) * XD]
                            act.activation(own, own, ACT.Square,
                                           accum_out=ss[:, j // 2, head:head + 1])
                        act.activation(sq[:, j % 2, :], k_cols[:, 0:WH * XD], ACT.Square).then_inc(squared, 1)
                    if split_at(ph, j):
                        ahead, c = split_at(ph, j)
                        split_high(ph.shift(ahead), c)
                    if closes(ph, j):
                        n = ph.at(2, h - 1)
                        act.wait_ge(s_done, pos_d(ph, h) + 1)
                        wait(act, o_taken, ph.at(2, h - 2))
                        act.activation(lden[:, :], s_ps[:, bank_d(ph, h), 0:UW], ACT.Ln).then_inc(den_ln, 1)
                        act.wait_ge(den_ln, n)
                        act.activation(rden[:, :], lden[:, :], ACT.Exp, scale=-1.0).then_inc(den_table, 1)
                    y = lagged(ph, j, SHIFT_LAG)
                    if y is not None:
                        wait(act, shift_done, ph.at(STEPS, y + 1))
                        wait(act, pv_done, ph.at(STEPS, y - NPR + 1))
                        wait(act, den_done, ph.at(STEPS, y - NPR + 1))
                        act.activation(probs[:, y % NPR, :], shifted[:, y % 2, :], ACT.Exp).then_inc(exp_done, 1)
                    for step, ahead, g in ((13, 1, slice(0, 6)), (1, 0, slice(6, 12))):
                        if j == step and ph.shift(ahead).within(0, 15):
                            n = ph.at(2, 3 if ahead else 2)
                            act.wait_ge(mean_ready, n)
                            act.activation(lg[:, g, :], ss[:, g, :], ACT.Ln).then_inc(ln_ready, 1)
                            act.wait_ge(ln_ready, n)
                            act.activation(rk[:, ph.shift(ahead).parity(), g, :], lg[:, g, :], ACT.Exp, scale=-0.5
                                           ).then_inc(table_ready, 1)
                    if t == 4 and ph.within(0, 15) and not (ph.b == 15 and h == 1):
                        if h == 1:
                            act.wait_ge(s_done, pos_s(ph, KT - 1) + 1)
                        elif ph.b != 0:
                            act.wait_ge(s_done, pos_s(ph.shift(-1), STEPS - 1) + 1)
                        q_high(ph.shift(h), 1 - h)

            act.wait_ge(wk_loaded, 16)
            act.activation(wk_hi[:, :], wk_in, ACT.Copy).then_inc(wk_hi_ready, 1)
            split_high(Phase(0), 0)
            q_high(Phase(0), 0)
            each_phase(act, body, 14)

        @block.vector
        def _(dve):
            def split_low(ph, c):
                i = ph.parity()
                dve.wait_ge(hi_ready, ph.at(KT // 2, c + 1))
                dve.tensor_tensor(ctxT_lo[:, i, 2 * c:2 * c + 2, :], ctxT_in[:, i, 2 * c:2 * c + 2, :],
                                  ctxT_hi[:, i, 2 * c:2 * c + 2, :].bitcast(F32), ALU.subtract).then_inc(lo_ready, 1)

            def body(ph):
                for j in range(STEPS):
                    h, t = divmod(j, KT)
                    if ph.within(0, 15):
                        wait(dve, s_done, pos_s(ph, j) + 1)
                        if j in (0, 6):
                            dve.wait_ge(rk_ready, ph.at(2, 1 + j // 6))
                        wait(dve, shift_done, ph.at(STEPS, j - STEPS + 1))
                        dve.tensor_tensor(scores[0:KP, j, :, :],
                                          s_ps[0:KP, bank_s(ph, j), 0:UW].rearrange("p (g q) -> p g q", q=T),
                                          rk[:, ph.parity(), t, UH * h:UH * h + UH].unsqueeze(2)
                                          .broadcast_to([KP, UH, T]), ALU.mult).then_inc(s_taken, 1)
                    if (ph.within(-1, 14) and j >= 1) or (ph.within(0, 15) and j == 0):
                        i = (j - 1) % STEPS
                        dve.wait_ge(squared, ph.at(STEPS, STEPS + j))
                        dve.tensor_reduce(ss[:, i // 2, UH * (i % 2):UH * (i % 2) + WH],
                                          sq[:, i % 2, :].rearrange("p (g d) -> p g d", d=XD), AX.X, ALU.add
                                          ).then_inc(summed, 1)
                    if ph.within(0, 15) and t >= 1:
                        dve.wait_ge(s_taken, pos_s(ph, j) + 1)
                        if t == 1:
                            wait(dve, gmax_ready, ph.at(2, h - 1))
                            dve.tensor_tensor(cmax[:, h, :], score_slot(j), score_slot(j - 1), ALU.max
                                              ).then_inc(max_done, 1)
                        else:
                            wait(dve, max_done, ph.at(2 * (KT - 1), (KT - 1) * h + t - 1))
                            dve.tensor_tensor(cmax[:, h, :], score_slot(j), cmax[:, h, :], ALU.max
                                              ).then_inc(max_done, 1)
                    for step, ahead, g in ((13, 1, slice(0, 6)), (1, 0, slice(6, 12))):
                        if not ph.shift(ahead).within(0, 15):
                            continue
                        n = 3 if ahead else 2
                        if j == step:
                            dve.wait_ge(summed, ph.at(STEPS, STEPS + KT if ahead else STEPS))
                            dve.tensor_scalar(ss[:, g, :], ss[:, g, :], 1.0 / XD, RMS_EPS, ALU.mult, ALU.add
                                              ).then_inc(mean_ready, 1)
                        if j == step + 1:
                            dve.wait_ge(table_ready, ph.at(2, n))
                            count = [0]

                            def link(ins):
                                count[0] += 1
                                ins.then_inc(newton, 1)
                                dve.wait_ge(newton, ph.at(6, 3 * (n - 1) + count[0]))

                            rsqrt_refine(dve, link, rk[:, ph.shift(ahead).parity(), g, :], ss[:, g, :], nt[:, g, :],
                                         XD ** -0.5).then_inc(rk_ready, 1)
                    y = lagged(ph, j, SHIFT_LAG)
                    if y is not None and vector_shifts(ph):
                        if y % KT == 0:
                            dve.wait_ge(gmax_ready, ph.at(2, y // KT + 1))
                        dve.wait_ge(shift_done, ph.at(STEPS, y))
                        dve.wait_ge(exp_done, ph.at(STEPS, y - 1))
                        dve.tensor_tensor(shifted[:, y % 2, :], score_slot(y), gmax[:, (y // KT) % 2, :],
                                          ALU.subtract).then_inc(shift_done, 1)
                    if closes(ph, j):
                        dve.wait_ge(den_table, ph.at(2, h - 1))
                        dve.tensor_tensor(lden[:, :], s_ps[:, bank_d(ph, h), 0:UW], rden[:, :], ALU.mult
                                          ).then_inc(s_taken, 1)
                        dve.wait_ge(s_taken, pos_d(ph, h) + 1)
                        dve.scalar_tensor_tensor(rden[:, :], lden[:, :], 2.0, rden[:, :], ALU.subtract, ALU.mult
                                                 ).then_inc(den_step, 1)
                        dve.wait_ge(den_step, ph.at(2, h - 1))
                        dve.wait_ge(pv_done, ph.at(STEPS, KT * (h - 1)))
                        dve.scalar_tensor_tensor(qo[:, UH * h:UH * h + UH, ph.shift(-1).tokens()],
                                                 o_ps[:, h, 0:UW].rearrange("p (g q) -> p g q", q=T), -1.0,
                                                 rden[:, :].rearrange("p (g q) -> p g q", q=T), ALU.mult, ALU.mult
                                                 ).then_inc(o_taken, 1)
                    if split_at(ph, j):
                        ahead, c = split_at(ph, j)
                        split_low(ph.shift(ahead), c)

            dve.wait_ge(wk_loaded, 16)
            dve.wait_ge(wk_hi_ready, 1)
            dve.tensor_tensor(wk_lo[:, :], wk_in, wk_hi[:, :].bitcast(F32), ALU.subtract).then_inc(wk_lo_ready, 1)
            split_low(Phase(0), 0)
            each_phase(dve, body, 14)

        @block.tensor
        def _(pe):
            def three(out, l_hi, l_lo, r_hi, r_lo):
                pe.matmul(out, l_hi, r_hi, start=True, stop=False)
                pe.matmul(out, l_hi, r_lo, start=False, stop=False)
                return pe.matmul(out, l_lo, r_hi, start=False, stop=True)

            def project_k(ph, j, c):
                i, t, cols = ph.shift(1).parity(), j // 2, slice((2 * (j % 2) + c) * 512, (2 * (j % 2) + c + 1) * 512)
                return three(k_ps[0:KP, j % 2, c, :], ctxT_hi[:, i, t, :], ctxT_lo[:, i, t, :],
                             wk_hi[:, cols], wk_lo[:, cols])

            def body(ph):
                for j in range(STEPS):
                    h, t = divmod(j, KT)
                    if ph.within(-1, 14):
                        if j % 4 == 0:
                            pe.wait_ge(hi_ready, ph.at(KT // 2, KT // 2 + j // 4 + 1))
                            pe.wait_ge(lo_ready, ph.at(KT // 2, KT // 2 + j // 4 + 1))
                        wait(pe, squared, ph.at(STEPS, STEPS + j - 1))
                        project_k(ph, j, 0)
                    if ph.within(0, 15):
                        if t == 0:
                            pe.wait_ge(qhi_ready, ph.at(2, h + 1))
                            pe.wait_ge(qlo_ready, ph.at(2, h + 1))
                        wait(pe, s_taken, pos_s(ph, j) - 1)
                        i = ph.parity()
                        three(s_ps[0:KP, bank_s(ph, j), 0:UW], ctxT_hi[:, i, t, :], ctxT_lo[:, i, t, :],
                              q_hi[:, h, :, :].rearrange("p g q -> p (g q)"),
                              q_lo[:, h, :, :].rearrange("p g q -> p (g q)")).then_inc(s_done, 1)
                    if closes(ph, j):
                        pe.wait_ge(den_done, ph.at(STEPS, KT * (h - 1)))
                        wait(pe, s_taken, pos_d(ph, h) - 1)
                        pe.matmul(s_ps[:, bank_d(ph, h), 0:UW], ones[:, :], den[:, h, :], start=True, stop=True
                                  ).then_inc(s_done, 1)
                    if ph.within(-1, 14):
                        project_k(ph, j, 1).then_inc(k_done, 1)
                    y = lagged(ph, j, PV_LAG)
                    if y is not None:
                        ty, hy, of = y % KT, (y // KT) % 2, ph.shift(y // STEPS)
                        if ty == 0:
                            wait(pe, o_taken, ph.at(2, y // KT - 1))
                            if hy == 0:
                                pe.wait_ge(nat_loaded[of.parity()], 16 * (of.b // 2 + 1) if of.b is not None else
                                           of.pair * 16 + 16 * (of.i // 2 + 1))
                        wait(pe, exp_done, ph.at(STEPS, y + 1))
                        pe.matmul(o_ps[:, hy, 0:UW], ctx_nat[:, of.parity(), ty, :], probs[:, y % NPR, :],
                                  start=(ty == 0), stop=(ty == KT - 1)).then_inc(pv_done, 1)

            pe.wait_ge(wk_hi_ready, 1)
            pe.wait_ge(wk_lo_ready, 1)
            pe.wait_ge(ones_set, 1)
            each_phase(pe, body, 14)


def output_and_mlp(nc, a, qo):
    ctx = ExitStack()
    with ctx:
        def sb(name, shape, dt=F32):
            return ctx.enter_context(nc.sbuf_tensor(name, shape, dt))

        def sem(name):
            return ctx.enter_context(nc.semaphore(name))

        FC = FF // P
        wvT = sb("om_wvT", [P, XH, C])
        wo = sb("om_wo", [P, XH, E])
        vo = sb("om_vo", [P, XH, E])
        w1 = sb("om_w1", [P, EC, FF])
        w2 = sb("om_w2", [P, FC, E])
        b1 = sb("om_b1", [P, FC])
        b2 = sb("om_b2", [P, E])
        ident = sb("om_ident", [P, P])
        x1 = sb("om_x1", [P, NT, E])
        z = sb("om_z", [P, NT, E])
        x2T = sb("om_x2T", [P, EC, TOK])
        xb = sb("om_xb", [P, NT, E])
        hT = sb("om_hT", [P, FC, TOK])
        stat = sb("om_stat", [P, NT, 6])
        mv = sb("om_mv", [P, NT, 2])
        lna = sb("om_lna", [P, 2, NT])
        lnl = sb("om_lnl", [P, 2, NT])
        lny = sb("om_lny", [P, 2, NT])
        lnt = sb("om_lnt", [P, 2, NT])
        ps = ctx.enter_context(nc.psum_tensor("om_ps", [P, 8, 512], F32))
        vo_loaded, x1_loaded, mlp_loaded = sem("om_vo_loaded"), sem("om_x1_loaded"), sem("om_mlp_loaded")
        vo_mm, vo_ready, z_mm, stat_ready, ln_a, ln_l, ln_y, x2_ready, xb_ready = (
            sem("om_vo_mm"), sem("om_vo_ready"), sem("om_z_mm"), sem("om_stat_ready"), sem("om_ln_a"),
            sem("om_ln_l"), sem("om_ln_y"), sem("om_x2_ready"), sem("om_xb_ready"))
        x2T_mm, x2T_ready, h_mm, h_ready, y_mm, out_ready, stored, dve_chain = (
            sem("om_x2T_mm"), sem("om_x2T_ready"), sem("om_h_mm"), sem("om_h_ready"), sem("om_y_mm"),
            sem("om_out_ready"), sem("om_stored"), sem("om_dve_chain"))
        block = ctx.enter_context(nc.Block())

        @block.sync
        def _(sp):
            sp.dma_start(wvT[:, :, :], a.xv_wT.rearrange("(h d) c -> d h c", d=XD)).then_inc(vo_loaded, 16)
            sp.dma_start(wo[:, :, :], a.xo_w.rearrange("(h d) e -> d h e", d=XD)).then_inc(vo_loaded, 16)
            sp.dma_start(x1[:, :, :], a.x1.rearrange("(n p) e -> p n e", p=P)).then_inc(x1_loaded, 16)
            sp.dma_start(ident[:, :], a.ident).then_inc(x1_loaded, 16)
            sp.dma_start(w1[:, :, :], a.w1T.rearrange("(k p) f -> p k f", p=P)).then_inc(mlp_loaded, 16)
            sp.dma_start(w2[:, :, :], a.w2T.rearrange("(k p) e -> p k e", p=P)).then_inc(mlp_loaded, 16)
            sp.dma_start(b1[:, :], a.b1).then_inc(mlp_loaded, 16)
            sp.dma_start(b2[:, :], a.b2.partition_broadcast(P)).then_inc(mlp_loaded, 16)
            for n in range(NT):
                sp.wait_ge(out_ready, n + 1)
                sp.dma_start(a.out[n * P:(n + 1) * P, :], z[:, n, :]).then_inc(stored, 16)
            sp.wait_ge(stored, 16 * NT)

        @block.gpsimd
        def _(pool):
            pool.wait_ge(mlp_loaded, 64)
            for n in range(NT):
                pool.wait_ge(x2_ready, n + 1)
                pool.tensor_tensor(xb[:, n, :], z[:, n, :], b2[:, :], ALU.add).then_inc(xb_ready, 1)

        @block.scalar
        def _(act):
            act.preload_act_table_set(TABLES)
            for m in range(XH // 2):
                act.wait_ge(vo_mm, m + 1)
                act.activation(vo[:, 2 * m:2 * m + 2, :].rearrange("p h e -> p (h e)"), ps[:, m % 4, :],
                               ACT.Copy).then_inc(vo_ready, 1)

            def table(i):
                act.wait_ge(ln_a, i + 1)
                act.activation(lnl[:, i, :], lna[:, i, :], ACT.Ln).then_inc(ln_l, 1)
                act.wait_ge(ln_l, i + 1)
                act.activation(lny[:, i, :], lnl[:, i, :], ACT.Exp, scale=-0.5).then_inc(ln_y, 1)

            table(0)
            for n in range(NT):
                act.wait_ge(x2T_mm, n + 1)
                act.activation(x2T[:, :, n * P:(n + 1) * P],
                               ps[:, n % 2, 0:EC * P].rearrange("p (k t) -> p k t", k=EC),
                               ACT.Copy).then_inc(x2T_ready, 1)
            act.wait_ge(mlp_loaded, 64)
            for m in range(2 * FC):
                f, n = divmod(m, 2)
                act.wait_ge(h_mm, m + 1)
                act.activation(hT[:, f, n * UW:(n + 1) * UW], ps[:, 2 + m % 4, 0:UW], ACT.Gelu,
                               bias=b1[:, f:f + 1]).then_inc(h_ready, 1)
            act.preload_act_table_set(TABLES)
            table(1)

        @block.vector
        def _(dve):
            link = linker(dve, dve_chain)

            def layer_norm(i, banks, width_mm, other, other_ready, per):
                for n in range(NT):
                    dve.wait_ge(width_mm, n + 1)
                    dve.wait_ge(other_ready, per(n))
                    link(dve.tensor_tensor(z[:, n, :], ps[:, banks[n % len(banks)], 0:E], other[:, n, :], ALU.add))
                    link(dve.bn_stats(stat[:, n, :], z[:, n, :]))
                    dve.bn_aggr(mv[:, n, :], stat[:, n, :]).then_inc(stat_ready, 1)
                dve.wait_ge(stat_ready, NT * (i + 1))
                dve.tensor_scalar(lna[:, i, :], mv[:, :, 1], LN_EPS, None, ALU.add).then_inc(ln_a, 1)
                dve.wait_ge(ln_a, i + 1)
                dve.wait_ge(ln_y, i + 1)
                link(rsqrt_refine(dve, link, lny[:, i, :], lna[:, i, :], lnt[:, i, :]))
                for n in range(NT):
                    dve.tensor_scalar(z[:, n, :], z[:, n, :], mv[:, n, 0:1], lny[:, i, n:n + 1],
                                      ALU.subtract, ALU.mult).then_inc(out_ready if i else x2_ready, 1)

            layer_norm(0, (4, 5, 6, 7), z_mm, x1, x1_loaded, lambda n: 32)
            layer_norm(1, (6, 7, 0, 1), y_mm, xb, xb_ready, lambda n: n + 1)

        @block.tensor
        def _(pe):
            pe.wait_ge(vo_loaded, 32)
            for h in range(XH):
                m = h // 2
                if m >= 4 and h % 2 == 0:
                    pe.wait_ge(vo_ready, m - 3)
                mm = pe.matmul(ps[:, m % 4, (h % 2) * E:(h % 2 + 1) * E], wvT[:, h, :], wo[:, h, :],
                               start=True, stop=True)
                if h % 2:
                    mm.then_inc(vo_mm, 1)
            for n in range(NT):
                if n >= 4:
                    pe.wait_ge(stat_ready, n - 3)
                for h in range(XH):
                    if n == 0:
                        pe.wait_ge(vo_ready, h // 2 + 1)
                    mm = pe.matmul(ps[:, 4 + n % 4, 0:E], qo[:, h, n * P:(n + 1) * P], vo[:, h, :],
                                   start=(h == 0), stop=(h == XH - 1))
                mm.then_inc(z_mm, 1)
            pe.wait_ge(x1_loaded, 32)
            for n in range(NT):
                pe.wait_ge(x2_ready, n + 1)
                if n >= 2:
                    pe.wait_ge(x2T_ready, n - 1)
                for k in range(EC):
                    mm = pe.transpose(ps[:, n % 2, k * P:(k + 1) * P], z[:, n, k * P:(k + 1) * P], ident[:, :])
                mm.then_inc(x2T_mm, 1)
            pe.wait_ge(mlp_loaded, 64)
            for m in range(2 * FC):
                f, n = divmod(m, 2)
                pe.wait_ge(x2T_ready, 4 if n == 0 else NT)
                if m >= 4:
                    pe.wait_ge(h_ready, m - 3)
                for k in range(EC):
                    mm = pe.matmul(ps[:, 2 + m % 4, 0:UW], w1[:, k, f * P:(f + 1) * P],
                                   x2T[:, k, n * UW:(n + 1) * UW], start=(k == 0), stop=(k == EC - 1))
                mm.then_inc(h_mm, 1)
            for n in range(NT):
                if n == 0:
                    pe.wait_ge(h_ready, 2 * FC)
                if n >= 4:
                    pe.wait_ge(stat_ready, NT + n - 3)
                for f in range(FC):
                    mm = pe.matmul(ps[:, (6, 7, 0, 1)[n % 4], 0:E], hT[:, f, n * P:(n + 1) * P], w2[:, f, :],
                                   start=(f == 0), stop=(f == FC - 1))
                mm.then_inc(y_mm, 1)


class Arrays:
    pass


def program(nc, a):
    qo_ctx = ExitStack()
    with qo_ctx:
        qo = qo_ctx.enter_context(nc.sbuf_tensor("qo", [P, XH, TOK], F32))
        with nc.sbuf_tensor("x1T", [P, EC, TOK], F32) as x1T:
            self_attention(nc, a, x1T)
            query_path(nc, a, x1T, qo)
        cross_attention(nc, a, qo)
        output_and_mlp(nc, a, qo)


def kernel(**inputs):
    import numpy as np
    import concourse.bacc as bacc
    from concourse.bass_utils import run_bass_kernel_spmd

    g = {k: np.asarray(v) for k, v in inputs.items()}

    def heads_in(w):
        return w.transpose(1, 0, 2).reshape(E, NH * HD)

    def columns(v):
        return v.reshape(-1, P).T

    rows = np.arange(P)
    queries, keys = np.meshgrid(rows % 64, np.arange(T), indexing="ij")
    x = g["x"].reshape(TOK, E)
    ctx = g["ctx_1024"]
    host = {
        "x": x,
        "xT": x.T,
        "ctx": ctx,
        "ctxT": ctx.reshape(B, KP, KT, C).transpose(0, 3, 2, 1).reshape(B, C, SK),
        "sa_wq": heads_in(g["L0_attn_Wq"]), "sa_wk": heads_in(g["L0_attn_Wk"]), "sa_wv": heads_in(g["L0_attn_Wv"]),
        "sa_wo": g["L0_attn_Wo"],
        "sa_bias": np.stack([columns(g["L0_attn_" + n].reshape(-1)) for n in ("bq", "bk", "bv")], axis=1),
        "sa_bo": g["L0_attn_bo"],
        "xq_w": g["L0_xattn_Wq"], "xk_w": g["L0_xattn_Wk"], "xk_wT": g["L0_xattn_Wk"].T,
        "xv_wT": g["L0_xattn_Wv"].T, "xo_w": g["L0_xattn_Wo"],
        "gains": np.stack([g["L0_xattn_gq"], g["L0_xattn_gk"]], axis=1),
        "w1T": g["L0_ffn_proj1"].T, "b1": columns(g["L0_ffn_proj1_bias"]),
        "w2T": g["L0_ffn_proj2"].T, "b2": g["L0_ffn_proj2_bias"],
        "ident": np.eye(P, dtype=np.float32),
        "causal": np.where((keys > queries) & (queries < T), np.finfo(np.float32).min, 0).astype(np.float32),
        "parity": np.stack([(rows // HD + 1) % 2, rows // HD % 2], axis=1).astype(np.float32),
    }
    nc = bacc.Bacc("TRN2", target_bir_lowering=False, num_devices=1)
    a, arrays = Arrays(), {}
    for name, v in host.items():
        v = np.ascontiguousarray(v)
        arrays["in_" + name] = v
        a.__dict__[name] = nc.dram_tensor("in_" + name, v.shape, mybir.dt.from_np(v.dtype), kind="ExternalInput").ap()
    a.out = nc.dram_tensor("out", (TOK, E), F32, kind="ExternalOutput").ap()
    a.x1 = nc.dram_tensor("x1_scratch", (TOK, E), F32, kind="Internal").ap()
    program(nc, a)
    r = run_bass_kernel_spmd(nc, [arrays], core_ids=[0])
    return r.results[0]["out"].reshape(B, T, E)
```

```python
import concourse.bass as bass
from concourse import mybir
from contextlib import ExitStack

F32 = mybir.dt.float32
F32R = mybir.dt.float32r
ALU = mybir.AluOpType
ACT = mybir.ActivationFunctionType
AX = mybir.AxisListType

B, T, E = 16, 56, 256
C, SK = 128, 1500
NH, HD = 16, 16
XH, XD = 16, 128
FF = 1024
P = 128
TOK = B * T
NT = TOK // P
EC = E // P
KT = 12
KP = SK // KT
UH = 8
UW = UH * T
LN_EPS = 1e-5
RMS_EPS = 1e-5
bass_max = bass.bass_isa.ReduceOp.max
TABLES = "natural_log_exp_and_others"


def overlay(nc, name, shape, dt=F32):
    with nc.sbuf_tensor(name, shape, dt) as t:
        return t


def rsqrt_refine(dve, link, y, a, t, gain=1.0):
    link(dve.tensor_tensor(t, y, y, ALU.mult))
    link(dve.tensor_tensor(t, t, a, ALU.mult))
    link(dve.tensor_scalar(t, t, -0.5, 1.5, ALU.mult, ALU.add))
    return dve.scalar_tensor_tensor(y, y, gain, t, ALU.mult, ALU.mult)


def linker(dve, sem):
    n = [0]

    def link(ins):
        n[0] += 1
        ins.then_inc(sem, 1)
        dve.wait_ge(sem, n[0])
    return link


def self_attention(nc, a, xT, x1T_hi, x1T_lo, qo, wk_parts, xq_lo):
    ctx = ExitStack()
    with ctx:
        def sb(name, shape, dt=F32):
            return ctx.enter_context(nc.sbuf_tensor(name, shape, dt))

        def sem(name):
            return ctx.enter_context(nc.semaphore(name))

        PAIRS = B // 2
        NP = 4
        x_nat = sb("sa_x", [P, NT, E])
        wq = sb("sa_wq", [P, EC, E])
        wk = sb("sa_wk", [P, EC, E])
        wv = sb("sa_wv", [P, EC, E])
        wo = wk
        bias = sb("sa_bias", [P, 3, EC])
        bo = sb("sa_bo", [P, E])
        ident = sb("sa_ident", [P, P])
        causal = sb("sa_causal", [P, T])
        parity = sb("sa_parity", [P, 2])
        qT = sb("sa_qT", [P, EC, TOK + 8])
        kT2 = sb("sa_kT2", [P, EC, 2, TOK])
        vbd = sb("sa_vbd", [P, B, NH // 2, 2 * HD])
        probs = sb("sa_probs", [P, NP, NH, 64])
        pT = sb("sa_pT", [P, 2, NH // 2, P])
        yT = sb("sa_yT", [P, EC, TOK])
        z = x_nat
        stat = sb("sa_stat", [P, NT, 6])
        mv = sb("sa_mv", [P, NT, 2])
        rmax = sb("sa_rmax", [P, NP, NH])
        rsum = sb("sa_rsum", [P, 2, NH])
        lna = sb("sa_lna", [P, NT])
        lnl = sb("sa_lnl", [P, NT])
        lny = sb("sa_lny", [P, NT])
        lnt = sb("sa_lnt", [P, NT])
        ps = ctx.enter_context(nc.psum_tensor("sa_ps", [P, 8, 512], F32))
        scratch = qo[:, :, :].rearrange("p h t -> p (h t)")
        xwvT = scratch[:, 0:XH * C].rearrange("p (h c) -> p h c", h=XH)
        xwo = scratch[:, XH * C:XH * (C + E)].rearrange("p (h e) -> p h e", h=XH)
        vo = scratch[:, XH * (C + E):XH * (C + 2 * E)]
        xwq = scratch[:, XH * (C + 2 * E):XH * (C + 2 * E) + EC * XH * XD]
        xq_hi = wk_parts[:, :, :].rearrange("p s n -> p (s n)")
        WQ_PART = EC * XH * XD // PAIRS

        qk_loaded, v_loaded, bias_loaded, ident_loaded, x_loaded, o_loaded, xvo_loaded, xwq_loaded = (
            sem("sa_qk_loaded"), sem("sa_v_loaded"), sem("sa_bias_loaded"), sem("sa_ident_loaded"),
            sem("sa_x_loaded"), sem("sa_o_loaded"), sem("sa_xvo_loaded"), sem("sa_xwq_loaded"))
        cleared, xb_ready = sem("sa_cleared"), sem("sa_xb_ready")
        qT_mm, kT_mm, v_mm, qT_ready, kT_ready, v_low, v_high = (
            sem("sa_qT_mm"), sem("sa_kT_mm"), sem("sa_v_mm"), sem("sa_qT_ready"), sem("sa_kT_ready"),
            sem("sa_v_low"), sem("sa_v_high"))
        s_mm, s_masked, max_ready, shifted, exped, sum_ready, normed = (
            sem("sa_s_mm"), sem("sa_s_masked"), sem("sa_max_ready"), sem("sa_shifted"), sem("sa_exped"),
            sem("sa_sum_ready"), sem("sa_normed"))
        pT_mm, pT_ready, y_mm, yT_ready = sem("sa_pT_mm"), sem("sa_pT_ready"), sem("sa_y_mm"), sem("sa_yT_ready")
        vo_mm, vo_ready, xq_hi_ready, xq_lo_ready = (
            sem("sa_vo_mm"), sem("sa_vo_ready"), sem("sa_xq_hi_ready"), sem("sa_xq_lo_ready"))
        o_mm, stat_ready, ln_table, x1_ready, x1T_mm, hi_ready, lo_ready, stored, dve_chain, ln_log, ln_est = (
            sem("sa_o_mm"), sem("sa_stat_ready"), sem("sa_ln_table"), sem("sa_x1_ready"),
            sem("sa_x1T_mm"), sem("sa_hi_ready"), sem("sa_lo_ready"), sem("sa_stored"), sem("sa_dve_chain"),
            sem("sa_ln_log"), sem("sa_ln_est"))
        GROUPS = (0, 4), (4, NT)
        block = ctx.enter_context(nc.Block())

        @block.sync
        def _(sp):
            sp.dma_start(wq[:, :, :], a.sa_wq.rearrange("(k p) n -> p k n", p=P)).then_inc(qk_loaded, 16)
            for k in range(EC):
                sp.dma_start(xT[:, k, :], a.xT[k * P:(k + 1) * P, :]).then_inc(qk_loaded, 16)
            sp.dma_start(wk[:, :, :], a.sa_wk.rearrange("(k p) n -> p k n", p=P)).then_inc(qk_loaded, 16)
            sp.dma_start(wv[:, :, :], a.sa_wv.rearrange("(k p) n -> p k n", p=P)).then_inc(v_loaded, 16)
            sp.dma_start(xwq.rearrange("p (k n) -> p k n", k=EC), a.xq_w.rearrange("(k p) n -> p k n", p=P)
                         ).then_inc(xwq_loaded, 16)
            sp.dma_start(x_nat[:, :, :], a.x.rearrange("(n p) e -> p n e", p=P)).then_inc(x_loaded, 16)
            sp.dma_start(bo[:, :], a.sa_bo.partition_broadcast(P)).then_inc(x_loaded, 16)
            sp.dma_start(xwvT, a.xv_wT.rearrange("(h d) c -> d h c", d=XD)).then_inc(xvo_loaded, 16)
            sp.dma_start(xwo, a.xo_w.rearrange("(h d) e -> d h e", d=XD)).then_inc(xvo_loaded, 16)
            sp.wait_ge(kT_mm, 4)
            sp.dma_start(wo[:, :, :], a.sa_wo.rearrange("(k p) n -> p k n", p=P)).then_inc(o_loaded, 16)
            sp.wait_ge(x1_ready, NT)
            sp.dma_start(a.x1.rearrange("(n p) e -> p n e", p=P), z[:, :, :]).then_inc(stored, 16)
            sp.wait_ge(vo_ready, XH // 2)
            sp.dma_start(a.vo.rearrange("p h e -> p (h e)"), vo).then_inc(stored, 16)
            sp.wait_ge(stored, 32)

        @block.gpsimd
        def _(pool):
            pool.memset(qT[:, :, TOK:TOK + 8], 0.0).then_inc(cleared, 1)
            pool.memset(vbd[:, :, :, :], 0.0).then_inc(cleared, 1)
            pool.memset(probs[:, :, :, :], 0.0).then_inc(cleared, 1)

            def shift(p):
                pr = probs[:, p % NP, :, 0:T]
                pool.wait_ge(max_ready, p + 1)
                pool.tensor_tensor(pr, pr, rmax[:, p % NP, :].unsqueeze(2).broadcast_to([P, NH, T]),
                                   ALU.subtract).then_inc(shifted, 1)

            def norm(p):
                pr = probs[:, p % NP, :, 0:T]
                pool.wait_ge(sum_ready, p + 1)
                pool.tensor_tensor(pr, pr, rsum[:, p % 2, :].unsqueeze(2).broadcast_to([P, NH, T]),
                                   ALU.mult).then_inc(normed, 1)

            for p in range(3):
                shift(p)
            norm(0)
            for p in range(PAIRS):
                if p + 1 < PAIRS:
                    norm(p + 1)
                if p + 3 < PAIRS:
                    shift(p + 3)
                if p == 5:
                    pool.wait_ge(x_loaded, 32)
                if p >= 5:
                    for n in ((0, 1, 2), (3, 4), (5, 6))[p - 5]:
                        pool.tensor_tensor(x_nat[:, n, :], x_nat[:, n, :], bo[:, :], ALU.add).then_inc(xb_ready, 1)

        @block.scalar
        def _(act):
            act.dma_start(bias[:, :, :], a.sa_bias).then_inc(bias_loaded, 16)
            act.dma_start(parity[:, :], a.parity).then_inc(bias_loaded, 16)
            act.dma_start(causal[:, :], a.causal).then_inc(bias_loaded, 16)
            act.dma_start(ident[:, :], a.ident).then_inc(ident_loaded, 16)
            act.preload_act_table_set(TABLES)
            act.wait_ge(bias_loaded, 48)
            for m in range(4):
                i, n = divmod(m, 2)
                act.wait_ge(qT_mm, m + 1)
                act.activation(qT[:, i, n * UW:(n + 1) * UW], ps[:, m, 0:UW], ACT.Identity,
                               bias=bias[:, 0, i:i + 1]).then_inc(qT_ready, 1)

            def take_v(m):
                act.wait_ge(v_mm, m + 1)
                if m == 0:
                    act.wait_ge(cleared, 2)
                act.activation(vbd[0:T, 4 * m:4 * m + 4, :, 0:HD],
                               ps[0:T, m, :].rearrange("p (b g d) -> p b g d", b=4, d=HD),
                               ACT.Copy).then_inc(v_low, 1)

            def exp(p):
                pr = probs[:, p % NP, :, 0:T]
                act.wait_ge(shifted, p + 1)
                act.activation(pr, pr, ACT.Exp).then_inc(exped, 1)

            def take_pT(p):
                act.wait_ge(pT_mm, p + 1)
                if p >= 2:
                    act.wait_ge(y_mm, p - 1)
                act.activation(pT[:, p % 2, :, :], ps[:, 0:2, :].rearrange("p k (g q) -> p (k g) q", q=P),
                               ACT.Copy).then_inc(pT_ready, 1)

            def take_y(p):
                act.wait_ge(y_mm, p + 1)
                for i in range(EC):
                    act.activation(yT[:, i, 2 * p * T:2 * (p + 1) * T], ps[:, 2 + p % 2, i * 128:i * 128 + 2 * T],
                                   ACT.Identity, bias=bias[:, 2, i:i + 1]).then_inc(yT_ready, 1)

            def take_vo(m):
                act.wait_ge(vo_mm, m + 1)
                act.activation(vo[:, m * 2 * E:(m + 1) * 2 * E], ps[:, 2 + m % 2, :], ACT.Copy).then_inc(vo_ready, 1)

            def table(g):
                tiles = slice(*GROUPS[g])
                act.wait_ge(ln_table, g + 1)
                act.activation(lnl[:, tiles], lna[:, tiles], ACT.Ln).then_inc(ln_log, 1)
                act.wait_ge(ln_log, g + 1)
                act.activation(lny[:, tiles], lnl[:, tiles], ACT.Exp, scale=-0.5).then_inc(ln_est, 1)

            def x1T_high(n):
                act.wait_ge(x1T_mm, n + 1)
                act.activation(x1T_hi[:, :, n * P:(n + 1) * P],
                               ps[:, n % 2, 0:EC * P].rearrange("p (k t) -> p k t", k=EC),
                               ACT.Copy).then_inc(hi_ready, 1)

            for m in range(4):
                take_v(m)
                if m < 3:
                    exp(m)
            act.wait_ge(xwq_loaded, 16)
            for p in range(PAIRS):
                take_pT(p)
                if p >= 1:
                    take_y(p - 1)
                if p + 3 < PAIRS:
                    exp(p + 3)
                part = slice(p * WQ_PART, (p + 1) * WQ_PART)
                act.activation(xq_hi[:, part], xwq[:, part], ACT.Copy).then_inc(xq_hi_ready, 1)
            take_y(PAIRS - 1)
            table(0)
            for m in range(4):
                take_vo(m)
            table(1)
            for n in range(*GROUPS[0]):
                x1T_high(n)
            for m in range(4, XH // 2):
                take_vo(m)
            for n in range(*GROUPS[1]):
                x1T_high(n)

        @block.vector
        def _(dve):
            link = linker(dve, dve_chain)
            dve.wait_ge(bias_loaded, 48)
            for m in range(4):
                i, n = divmod(m, 2)
                dve.wait_ge(kT_mm, m + 1)
                for par in range(2):
                    dve.tensor_scalar(kT2[:, i, par, n * UW:(n + 1) * UW], ps[:, 4 + m, 0:UW],
                                      bias[:, 1, i:i + 1], parity[:, par:par + 1],
                                      ALU.add, ALU.mult).then_inc(kT_ready, 1)

            def take_v(m):
                dve.wait_ge(v_mm, m + 1)
                dve.tensor_copy(vbd[64:64 + T, 4 * m:4 * m + 4, :, HD:2 * HD],
                                ps[64:64 + T, m, :].rearrange("p (b g d) -> p b g d", b=4, d=HD)
                                ).then_inc(v_high, 1)

            def head_rows(p):
                dve.wait_ge(s_mm, p + 1)
                if p == 0:
                    dve.wait_ge(cleared, 3)
                if p >= NP:
                    dve.wait_ge(pT_mm, p - NP + 1)
                for i in range(EC):
                    for o in range(2):
                        col = 2 * T * i + T * o
                        dve.scalar_tensor_tensor(
                            probs[:, p % NP, 8 * i + o:8 * i + 8:2, 0:T], ps[:, 4:8, col:col + T], HD ** -0.5,
                            causal[:, :].unsqueeze(1).broadcast_to([P, 4, T]), ALU.mult, ALU.add
                        ).then_inc(s_masked, 1)
                dve.wait_ge(s_masked, 4 * (p + 1))
                dve.tensor_reduce(rmax[:, p % NP, :], probs[:, p % NP, :, 0:T], AX.X, ALU.max).then_inc(max_ready, 1)

            def row_sums(p):
                dve.wait_ge(exped, p + 1)
                if p >= 2:
                    dve.wait_ge(normed, p - 1)
                link(dve.tensor_reduce(rsum[:, p % 2, :], probs[:, p % NP, :, 0:T], AX.X, ALU.add))
                dve.reciprocal(rsum[:, p % 2, :], rsum[:, p % 2, :]).then_inc(sum_ready, 1)

            def stats(n):
                dve.wait_ge(o_mm, n + 1)
                dve.wait_ge(xb_ready, n + 1)
                link(dve.tensor_tensor(z[:, n, :], ps[:, 4 + n % 4, 0:E], z[:, n, :], ALU.add))
                link(dve.bn_stats(stat[:, n, :], z[:, n, :]))
                dve.bn_aggr(mv[:, n, :], stat[:, n, :]).then_inc(stat_ready, 1)

            def variances(g):
                tiles = slice(*GROUPS[g])
                dve.wait_ge(stat_ready, tiles.stop)
                dve.tensor_scalar(lna[:, tiles], mv[:, tiles, 1], LN_EPS, None, ALU.add).then_inc(ln_table, 1)

            def normalise(g):
                tiles = slice(*GROUPS[g])
                dve.wait_ge(ln_table, g + 1)
                dve.wait_ge(ln_est, g + 1)
                link(rsqrt_refine(dve, link, lny[:, tiles], lna[:, tiles], lnt[:, tiles]))
                for n in range(*GROUPS[g]):
                    dve.tensor_scalar(z[:, n, :], z[:, n, :], mv[:, n, 0:1], lny[:, n:n + 1],
                                      ALU.subtract, ALU.mult).then_inc(x1_ready, 1)

            def x1T_low(n):
                dve.wait_ge(hi_ready, n + 1)
                dve.tensor_tensor(x1T_lo[:, :, n * P:(n + 1) * P],
                                  ps[:, n % 2, 0:EC * P].rearrange("p (k t) -> p k t", k=EC),
                                  x1T_hi[:, :, n * P:(n + 1) * P].bitcast(F32), ALU.subtract).then_inc(lo_ready, 1)

            for p in range(3):
                head_rows(p)
                take_v(p)
            row_sums(0)
            take_v(3)
            for p in range(PAIRS):
                if p + 1 < PAIRS:
                    row_sums(p + 1)
                if p + 3 < PAIRS:
                    head_rows(p + 3)
                if p >= 1:
                    part = slice((p - 1) * WQ_PART, p * WQ_PART)
                    dve.wait_ge(xq_hi_ready, p)
                    dve.tensor_tensor(xq_lo[:, part], xwq[:, part], xq_hi[:, part].bitcast(F32), ALU.subtract
                                      ).then_inc(xq_lo_ready, 1)
            for n in range(*GROUPS[0]):
                stats(n)
            variances(0)
            stats(4)
            normalise(0)
            stats(5)
            stats(6)
            variances(1)
            part = slice((PAIRS - 1) * WQ_PART, PAIRS * WQ_PART)
            dve.wait_ge(xq_hi_ready, PAIRS)
            dve.tensor_tensor(xq_lo[:, part], xwq[:, part], xq_hi[:, part].bitcast(F32), ALU.subtract
                              ).then_inc(xq_lo_ready, 1)
            normalise(1)
            for n in range(NT):
                x1T_low(n)

        @block.tensor
        def _(pe):
            pe.wait_ge(qk_loaded, 64)
            for w, base, done in ((wq, 0, qT_mm), (wk, 4, kT_mm)):
                for m in range(4):
                    i, n = divmod(m, 2)
                    for k in range(EC):
                        mm = pe.matmul(ps[:, base + m, 0:UW], w[:, k, i * P:(i + 1) * P],
                                       xT[:, k, n * UW:(n + 1) * UW], start=(k == 0), stop=(k == EC - 1))
                    mm.then_inc(done, 1)

            def project_v(m):
                if m == 0:
                    pe.wait_ge(v_loaded, 16)
                pe.wait_ge(qT_ready, m + 1)
                for b in range(4 * m, 4 * m + 4):
                    for par in range(2):
                        for k in range(EC):
                            mm = pe.matmul(ps[64 * par:64 * par + T, m, (b % 4) * P:(b % 4 + 1) * P],
                                           xT[:, k, b * T:(b + 1) * T],
                                           wv[:, k, :].rearrange("p (g q d) -> p q g d", q=2, d=HD)[:, par],
                                           start=(k == 0), stop=(k == EC - 1))
                mm.then_inc(v_mm, 1)

            def scores(p):
                if p >= 1:
                    pe.wait_ge(s_masked, 4 * p)
                else:
                    pe.wait_ge(kT_ready, 8)
                    pe.wait_ge(qT_ready, 4)
                    pe.wait_ge(cleared, 1)
                for e in range(2):
                    b = 2 * p + e
                    for i in range(EC):
                        for r in range(4):
                            rows = slice(32 * r, 32 * r + 32)
                            col = 2 * T * i
                            mm = pe.matmul(ps[64 * e:64 * e + 64, 4 + r, col:col + 2 * T],
                                           qT[rows, i, b * T:b * T + 64], kT2[rows, i, :, b * T:(b + 1) * T],
                                           start=True, stop=True)
                mm.then_inc(s_mm, 1)

            def turn(p):
                pe.wait_ge(normed, p + 1)
                if p >= 1:
                    pe.wait_ge(pT_ready, p)
                else:
                    pe.wait_ge(v_low, 4)
                    pe.wait_ge(v_high, 4)
                    pe.wait_ge(ident_loaded, 16)
                for g in range(NH // 2):
                    mm = pe.transpose(ps[:, g // 4, (g % 4) * P:(g % 4 + 1) * P],
                                      probs[:, p % NP, 2 * g:2 * g + 2, :], ident[:, :])
                mm.then_inc(pT_mm, 1)

            def weigh(p):
                pe.wait_ge(pT_ready, p + 1)
                if p >= 2:
                    pe.wait_ge(yT_ready, 2 * (p - 1))
                for e in range(2):
                    for g in range(NH // 2):
                        r = 32 * (g % 4)
                        mm = pe.matmul(ps[r:r + 32, 2 + p % 2, (g // 4) * P + e * T:(g // 4) * P + (e + 1) * T],
                                       vbd[:, 2 * p + e, g, :], pT[:, p % 2, g, 64 * e:64 * e + T],
                                       start=True, stop=True)
                mm.then_inc(y_mm, 1)

            def project_out(n):
                if n == 0:
                    pe.wait_ge(o_loaded, 16)
                    pe.wait_ge(s_masked, 4 * PAIRS)
                pe.wait_ge(yT_ready, 2 * ((n * P + P - 1) // (2 * T) + 1))
                if n >= 4:
                    pe.wait_ge(stat_ready, n - 3)
                for k in range(EC):
                    mm = pe.matmul(ps[:, 4 + n % 4, 0:E], yT[:, k, n * P:(n + 1) * P], wo[:, k, :],
                                   start=(k == 0), stop=(k == EC - 1))
                mm.then_inc(o_mm, 1)

            def project_vo(m):
                if m == 0:
                    pe.wait_ge(xvo_loaded, 32)
                if m < 2:
                    pe.wait_ge(yT_ready, 2 * PAIRS)
                else:
                    pe.wait_ge(vo_ready, m - 1)
                for h in (2 * m, 2 * m + 1):
                    mm = pe.matmul(ps[:, 2 + m % 2, (h % 2) * E:(h % 2 + 1) * E], xwvT[:, h, :], xwo[:, h, :],
                                   start=True, stop=True)
                mm.then_inc(vo_mm, 1)

            def turn_x1(n):
                pe.wait_ge(x1_ready, n + 1)
                if n >= 2:
                    pe.wait_ge(lo_ready, n - 1)
                for k in range(EC):
                    mm = pe.transpose(ps[:, n % 2, k * P:(k + 1) * P], z[:, n, k * P:(k + 1) * P], ident[:, :])
                mm.then_inc(x1T_mm, 1)

            for p in range(3):
                scores(p)
                project_v(p)
            project_v(3)
            for p in range(PAIRS):
                if p + 3 < PAIRS:
                    scores(p + 3)
                turn(p)
                if p >= 1:
                    weigh(p - 1)
                if p == PAIRS - 2:
                    for n in range(3):
                        project_out(n)
                if p == PAIRS - 1:
                    project_out(3)
            weigh(PAIRS - 1)
            for n in range(4, NT):
                project_out(n)
            for m in range(4):
                project_vo(m)
            for n in range(*GROUPS[0]):
                turn_x1(n)
            for m in range(4, XH // 2):
                project_vo(m)
            for n in range(*GROUPS[1]):
                turn_x1(n)


def query_path(nc, a, x1T_hi, x1T_lo, qo, wk_parts, xq_lo, wk_in, ctxT_in, wk_loaded, ctxT_loaded):
    ctx = ExitStack()
    with ctx:
        def sb(name, shape, dt=F32):
            return ctx.enter_context(nc.sbuf_tensor(name, shape, dt))

        def sem(name):
            return ctx.enter_context(nc.semaphore(name))

        wq_hi = wk_parts
        wq_lo = xq_lo[:, :].rearrange("p (k n) -> p k n", k=EC)
        wkT = sb("xq_wkT", [P, XH, C])
        ident = sb("xq_ident", [P, P])
        gains = sb("xq_gains", [P, 2])
        gqk = sb("xq_gqk", [P, 1])
        sq = sb("xq_sq", [P, 2, UH * XD])
        qn = sb("xq_qn", [P, 2, UH, XD])
        qhT = sb("xq_qhT", [P, 2, 4, P])
        ss = sb("xq_ss", [P, 2, UH])
        lg = sb("xq_lg", [P, 2, UH])
        rs = sb("xq_rs", [P, 2, UH])
        rt = sb("xq_rt", [P, 2, UH])
        ps = ctx.enter_context(nc.psum_tensor("xq_ps", [P, 8, 512], F32))
        rest_loaded, gains_ready = sem("xq_rest_loaded"), sem("xq_gains_ready")
        q_mm, squared, mean_ready, table_ready, qn_ready, dve_chain, act_chain = (
            sem("xq_q_mm"), sem("xq_squared"), sem("xq_mean_ready"), sem("xq_table_ready"), sem("xq_qn_ready"),
            sem("xq_dve_chain"), sem("xq_act_chain"))
        qT_mm, qhT_ready, qp_mm, qp_ready = (
            sem("xq_qT_mm"), sem("xq_qhT_ready"), sem("xq_qp_mm"), sem("xq_qp_ready"))
        V = 2 * NT
        block = ctx.enter_context(nc.Block())

        @block.sync
        def _(sp):
            sp.dma_start(wkT[:, :, :], a.xk_wT.rearrange("(h d) c -> d h c", d=XD)).then_inc(rest_loaded, 16)
            sp.dma_start(ident[:, :], a.ident).then_inc(rest_loaded, 16)
            sp.dma_start(gains[:, :], a.gains).then_inc(rest_loaded, 16)
            sp.dma_start(wk_in, a.xk_w).then_inc(wk_loaded, 16)
            for b in range(2):
                sp.dma_start(ctxT_in[:, b, :, :].rearrange("c t p -> c (t p)"), a.ctxT[b]
                             ).then_inc(ctxT_loaded[b], 16)

        @block.tensor
        def _(pe):
            for v in range(V + 1):
                if v < V:
                    n, half = divmod(v, 2)
                    if v >= 2:
                        pe.wait_ge(qn_ready, v - 1)
                    for c in range(2):
                        col = (2 * half + c) * 512
                        out, rows, cols = ps[:, 2 * (v % 2) + c, :], slice(n * P, (n + 1) * P), slice(col, col + 512)
                        for k in range(EC):
                            pe.matmul(out, x1T_hi[:, k, rows], wq_hi[:, k, cols], start=(k == 0), stop=False)
                            pe.matmul(out, x1T_hi[:, k, rows], wq_lo[:, k, cols], start=False, stop=False)
                            mm = pe.matmul(out, x1T_lo[:, k, rows], wq_hi[:, k, cols], start=False,
                                           stop=(k == EC - 1))
                    mm.then_inc(q_mm, 1)
                if v >= 1:
                    w = v - 1
                    pe.wait_ge(qn_ready, w + 1)
                    if w == 0:
                        pe.wait_ge(rest_loaded, 48)
                    for s in range(2):
                        m = 2 * w + s
                        if m >= 2:
                            pe.wait_ge(qhT_ready, m - 1)
                        for g in range(4):
                            mm = pe.transpose(ps[:, 4 + s, g * P:(g + 1) * P], qn[:, w % 2, 4 * s + g, :],
                                              ident[:, :])
                        mm.then_inc(qT_mm, 1)
                    for s in range(2):
                        m = 2 * w + s
                        pe.wait_ge(qhT_ready, m + 1)
                        if m >= 2:
                            pe.wait_ge(qp_ready, m - 1)
                        for g in range(4):
                            mm = pe.matmul(ps[:, 6 + s, g * P:(g + 1) * P], wkT[:, 8 * (w % 2) + 4 * s + g, :],
                                           qhT[:, s, g, :], start=True, stop=True)
                        mm.then_inc(qp_mm, 1)

        @block.scalar
        def _(act):
            def turn_out(w):
                for s in range(2):
                    m = 2 * w + s
                    act.wait_ge(qT_mm, m + 1)
                    if m >= 2:
                        act.wait_ge(qp_mm, m - 1)
                    act.activation(qhT[:, s, :, :], ps[:, 4 + s, :].rearrange("p (g t) -> p g t", g=4), ACT.Copy,
                                   scale=gqk[:, 0:1]).then_inc(qhT_ready, 1)

            act.wait_ge(gains_ready, 1)
            for v in range(V + 1):
                if v < V:
                    act.wait_ge(q_mm, v + 1)
                    if v >= 2:
                        act.wait_ge(mean_ready, v - 1)
                    act.activation(sq[:, v % 2, :], ps[:, 2 * (v % 2):2 * (v % 2) + 2, :].rearrange("p k n -> p (k n)"),
                                   ACT.Square).then_inc(squared, 1)
                if v >= 1:
                    turn_out(v - 1)
                if v < V:
                    act.wait_ge(mean_ready, v + 1)
                    act.activation(lg[:, v % 2, :], ss[:, v % 2, :], ACT.Ln).then_inc(act_chain, 1)
                    act.wait_ge(act_chain, v + 1)
                    act.activation(rs[:, v % 2, :], lg[:, v % 2, :], ACT.Exp, scale=-0.5).then_inc(table_ready, 1)

        @block.vector
        def _(dve):
            link = linker(dve, dve_chain)
            dve.wait_ge(rest_loaded, 48)
            dve.tensor_tensor(gqk[:, :], gains[:, 0:1], gains[:, 1:2], ALU.mult).then_inc(gains_ready, 1)
            for v in range(V + 1):
                if v < V:
                    i = v % 2
                    dve.wait_ge(squared, v + 1)
                    link(dve.tensor_reduce(ss[:, i, :], sq[:, i, :].rearrange("p (h d) -> p h d", d=XD), AX.X, ALU.add))
                    dve.tensor_scalar(ss[:, i, :], ss[:, i, :], 1.0 / XD, RMS_EPS, ALU.mult, ALU.add
                                      ).then_inc(mean_ready, 1)
                if v >= 1:
                    w = v - 1
                    n, half = divmod(w, 2)
                    for s in range(2):
                        m = 2 * w + s
                        dve.wait_ge(qp_mm, m + 1)
                        dve.tensor_copy(qo[:, 8 * half + 4 * s:8 * half + 4 * s + 4, n * P:(n + 1) * P],
                                        ps[:, 6 + s, :].rearrange("p (g t) -> p g t", g=4)).then_inc(qp_ready, 1)
                if v < V:
                    dve.wait_ge(table_ready, v + 1)
                    link(rsqrt_refine(dve, link, rs[:, i, :], ss[:, i, :], rt[:, i, :]))
                    if v >= 2:
                        dve.wait_ge(qT_mm, 2 * (v - 1))
                    dve.tensor_tensor(qn[:, i, :, :],
                                      ps[:, 2 * i:2 * i + 2, :].rearrange("p k (h d) -> p (k h) d", d=XD),
                                      rs[:, i, :].unsqueeze(2).broadcast_to([P, UH, XD]), ALU.mult
                                      ).then_inc(qn_ready, 1)


class Phase:

    def __init__(self, b=None, pair=None, i=0):
        self.b, self.pair, self.i = b, pair, i

    def shift(self, n):
        return Phase(self.b + n) if self.pair is None else Phase(None, self.pair, self.i + n)

    def at(self, per_phase, const):
        if self.pair is None:
            return per_phase * self.b + const
        return self.pair * (2 * per_phase) + (per_phase * self.i + const)

    def parity(self):
        return (self.i if self.b is None else self.b) % 2

    def within(self, first, last):
        return self.b is None or first <= self.b <= last

    def tokens(self):
        start = self.at(T, 0)
        return slice(start, start + T) if self.pair is None else bass.ds(start, T)


def each_phase(eng, body, loop_end):
    for b in (-1, 0, 1):
        body(Phase(b))
    with eng.Fori(1, loop_end // 2) as pair:
        for i in range(2):
            body(Phase(None, pair, i))
    for b in range(loop_end, B + 1):
        body(Phase(b))


def wait(eng, s, value):
    if not isinstance(value, int) or value > 0:
        eng.wait_ge(s, value)


STEPS = 2 * KT
SHIFT_LAG = KT + 2
DEN_LAG = SHIFT_LAG + 1
PV_LAG = SHIFT_LAG + 3
TD = 5
NPR = 6
WH = 6


def pos_s(ph, j):
    h, t = divmod(j, KT)
    if ph.b is not None:
        u = 2 * ph.b + h
        return KT * u + t + (u - 2 + (t > TD) if u >= 2 else 0)
    return ph.at(2 * (KT + 1), (KT + 1) * h + t - 2 + (t > TD))


def pos_d(ph, h):
    if ph.b is not None:
        u = 2 * ph.b + h
        return min(KT * u + TD + 1, STEPS * B) + u - 2
    return ph.at(2 * (KT + 1), (KT + 1) * h + TD - 1)


def bank_s(ph, j):
    h, t = divmod(j, KT)
    return pos_s(ph, j) % 2 if ph.b is not None else (h + t + (t > TD)) % 2


def bank_d(ph, h):
    return pos_d(ph, h) % 2 if ph.b is not None else (h + TD + 1) % 2


def closes(ph, j):
    return j % KT == TD and (ph.b is None or 2 <= 2 * ph.b + j // KT <= 2 * B + 1)


def lagged(ph, j, lag):
    y = j - lag
    return y if ph.b is None or 0 <= STEPS * ph.b + y < STEPS * B else None


def vector_shifts(ph):
    return ph.b is not None and ph.b >= B - 1


def split_at(ph, j):
    if j % 4 or not ph.within(-1, 14):
        return None
    if j == 20:
        return (2, 0) if ph.within(-1, 13) else None
    return (1, j // 4 + 1)


def cross_attention(nc, a, qo, wk_parts, ctxT_in, probs, wk_in, wk_loaded, ctxT_loaded, vo, vo_loaded):
    ctx = ExitStack()
    with ctx:
        def sb(name, shape, dt=F32):
            return ctx.enter_context(nc.sbuf_tensor(name, shape, dt))

        def sem(name):
            return ctx.enter_context(nc.semaphore(name))

        wk_hi, wk_lo = wk_parts[:, 0, :], wk_parts[:, 1, :]
        ctxT_hi = sb("xa_ctxT_hi", [P, 2, KT, KP], F32R)
        ctxT_lo = sb("xa_ctxT_lo", [P, 2, KT, KP], F32R)
        ctx_nat = sb("xa_ctx_nat", [KP, 2, KT, C])
        q_hi = sb("xa_q_hi", [P, 2, UH, T], F32R)
        q_lo = sb("xa_q_lo", [P, 2, UH, T], F32R)
        scores = sb("xa_scores", [P, STEPS, UH, T])
        shifted = sb("xa_shifted", [KP, 2, UW])
        sq = sb("xa_sq", [KP, 2, WH * XD])
        cmax = sb("xa_cmax", [KP, 2, UW])
        gmax = sb("xa_gmax", [KP, 2, UW])
        den = sb("xa_den", [KP, 2, UW])
        rden = sb("xa_rden", [P, UW])
        lden = sb("xa_lden", [P, UW])
        ss = sb("xa_ss", [KP, KT, XH])
        lg = sb("xa_lg", [KP, KT, XH])
        nt = sb("xa_nt", [KP, KT, XH])
        rk = sb("xa_rk", [KP, 2, KT, XH])
        ones = sb("xa_ones", [KP, P])
        spare = sb("xa_spare", [KP, 1])
        k_ps = ctx.enter_context(nc.psum_tensor("xa_k_ps", [P, 2, 2, 512], F32))
        s_ps = ctx.enter_context(nc.psum_tensor("xa_s_ps", [P, 2, 512], F32))
        o_ps = ctx.enter_context(nc.psum_tensor("xa_o_ps", [P, 2, 512], F32))

        def score_slot(j):
            return scores[0:KP, j % STEPS, :, :].rearrange("p h q -> p (h q)")

        wk_hi_ready, wk_lo_ready, ones_set = (
            sem("xa_wk_hi_ready"), sem("xa_wk_lo_ready"), sem("xa_ones_set"))
        nat_loaded = [sem(f"xa_nat_loaded{i}") for i in range(2)]
        hi_ready, lo_ready = sem("xa_hi_ready"), sem("xa_lo_ready")
        qhi_ready, qlo_ready = sem("xa_qhi_ready"), sem("xa_qlo_ready")
        k_done, squared, summed = sem("xa_k_done"), sem("xa_squared"), sem("xa_summed")
        mean_ready, ln_ready, table_ready, rk_ready = (
            sem("xa_mean_ready"), sem("xa_ln_ready"), sem("xa_table_ready"), sem("xa_rk_ready"))
        den_ln, den_table, den_step = (
            sem("xa_den_ln"), sem("xa_den_table"), sem("xa_den_step"))
        newton = sem("xa_newton")
        s_done, s_taken = sem("xa_s_done"), sem("xa_s_taken")
        max_done, gmax_ready = sem("xa_max_done"), sem("xa_gmax_ready")
        shift_done, exp_done, den_done, pv_done = (
            sem("xa_shift_done"), sem("xa_exp_done"), sem("xa_den_done"), sem("xa_pv_done"))
        o_taken = sem("xa_o_taken")
        block = ctx.enter_context(nc.Block())

        @block.sync
        def _(sp):
            def load_ctxT(ph):
                src = a.ctxT[ph.b] if ph.b is not None else a.ctxT[bass.ds(ph.at(1, 0), 1)].rearrange("o c k -> (o c) k")
                sp.dma_start(ctxT_in[:, ph.parity(), :, :].rearrange("c t p -> c (t p)"), src
                             ).then_inc(ctxT_loaded[ph.parity()], 16)

            def load_nat(ph):
                src = a.ctx[ph.b].rearrange("(p t) c -> p (t c)", t=KT) if ph.b is not None else \
                    a.ctx[bass.ds(ph.at(1, 0), 1)].rearrange("o (p t) c -> (o p) (t c)", t=KT)
                sp.dma_start(ctx_nat[:, ph.parity(), :, :].rearrange("p t c -> p (t c)"), src
                             ).then_inc(nat_loaded[ph.parity()], 16)

            def body(ph):
                if ph.within(-1, 14):
                    wait(sp, pv_done, ph.at(STEPS, 0))
                    load_nat(ph.shift(1))
                if ph.within(-1, 12):
                    wait(sp, hi_ready, ph.at(KT // 2, KT))
                    wait(sp, lo_ready, ph.at(KT // 2, KT))
                    load_ctxT(ph.shift(3))
                if ph.b == B - 1:
                    sp.wait_ge(k_done, STEPS * B)
                    sp.dma_start(vo[:, :, :], a.vo).then_inc(vo_loaded, 16)

            each_phase(sp, body, 12)

        @block.gpsimd
        def _(pool):
            pool.memset(ones[:, :], 1.0).then_inc(ones_set, 1)
            pool.wait_ge(ones_set, 1)

            def q_low(ph, h):
                pool.wait_ge(qhi_ready, ph.at(2, h + 1))
                pool.tensor_tensor(q_lo[:, h, :, :], qo[:, UH * h:UH * h + UH, ph.tokens()],
                                   q_hi[:, h, :, :].bitcast(F32), ALU.subtract).then_inc(qlo_ready, 1)

            def body(ph):
                if ph.b == -1:
                    q_low(Phase(0), 0)
                    return
                for j in range(STEPS):
                    h, t = divmod(j, KT)
                    y = lagged(ph, j, SHIFT_LAG)
                    if y is not None and not vector_shifts(ph):
                        if y % KT == 0:
                            pool.wait_ge(gmax_ready, ph.at(2, y // KT + 1))
                        wait(pool, exp_done, ph.at(STEPS, y - 1))
                        pool.tensor_tensor(shifted[:, y % 2, :], score_slot(y), gmax[:, (y // KT) % 2, :],
                                           ALU.subtract).then_inc(shift_done, 1)
                    y = lagged(ph, j, DEN_LAG)
                    if y is not None and y % KT:
                        hy = (y // KT) % 2
                        wait(pool, exp_done, ph.at(STEPS, y + 1))
                        if y % KT == 1:
                            closing = ph if y > 0 else ph.shift(-1)
                            if closing.b is None or 2 * closing.b + hy >= 2:
                                wait(pool, s_done, pos_d(closing, hy) + 1)
                            pool.tensor_tensor(den[:, hy, :], probs[0:KP, y % NPR, :], probs[0:KP, (y - 1) % NPR, :], ALU.add
                                               ).then_inc(den_done, 2)
                        else:
                            wait(pool, den_done, ph.at(STEPS, y))
                            pool.tensor_tensor(den[:, hy, :], probs[0:KP, y % NPR, :], den[:, hy, :], ALU.add
                                               ).then_inc(den_done, 1)
                    if ph.within(0, 15) and t == KT - 1:
                        wait(pool, max_done, ph.at(2 * (KT - 1), (KT - 1) * (h + 1)))
                        wait(pool, shift_done, ph.at(STEPS, KT * (h - 1)))
                        pool.tensor_tensor(spare[:, :], ones[:, 0:1], ones[:, 1:2], ALU.mult)
                        pool.partition_all_reduce(gmax[:, h, :], cmax[:, h, :], KP, bass_max
                                                  ).then_inc(gmax_ready, 1)
                    if t == 6 and ph.within(0, 15) and not (ph.b == 15 and h == 1):
                        q_low(ph.shift(h), 1 - h)

            each_phase(pool, body, 14)

        @block.scalar
        def _(act):
            act.preload_act_table_set(TABLES)

            def q_high(ph, h):
                act.activation(q_hi[:, h, :, :], qo[:, UH * h:UH * h + UH, ph.tokens()], ACT.Copy
                               ).then_inc(qhi_ready, 1)

            def split_high(ph, c):
                i = ph.parity()
                act.wait_ge(ctxT_loaded[i], 16 * (ph.b // 2 + 1) if ph.b is not None else
                            ph.pair * 16 + 16 * (ph.i // 2 + 1))
                if ph.within(2, B):
                    act.wait_ge(s_done, pos_s(ph.shift(-2), KT + 2 * c + 1) + 1)
                act.activation(ctxT_hi[:, i, 2 * c:2 * c + 2, :], ctxT_in[:, i, 2 * c:2 * c + 2, :],
                               ACT.Copy).then_inc(hi_ready, 1)

            def body(ph):
                for j in range(STEPS):
                    h, t = divmod(j, KT)
                    if ph.within(-1, 14):
                        wait(act, k_done, ph.at(STEPS, STEPS + j + 1))
                        wait(act, summed, ph.at(STEPS, STEPS + j - 1))
                        k_cols = k_ps[0:KP, j % 2, :, :].rearrange("p k n -> p (k n)")
                        for g in range(WH, UH):
                            head = UH * (j % 2) + g
                            own = k_cols[:, g * XD:(g + 1) * XD]
                            act.activation(own, own, ACT.Square,
                                           accum_out=ss[:, j // 2, head:head + 1])
                        act.activation(sq[:, j % 2, :], k_cols[:, 0:WH * XD], ACT.Square).then_inc(squared, 1)
                    if split_at(ph, j):
                        ahead, c = split_at(ph, j)
                        split_high(ph.shift(ahead), c)
                    if closes(ph, j):
                        n = ph.at(2, h - 1)
                        act.wait_ge(s_done, pos_d(ph, h) + 1)
                        wait(act, o_taken, ph.at(2, h - 2))
                        act.activation(lden[:, :], s_ps[:, bank_d(ph, h), 0:UW], ACT.Ln).then_inc(den_ln, 1)
                        act.wait_ge(den_ln, n)
                        act.activation(rden[:, :], lden[:, :], ACT.Exp, scale=-1.0).then_inc(den_table, 1)
                    y = lagged(ph, j, SHIFT_LAG)
                    if y is not None:
                        wait(act, shift_done, ph.at(STEPS, y + 1))
                        wait(act, pv_done, ph.at(STEPS, y - NPR + 1))
                        wait(act, den_done, ph.at(STEPS, y - NPR + 1))
                        act.activation(probs[0:KP, y % NPR, :], shifted[:, y % 2, :], ACT.Exp).then_inc(exp_done, 1)
                    for step, ahead, g in ((13, 1, slice(0, 6)), (1, 0, slice(6, 12))):
                        if j == step and ph.shift(ahead).within(0, 15):
                            n = ph.at(2, 3 if ahead else 2)
                            act.wait_ge(mean_ready, n)
                            act.activation(lg[:, g, :], ss[:, g, :], ACT.Ln).then_inc(ln_ready, 1)
                            act.wait_ge(ln_ready, n)
                            act.activation(rk[:, ph.shift(ahead).parity(), g, :], lg[:, g, :], ACT.Exp, scale=-0.5
                                           ).then_inc(table_ready, 1)
                    if t == 4 and ph.within(0, 15) and not (ph.b == 15 and h == 1):
                        if h == 1:
                            act.wait_ge(s_done, pos_s(ph, KT - 1) + 1)
                        elif ph.b != 0:
                            act.wait_ge(s_done, pos_s(ph.shift(-1), STEPS - 1) + 1)
                        q_high(ph.shift(h), 1 - h)

            act.wait_ge(wk_loaded, 16)
            split_high(Phase(0), 0)
            for c in range(4):
                part = slice(c * 512, (c + 1) * 512)
                act.activation(wk_hi[:, part], wk_in[:, part], ACT.Copy).then_inc(wk_hi_ready, 1)
            q_high(Phase(0), 0)
            each_phase(act, body, 14)

        @block.vector
        def _(dve):
            def split_low(ph, c):
                i = ph.parity()
                dve.wait_ge(hi_ready, ph.at(KT // 2, c + 1))
                dve.tensor_tensor(ctxT_lo[:, i, 2 * c:2 * c + 2, :], ctxT_in[:, i, 2 * c:2 * c + 2, :],
                                  ctxT_hi[:, i, 2 * c:2 * c + 2, :].bitcast(F32), ALU.subtract).then_inc(lo_ready, 1)

            def body(ph):
                for j in range(STEPS):
                    h, t = divmod(j, KT)
                    if ph.within(0, 15):
                        wait(dve, s_done, pos_s(ph, j) + 1)
                        if j in (0, 6):
                            dve.wait_ge(rk_ready, ph.at(2, 1 + j // 6))
                        wait(dve, shift_done, ph.at(STEPS, j - STEPS + 1))
                        dve.tensor_tensor(scores[0:KP, j, :, :],
                                          s_ps[0:KP, bank_s(ph, j), 0:UW].rearrange("p (g q) -> p g q", q=T),
                                          rk[:, ph.parity(), t, UH * h:UH * h + UH].unsqueeze(2)
                                          .broadcast_to([KP, UH, T]), ALU.mult).then_inc(s_taken, 1)
                    if (ph.within(-1, 14) and j >= 1) or (ph.within(0, 15) and j == 0):
                        i = (j - 1) % STEPS
                        dve.wait_ge(squared, ph.at(STEPS, STEPS + j))
                        dve.tensor_reduce(ss[:, i // 2, UH * (i % 2):UH * (i % 2) + WH],
                                          sq[:, i % 2, :].rearrange("p (g d) -> p g d", d=XD), AX.X, ALU.add
                                          ).then_inc(summed, 1)
                    if ph.within(0, 15) and t >= 1:
                        dve.wait_ge(s_taken, pos_s(ph, j) + 1)
                        if t == 1:
                            wait(dve, gmax_ready, ph.at(2, h - 1))
                            dve.tensor_tensor(cmax[:, h, :], score_slot(j), score_slot(j - 1), ALU.max
                                              ).then_inc(max_done, 1)
                        else:
                            wait(dve, max_done, ph.at(2 * (KT - 1), (KT - 1) * h + t - 1))
                            dve.tensor_tensor(cmax[:, h, :], score_slot(j), cmax[:, h, :], ALU.max
                                              ).then_inc(max_done, 1)
                    for step, ahead, g in ((13, 1, slice(0, 6)), (1, 0, slice(6, 12))):
                        if not ph.shift(ahead).within(0, 15):
                            continue
                        n = 3 if ahead else 2
                        if j == step:
                            dve.wait_ge(summed, ph.at(STEPS, STEPS + KT if ahead else STEPS))
                            dve.tensor_scalar(ss[:, g, :], ss[:, g, :], 1.0 / XD, RMS_EPS, ALU.mult, ALU.add
                                              ).then_inc(mean_ready, 1)
                        if j == step + 1:
                            dve.wait_ge(table_ready, ph.at(2, n))
                            count = [0]

                            def link(ins):
                                count[0] += 1
                                ins.then_inc(newton, 1)
                                dve.wait_ge(newton, ph.at(6, 3 * (n - 1) + count[0]))

                            rsqrt_refine(dve, link, rk[:, ph.shift(ahead).parity(), g, :], ss[:, g, :], nt[:, g, :],
                                         XD ** -0.5).then_inc(rk_ready, 1)
                    y = lagged(ph, j, SHIFT_LAG)
                    if y is not None and vector_shifts(ph):
                        if y % KT == 0:
                            dve.wait_ge(gmax_ready, ph.at(2, y // KT + 1))
                        dve.wait_ge(shift_done, ph.at(STEPS, y))
                        dve.wait_ge(exp_done, ph.at(STEPS, y - 1))
                        dve.tensor_tensor(shifted[:, y % 2, :], score_slot(y), gmax[:, (y // KT) % 2, :],
                                          ALU.subtract).then_inc(shift_done, 1)
                    if closes(ph, j):
                        dve.wait_ge(den_table, ph.at(2, h - 1))
                        dve.tensor_tensor(lden[:, :], s_ps[:, bank_d(ph, h), 0:UW], rden[:, :], ALU.mult
                                          ).then_inc(s_taken, 1)
                        dve.wait_ge(s_taken, pos_d(ph, h) + 1)
                        dve.scalar_tensor_tensor(rden[:, :], lden[:, :], 2.0, rden[:, :], ALU.subtract, ALU.mult
                                                 ).then_inc(den_step, 1)
                        dve.wait_ge(den_step, ph.at(2, h - 1))
                        dve.wait_ge(pv_done, ph.at(STEPS, KT * (h - 1)))
                        dve.scalar_tensor_tensor(qo[:, UH * h:UH * h + UH, ph.shift(-1).tokens()],
                                                 o_ps[:, h, 0:UW].rearrange("p (g q) -> p g q", q=T), -1.0,
                                                 rden[:, :].rearrange("p (g q) -> p g q", q=T), ALU.mult, ALU.mult
                                                 ).then_inc(o_taken, 1)
                    if split_at(ph, j):
                        ahead, c = split_at(ph, j)
                        split_low(ph.shift(ahead), c)

            dve.wait_ge(wk_loaded, 16)
            split_low(Phase(0), 0)
            for c in range(4):
                part = slice(c * 512, (c + 1) * 512)
                dve.wait_ge(wk_hi_ready, c + 1)
                dve.tensor_tensor(wk_lo[:, part], wk_in[:, part], wk_hi[:, part].bitcast(F32), ALU.subtract
                                  ).then_inc(wk_lo_ready, 1)
            each_phase(dve, body, 14)

        @block.tensor
        def _(pe):
            def three(out, l_hi, l_lo, r_hi, r_lo):
                pe.matmul(out, l_hi, r_hi, start=True, stop=False)
                pe.matmul(out, l_hi, r_lo, start=False, stop=False)
                return pe.matmul(out, l_lo, r_hi, start=False, stop=True)

            def project_k(ph, j, c):
                if ph.b == -1 and j < 2:
                    pe.wait_ge(wk_lo_ready, 2 * j + c + 1)
                i, t, cols = ph.shift(1).parity(), j // 2, slice((2 * (j % 2) + c) * 512, (2 * (j % 2) + c + 1) * 512)
                return three(k_ps[0:KP, j % 2, c, :], ctxT_hi[:, i, t, :], ctxT_lo[:, i, t, :],
                             wk_hi[:, cols], wk_lo[:, cols])

            def body(ph):
                for j in range(STEPS):
                    h, t = divmod(j, KT)
                    if ph.within(-1, 14):
                        if j % 4 == 0:
                            pe.wait_ge(hi_ready, ph.at(KT // 2, KT // 2 + j // 4 + 1))
                            pe.wait_ge(lo_ready, ph.at(KT // 2, KT // 2 + j // 4 + 1))
                        wait(pe, squared, ph.at(STEPS, STEPS + j - 1))
                        project_k(ph, j, 0)
                    if ph.within(0, 15):
                        if t == 0:
                            pe.wait_ge(qhi_ready, ph.at(2, h + 1))
                            pe.wait_ge(qlo_ready, ph.at(2, h + 1))
                        wait(pe, s_taken, pos_s(ph, j) - 1)
                        i = ph.parity()
                        three(s_ps[0:KP, bank_s(ph, j), 0:UW], ctxT_hi[:, i, t, :], ctxT_lo[:, i, t, :],
                              q_hi[:, h, :, :].rearrange("p g q -> p (g q)"),
                              q_lo[:, h, :, :].rearrange("p g q -> p (g q)")).then_inc(s_done, 1)
                    if closes(ph, j):
                        pe.wait_ge(den_done, ph.at(STEPS, KT * (h - 1)))
                        wait(pe, s_taken, pos_d(ph, h) - 1)
                        pe.matmul(s_ps[:, bank_d(ph, h), 0:UW], ones[:, :], den[:, h, :], start=True, stop=True
                                  ).then_inc(s_done, 1)
                    if ph.within(-1, 14):
                        project_k(ph, j, 1).then_inc(k_done, 1)
                    y = lagged(ph, j, PV_LAG)
                    if y is not None:
                        ty, hy, of = y % KT, (y // KT) % 2, ph.shift(y // STEPS)
                        if ty == 0:
                            wait(pe, o_taken, ph.at(2, y // KT - 1))
                            if hy == 0:
                                pe.wait_ge(nat_loaded[of.parity()], 16 * (of.b // 2 + 1) if of.b is not None else
                                           of.pair * 16 + 16 * (of.i // 2 + 1))
                        wait(pe, exp_done, ph.at(STEPS, y + 1))
                        pe.matmul(o_ps[:, hy, 0:UW], ctx_nat[:, of.parity(), ty, :], probs[0:KP, y % NPR, :],
                                  start=(ty == 0), stop=(ty == KT - 1)).then_inc(pv_done, 1)

            pe.wait_ge(ones_set, 1)
            each_phase(pe, body, 14)


def output_and_mlp(nc, a, qo, hT_hi, hT_lo, vo, vo_lo, vo_loaded):
    ctx = ExitStack()
    with ctx:
        def sb(name, shape, dt=F32):
            return ctx.enter_context(nc.sbuf_tensor(name, shape, dt))

        def sem(name):
            return ctx.enter_context(nc.semaphore(name))

        FC = FF // P
        NHB = 4
        vo_hi = sb("om_vo_hi", [P, XH, E], F32R)
        q_hi = sb("om_q_hi", [P, 4, UH, P], F32R)
        q_lo = sb("om_q_lo", [P, 4, UH, P], F32R)
        w1_hi = sb("om_w1_hi", [P, EC, FF], F32R)
        w1 = overlay(nc, "om_w1", [P, EC, FF])
        w1_lo = sb("om_w1_lo", [P, EC, FF], F32R)
        w2_hi = sb("om_w2_hi", [P, FC, E], F32R)
        w2 = overlay(nc, "om_w2", [P, FC, E])
        w2_lo = sb("om_w2_lo", [P, FC, E], F32R)
        b1 = sb("om_b1", [P, FC])
        b2 = sb("om_b2", [P, E])
        ident = sb("om_ident", [P, P])
        x1 = sb("om_x1", [P, NT, E])
        z = sb("om_z", [P, NT, E])
        x2T_hi = sb("om_x2T_hi", [P, EC, TOK], F32R)
        x2T_lo = sb("om_x2T_lo", [P, EC, TOK], F32R)
        xb = sb("om_xb", [P, NT, E])
        h_in = sb("om_h", [P, NHB, UW])
        stat = sb("om_stat", [P, NT, 6])
        mv = sb("om_mv", [P, NT, 2])
        lna = sb("om_lna", [P, 2, NT])
        lnl = sb("om_lnl", [P, 2, NT])
        lny = sb("om_lny", [P, 2, NT])
        lnt = sb("om_lnt", [P, 2, NT])
        ps = ctx.enter_context(nc.psum_tensor("om_ps", [P, 8, 512], F32))
        x1_loaded, w_loaded, b_loaded = sem("om_x1_loaded"), sem("om_w_loaded"), sem("om_b_loaded")
        vo_hi_ready, vo_lo_ready, q_hi_ready, q_lo_ready, w_hi_ready, w_lo_ready = (
            sem("om_vo_hi_ready"), sem("om_vo_lo_ready"), sem("om_q_hi_ready"), sem("om_q_lo_ready"),
            sem("om_w_hi_ready"), sem("om_w_lo_ready"))
        z_mm, stat_ready, ln_a, ln_l, ln_y, x2_ready, xb_ready = (
            sem("om_z_mm"), sem("om_stat_ready"), sem("om_ln_a"),
            sem("om_ln_l"), sem("om_ln_y"), sem("om_x2_ready"), sem("om_xb_ready"))
        x2T_mm, x2T_hi_ready, x2T_lo_ready, h_mm, h_ready, h_hi_ready, h_lo_ready, y_mm, out_ready, stored, dve_chain = (
            sem("om_x2T_mm"), sem("om_x2T_hi_ready"), sem("om_x2T_lo_ready"), sem("om_h_mm"), sem("om_h_ready"),
            sem("om_h_hi_ready"), sem("om_h_lo_ready"), sem("om_y_mm"),
            sem("om_out_ready"), sem("om_stored"), sem("om_dve_chain"))
        GROUPS = ((0, 4), (4, 7)), ((0, 4), (4, 6), (6, 7))
        HALF_TILES = (4, NT)
        block = ctx.enter_context(nc.Block())

        @block.sync
        def _(sp):
            sp.dma_start(x1[:, :, :], a.x1.rearrange("(n p) e -> p n e", p=P)).then_inc(x1_loaded, 16)
            sp.dma_start(ident[:, :], a.ident).then_inc(x1_loaded, 16)
            sp.dma_start(w1[:, :, :], a.w1T.rearrange("(k p) f -> p k f", p=P)).then_inc(w_loaded, 16)
            sp.dma_start(w2[:, :, :], a.w2T.rearrange("(k p) e -> p k e", p=P)).then_inc(w_loaded, 16)
            sp.dma_start(b1[:, :], a.b1).then_inc(b_loaded, 16)
            sp.dma_start(b2[:, :], a.b2.partition_broadcast(P)).then_inc(b_loaded, 16)
            for n in range(NT):
                sp.wait_ge(out_ready, n + 1)
                sp.dma_start(a.out[n * P:(n + 1) * P, :], z[:, n, :]).then_inc(stored, 16)
            sp.wait_ge(stored, 16 * NT)

        @block.gpsimd
        def _(pool):
            for i, (w, hi, lo) in enumerate(((w1, w1_hi, w1_lo), (w2, w2_hi, w2_lo))):
                pool.wait_ge(w_hi_ready, i + 1)
                pool.tensor_tensor(lo[:, :, :], w[:, :, :], hi[:, :, :].bitcast(F32), ALU.subtract).then_inc(w_lo_ready, 1)
            pool.wait_ge(b_loaded, 32)
            for n in range(NT):
                pool.wait_ge(x2_ready, n + 1)
                pool.tensor_tensor(xb[:, n, :], z[:, n, :], b2[:, :], ALU.add).then_inc(xb_ready, 1)

        @block.scalar
        def _(act):
            def q_high(n):
                for s in range(2):
                    m = 2 * n + s
                    if n >= 2:
                        act.wait_ge(z_mm, n - 1)
                    act.activation(q_hi[:, m % 4, :, :], qo[:, UH * s:UH * s + UH, n * P:(n + 1) * P],
                                   ACT.Copy).then_inc(q_hi_ready, 1)
                    if n == 0:
                        for c in range(4 * s, 4 * s + 4):
                            act.activation(vo_hi[:, 2 * c:2 * c + 2, :], vo[:, 2 * c:2 * c + 2, :],
                                           ACT.Copy).then_inc(vo_hi_ready, 1)

            def table(i, g, count):
                tiles = slice(*GROUPS[i][g])
                act.wait_ge(ln_a, count)
                act.activation(lnl[:, i, tiles], lna[:, i, tiles], ACT.Ln).then_inc(ln_l, 1)
                act.wait_ge(ln_l, count)
                act.activation(lny[:, i, tiles], lnl[:, i, tiles], ACT.Exp, scale=-0.5).then_inc(ln_y, 1)

            def x2T_high(n):
                act.wait_ge(x2T_mm, n + 1)
                act.activation(x2T_hi[:, :, n * P:(n + 1) * P],
                               ps[:, n % 2, 0:EC * P].rearrange("p (k t) -> p k t", k=EC),
                               ACT.Copy).then_inc(x2T_hi_ready, 1)

            act.wait_ge(vo_loaded, 16)
            q_high(0)
            q_high(1)
            act.wait_ge(w_loaded, 32)
            for w, hi in ((w1, w1_hi), (w2, w2_hi)):
                act.activation(hi[:, :, :], w[:, :, :], ACT.Copy).then_inc(w_hi_ready, 1)
            for n in range(2, NT):
                q_high(n)
            table(0, 0, 1)
            for n in range(0, 4):
                x2T_high(n)
            table(0, 1, 2)
            act.wait_ge(b_loaded, 32)
            for m in range(2 * FC):
                n, f = divmod(m, FC)
                if m == FC:
                    for tile in range(4, NT):
                        x2T_high(tile)
                act.wait_ge(h_mm, m + 1)
                if m >= NHB:
                    act.wait_ge(h_lo_ready, m - NHB + 1)
                act.activation(h_in[:, m % NHB, :], ps[:, 2 + m % 4, 0:UW], ACT.Gelu,
                               bias=b1[:, f:f + 1]).then_inc(h_ready, 1)
                act.wait_ge(h_ready, m + 1)
                if m == 0:
                    act.wait_ge(z_mm, NT)
                    act.wait_ge(q_lo_ready, 2 * NT)
                act.activation(hT_hi[:, f, n * UW:(n + 1) * UW], h_in[:, m % NHB, :], ACT.Copy
                               ).then_inc(h_hi_ready, 1)
            act.preload_act_table_set(TABLES)
            for g in range(3):
                table(1, g, 3 + g)

        @block.vector
        def _(dve):
            link = linker(dve, dve_chain)

            def q_low(n):
                for s in range(2):
                    m = 2 * n + s
                    dve.wait_ge(q_hi_ready, m + 1)
                    dve.tensor_tensor(q_lo[:, m % 4, :, :], qo[:, UH * s:UH * s + UH, n * P:(n + 1) * P],
                                      q_hi[:, m % 4, :, :].bitcast(F32), ALU.subtract).then_inc(q_lo_ready, 1)
                    if n == 0:
                        for c in range(4 * s, 4 * s + 4):
                            dve.wait_ge(vo_hi_ready, c + 1)
                            dve.tensor_tensor(vo_lo[:, 2 * c:2 * c + 2, :], vo[:, 2 * c:2 * c + 2, :],
                                              vo_hi[:, 2 * c:2 * c + 2, :].bitcast(F32), ALU.subtract
                                              ).then_inc(vo_lo_ready, 1)

            def stats(i, n, bank, done, other):
                dve.wait_ge(done, n + 1)
                link(dve.tensor_tensor(z[:, n, :], ps[:, bank, 0:E], other[:, n, :], ALU.add))
                link(dve.bn_stats(stat[:, n, :], z[:, n, :]))
                dve.bn_aggr(mv[:, n, :], stat[:, n, :]).then_inc(stat_ready, 1)

            def variances(i, g, count):
                tiles = slice(*GROUPS[i][g])
                dve.wait_ge(stat_ready, NT * i + tiles.stop)
                dve.tensor_scalar(lna[:, i, tiles], mv[:, tiles, 1], LN_EPS, None, ALU.add).then_inc(ln_a, 1)

            def normalise(i, g, count):
                tiles = slice(*GROUPS[i][g])
                dve.wait_ge(ln_a, count)
                dve.wait_ge(ln_y, count)
                link(rsqrt_refine(dve, link, lny[:, i, tiles], lna[:, i, tiles], lnt[:, i, tiles]))
                for n in range(*GROUPS[i][g]):
                    dve.tensor_scalar(z[:, n, :], z[:, n, :], mv[:, n, 0:1], lny[:, i, n:n + 1],
                                      ALU.subtract, ALU.mult).then_inc(out_ready if i else x2_ready, 1)

            def x2T_low(n):
                dve.wait_ge(x2T_hi_ready, n + 1)
                dve.tensor_tensor(x2T_lo[:, :, n * P:(n + 1) * P],
                                  ps[:, n % 2, 0:EC * P].rearrange("p (k t) -> p k t", k=EC),
                                  x2T_hi[:, :, n * P:(n + 1) * P].bitcast(F32), ALU.subtract).then_inc(x2T_lo_ready, 1)

            q_low(0)
            q_low(1)
            dve.wait_ge(x1_loaded, 32)
            for n in range(NT):
                if n + 2 < NT:
                    q_low(n + 2)
                stats(0, n, 4 + n % 4, z_mm, x1)
                if n == 3:
                    variances(0, 0, 1)
                if n == 4:
                    normalise(0, 0, 1)
                if n == 5:
                    for tile in range(0, 4):
                        x2T_low(tile)
            variances(0, 1, 2)
            normalise(0, 1, 2)
            for m in range(2 * FC):
                n, f = divmod(m, FC)
                if m == FC:
                    for tile in range(4, NT):
                        x2T_low(tile)
                dve.wait_ge(h_hi_ready, m + 1)
                dve.tensor_tensor(hT_lo[:, f, n * UW:(n + 1) * UW], h_in[:, m % NHB, :],
                                  hT_hi[:, f, n * UW:(n + 1) * UW].bitcast(F32), ALU.subtract).then_inc(h_lo_ready, 1)
            for n in range(NT):
                dve.wait_ge(xb_ready, n + 1)
                stats(1, n, (6, 7, 0, 1)[n % 4], y_mm, xb)
                for g in range(3):
                    if n == GROUPS[1][g][1] - 1:
                        variances(1, g, 3 + g)
                        normalise(1, g, 3 + g)

        @block.tensor
        def _(pe):
            def three(out, l_hi, l_lo, r_hi, r_lo, first, last):
                pe.matmul(out, l_hi, r_hi, start=first, stop=False)
                pe.matmul(out, l_hi, r_lo, start=False, stop=False)
                return pe.matmul(out, l_lo, r_hi, start=False, stop=last)

            def project_out(n):
                if n >= 4:
                    pe.wait_ge(stat_ready, n - 3)
                for h in range(XH):
                    if h % UH == 0:
                        pe.wait_ge(q_hi_ready, 2 * n + h // UH + 1)
                        pe.wait_ge(q_lo_ready, 2 * n + h // UH + 1)
                    if n == 0:
                        pe.wait_ge(vo_lo_ready, h // 2 + 1)
                    m = (2 * n + h // UH) % 4
                    mm = three(ps[:, 4 + n % 4, 0:E], q_hi[:, m, h % UH, :], q_lo[:, m, h % UH, :],
                               vo_hi[:, h, :], vo_lo[:, h, :], h == 0, h == XH - 1)
                mm.then_inc(z_mm, 1)

            def turn(n):
                pe.wait_ge(x2_ready, n + 1)
                if n >= 2:
                    pe.wait_ge(x2T_lo_ready, n - 1)
                for k in range(EC):
                    mm = pe.transpose(ps[:, n % 2, k * P:(k + 1) * P], z[:, n, k * P:(k + 1) * P], ident[:, :])
                mm.then_inc(x2T_mm, 1)

            def up(n):
                pe.wait_ge(x2T_lo_ready, HALF_TILES[n])
                if n == 0:
                    pe.wait_ge(stat_ready, 6)
                    pe.wait_ge(w_lo_ready, 2)
                for f in range(FC):
                    m = n * FC + f
                    if m >= 4:
                        pe.wait_ge(h_ready, m - 3)
                    for k in range(EC):
                        cols = slice(n * UW, (n + 1) * UW)
                        mm = three(ps[:, 2 + m % 4, 0:UW], w1_hi[:, k, f * P:(f + 1) * P],
                                   w1_lo[:, k, f * P:(f + 1) * P], x2T_hi[:, k, cols], x2T_lo[:, k, cols],
                                   k == 0, k == EC - 1)
                    mm.then_inc(h_mm, 1)

            pe.wait_ge(x1_loaded, 32)
            for n in range(NT - 1):
                project_out(n)
            for n in range(4):
                turn(n)
            project_out(NT - 1)
            up(0)
            for n in range(4, NT):
                turn(n)
            up(1)
            for n in range(NT):
                pe.wait_ge(h_lo_ready, FC if n < 3 else 2 * FC)
                if n >= 4:
                    pe.wait_ge(stat_ready, NT + n - 3)
                rows = slice(n * P, (n + 1) * P)
                for f in range(FC):
                    mm = three(ps[:, (6, 7, 0, 1)[n % 4], 0:E], hT_hi[:, f, rows], hT_lo[:, f, rows],
                               w2_hi[:, f, :], w2_lo[:, f, :], f == 0, f == FC - 1)
                mm.then_inc(y_mm, 1)


class Arrays:
    pass


def program(nc, a):
    with ExitStack() as outer:
        vo_loaded = outer.enter_context(nc.semaphore("vo_loaded"))
        with ExitStack() as ctx:
            qo = ctx.enter_context(nc.sbuf_tensor("qo", [P, XH, TOK], F32))
            vo = overlay(nc, "vo", [P, XH, E])
            wk_parts = ctx.enter_context(nc.sbuf_tensor("wk_parts", [P, 2, XH * XD], F32R))
            ctxT_in = ctx.enter_context(nc.sbuf_tensor("ctxT_in", [P, 2, KT, KP], F32))
            probs = ctx.enter_context(nc.sbuf_tensor("probs", [P, NPR, UW], F32))
            wk_in = probs[:, :, :].rearrange("p n q -> p (n q)")[:, 0:XH * XD]
            wk_loaded = ctx.enter_context(nc.semaphore("wk_loaded"))
            ctxT_loaded = [ctx.enter_context(nc.semaphore(f"ctxT_loaded{i}")) for i in range(2)]
            xT = overlay(nc, "xT", [P, EC, TOK])
            with nc.sbuf_tensor("x1T_lo", [P, EC, TOK], F32R) as x1T_lo, \
                    nc.sbuf_tensor("x1T_hi", [P, EC, TOK], F32R) as x1T_hi, \
                    nc.sbuf_tensor("xq_lo", [P, EC * XH * XD], F32R) as xq_lo:
                self_attention(nc, a, xT, x1T_hi, x1T_lo, qo, wk_parts, xq_lo)
                query_path(nc, a, x1T_hi, x1T_lo, qo, wk_parts, xq_lo, wk_in, ctxT_in, wk_loaded, ctxT_loaded)
            cross_attention(nc, a, qo, wk_parts, ctxT_in, probs, wk_in, wk_loaded, ctxT_loaded, vo, vo_loaded)
        hT_hi = outer.enter_context(nc.sbuf_tensor("hT_hi", [P, FF // P, TOK], F32R))
        hT_lo = outer.enter_context(nc.sbuf_tensor("hT_lo", [P, FF // P, TOK], F32R))
        vo_lo = outer.enter_context(nc.sbuf_tensor("vo_lo", [P, XH, E], F32R))
        output_and_mlp(nc, a, qo, hT_hi, hT_lo, vo, vo_lo, vo_loaded)


def kernel(**inputs):
    import numpy as np
    import concourse.bacc as bacc
    from concourse.bass_utils import run_bass_kernel_spmd

    g = {k: np.asarray(v) for k, v in inputs.items()}

    def heads_in(w):
        return w.transpose(1, 0, 2).reshape(E, NH * HD)

    def columns(v):
        return v.reshape(-1, P).T

    rows = np.arange(P)
    queries, keys = np.meshgrid(rows % 64, np.arange(T), indexing="ij")
    x = g["x"].reshape(TOK, E)
    ctx = g["ctx_1024"]
    host = {
        "x": x,
        "xT": x.T,
        "ctx": ctx,
        "ctxT": ctx.reshape(B, KP, KT, C).transpose(0, 3, 2, 1).reshape(B, C, SK),
        "sa_wq": heads_in(g["L0_attn_Wq"]), "sa_wk": heads_in(g["L0_attn_Wk"]), "sa_wv": heads_in(g["L0_attn_Wv"]),
        "sa_wo": g["L0_attn_Wo"],
        "sa_bias": np.stack([columns(g["L0_attn_" + n].reshape(-1)) for n in ("bq", "bk", "bv")], axis=1),
        "sa_bo": g["L0_attn_bo"],
        "xq_w": g["L0_xattn_Wq"], "xk_w": g["L0_xattn_Wk"], "xk_wT": g["L0_xattn_Wk"].T,
        "xv_wT": g["L0_xattn_Wv"].T, "xo_w": g["L0_xattn_Wo"],
        "gains": np.stack([g["L0_xattn_gq"], g["L0_xattn_gk"]], axis=1),
        "w1T": g["L0_ffn_proj1"].T, "b1": columns(g["L0_ffn_proj1_bias"]),
        "w2T": g["L0_ffn_proj2"].T, "b2": g["L0_ffn_proj2_bias"],
        "ident": np.eye(P, dtype=np.float32),
        "causal": np.where((keys > queries) & (queries < T), np.finfo(np.float32).min, 0).astype(np.float32),
        "parity": np.stack([(rows // HD + 1) % 2, rows // HD % 2], axis=1).astype(np.float32),
    }
    nc = bacc.Bacc("TRN2", target_bir_lowering=False, num_devices=1)
    a, arrays = Arrays(), {}
    for name, v in host.items():
        v = np.ascontiguousarray(v)
        arrays["in_" + name] = v
        a.__dict__[name] = nc.dram_tensor("in_" + name, v.shape, mybir.dt.from_np(v.dtype), kind="ExternalInput").ap()
    a.out = nc.dram_tensor("out", (TOK, E), F32, kind="ExternalOutput").ap()
    a.x1 = nc.dram_tensor("x1_scratch", (TOK, E), F32, kind="Internal").ap()
    a.vo = nc.dram_tensor("vo_scratch", (P, XH, E), F32, kind="Internal").ap()
    program(nc, a)
    r = run_bass_kernel_spmd(nc, [arrays], core_ids=[0])
    return r.results[0]["out"].reshape(B, T, E)
```

```python
import concourse.bass as bass
from concourse import mybir
from contextlib import ExitStack

F32 = mybir.dt.float32
F32R = mybir.dt.float32r
ALU = mybir.AluOpType
ACT = mybir.ActivationFunctionType
AX = mybir.AxisListType

B, T, E = 16, 56, 256
C, SK = 128, 1500
NH, HD = 16, 16
XH, XD = 16, 128
FF = 1024
P = 128
TOK = B * T
NT = TOK // P
EC = E // P
KT = 12
KP = SK // KT
UH = 8
UW = UH * T
LN_EPS = 1e-5
RMS_EPS = 1e-5
bass_max = bass.bass_isa.ReduceOp.max
TABLES = "natural_log_exp_and_others"


def overlay(nc, name, shape, dt=F32):
    with nc.sbuf_tensor(name, shape, dt) as t:
        return t


def rsqrt_refine(dve, link, y, a, t, gain=1.0):
    link(dve.tensor_tensor(t, y, y, ALU.mult))
    link(dve.tensor_tensor(t, t, a, ALU.mult))
    link(dve.tensor_scalar(t, t, -0.5, 1.5, ALU.mult, ALU.add))
    return dve.scalar_tensor_tensor(y, y, gain, t, ALU.mult, ALU.mult)


def linker(dve, sem):
    n = [0]

    def link(ins):
        n[0] += 1
        ins.then_inc(sem, 1)
        dve.wait_ge(sem, n[0])
    return link


def self_attention(nc, a, ident, gains, x_nat, xT, x1T_hi, x1T_lo, qo, wk_parts, xq_lo, vo_stored):
    ctx = ExitStack()
    with ctx:
        def sb(name, shape, dt=F32):
            return ctx.enter_context(nc.sbuf_tensor(name, shape, dt))

        def sem(name):
            return ctx.enter_context(nc.semaphore(name))

        PAIRS = B // 2
        NP = 4
        wq = sb("sa_wq", [P, EC, E])
        wk = sb("sa_wk", [P, EC, E])
        wv = sb("sa_wv", [P, EC, E])
        wo = wk
        bias = sb("sa_bias", [P, 3, EC])
        bo = sb("sa_bo", [P, E])
        causal = sb("sa_causal", [P, T])
        parity = sb("sa_parity", [P, 2])
        qT = sb("sa_qT", [P, EC, TOK + 8])
        kT2 = sb("sa_kT2", [P, EC, 2, TOK])
        vbd = sb("sa_vbd", [P, B, NH // 2, 2 * HD])
        probs = sb("sa_probs", [P, NP, NH, 64])
        pT = sb("sa_pT", [P, 2, NH // 2, P])
        yT = sb("sa_yT", [P, EC, TOK])
        z = x_nat
        stat = sb("sa_stat", [P, NT, 6])
        mv = sb("sa_mv", [P, NT, 2])
        rmax = sb("sa_rmax", [P, NP, NH])
        rsum = sb("sa_rsum", [P, 2, NH])
        lna = sb("sa_lna", [P, NT])
        lnl = sb("sa_lnl", [P, NT])
        lny = sb("sa_lny", [P, NT])
        lnt = sb("sa_lnt", [P, NT])
        ps = ctx.enter_context(nc.psum_tensor("sa_ps", [P, 8, 512], F32))
        scratch = qo[:, :, :].rearrange("p h t -> p (h t)")
        xwvT = scratch[:, 0:XH * C].rearrange("p (h c) -> p h c", h=XH)
        xwo = scratch[:, XH * C:XH * (C + E)].rearrange("p (h e) -> p h e", h=XH)
        vo = scratch[:, XH * (C + E):XH * (C + 2 * E)]
        xwq = scratch[:, XH * (C + 2 * E):XH * (C + 2 * E) + EC * XH * XD]
        xq_hi = wk_parts[:, :, :].rearrange("p s n -> p (s n)")
        WQ_PART = EC * XH * XD // PAIRS

        q_loaded, v_loaded, bias_loaded, ident_loaded, x_loaded, o_loaded, xvo_loaded, xwq_loaded = (
            sem("sa_q_loaded"), sem("sa_v_loaded"), sem("sa_bias_loaded"), sem("sa_ident_loaded"),
            sem("sa_x_loaded"), sem("sa_o_loaded"), sem("sa_xvo_loaded"), sem("sa_xwq_loaded"))
        WARM = 3
        VO_BESIDE = {5: (0, 1), 6: (2, 3)}
        OUT_BESIDE = {6: (0, 1), 7: (2, 3)}
        warm_set, k_loaded = sem("sa_warm_set"), sem("sa_k_loaded")
        cleared, xb_ready = sem("sa_cleared"), sem("sa_xb_ready")
        qT_mm, kT_mm, v_mm, qT_ready, kT_ready, v_low, v_high = (
            sem("sa_qT_mm"), sem("sa_kT_mm"), sem("sa_v_mm"), sem("sa_qT_ready"), sem("sa_kT_ready"),
            sem("sa_v_low"), sem("sa_v_high"))
        s_mm, s_masked, max_ready, shifted, exped, sum_ready, normed = (
            sem("sa_s_mm"), sem("sa_s_masked"), sem("sa_max_ready"), sem("sa_shifted"), sem("sa_exped"),
            sem("sa_sum_ready"), sem("sa_normed"))
        pT_mm, pT_ready, y_mm, yT_ready = sem("sa_pT_mm"), sem("sa_pT_ready"), sem("sa_y_mm"), sem("sa_yT_ready")
        vo_mm, vo_ready, xq_hi_ready, xq_lo_ready = (
            sem("sa_vo_mm"), sem("sa_vo_ready"), sem("sa_xq_hi_ready"), sem("sa_xq_lo_ready"))
        o_mm, stat_ready, ln_table, x1_ready, x1T_mm, hi_ready, lo_ready, dve_chain, ln_log, ln_est = (
            sem("sa_o_mm"), sem("sa_stat_ready"), sem("sa_ln_table"), sem("sa_x1_ready"),
            sem("sa_x1T_mm"), sem("sa_hi_ready"), sem("sa_lo_ready"), sem("sa_dve_chain"),
            sem("sa_ln_log"), sem("sa_ln_est"))
        GROUPS = (0, 4), (4, NT)
        block = ctx.enter_context(nc.Block())

        @block.sync
        def _(sp):
            sp.dma_start(wq[:, :, :], a.sa_wq.rearrange("(k p) n -> p k n", p=P)).then_inc(q_loaded, 16)
            for k in range(EC):
                sp.dma_start(xT[:, k, :], a.xT[k * P:(k + 1) * P, :]).then_inc(q_loaded, 16)
            sp.dma_start(wk[:, :, :], a.sa_wk.rearrange("(k p) n -> p k n", p=P)).then_inc(k_loaded, 16)
            sp.dma_start(wv[:, :, :], a.sa_wv.rearrange("(k p) n -> p k n", p=P)).then_inc(v_loaded, 16)
            sp.dma_start(xwq.rearrange("p (k n) -> p k n", k=EC), a.xq_w.rearrange("(k p) n -> p k n", p=P)
                         ).then_inc(xwq_loaded, 16)
            sp.dma_start(x_nat[:, :, :], a.x.rearrange("(n p) e -> p n e", p=P)).then_inc(x_loaded, 16)
            sp.dma_start(bo[:, :], a.sa_bo.partition_broadcast(P)).then_inc(x_loaded, 16)
            sp.dma_start(xwvT, a.xv_wT.rearrange("(h d) c -> d h c", d=XD)).then_inc(xvo_loaded, 16)
            sp.dma_start(xwo, a.xo_w.rearrange("(h d) e -> d h e", d=XD)).then_inc(xvo_loaded, 16)
            sp.wait_ge(kT_mm, 4)
            sp.dma_start(wo[:, :, :], a.sa_wo.rearrange("(k p) n -> p k n", p=P)).then_inc(o_loaded, 16)
            sp.wait_ge(vo_ready, XH // 4)
            half = XH * E // 2
            sp.dma_start(a.vo.rearrange("p h e -> p (h e)")[:, 0:half], vo[:, 0:half]).then_inc(vo_stored, 16)
            sp.wait_ge(vo_ready, XH // 2)
            sp.dma_start(a.vo.rearrange("p h e -> p (h e)")[:, half:], vo[:, half:]).then_inc(vo_stored, 16)

        @block.gpsimd
        def _(pool):
            pool.memset(qT[:, :, TOK:TOK + 8], 0.0).then_inc(cleared, 1)
            pool.memset(vbd[:, :, :, :], 0.0).then_inc(cleared, 1)
            pool.memset(probs[:, :, :, :], 0.0).then_inc(cleared, 1)

            def shift(p):
                pr = probs[:, p % NP, :, 0:T]
                pool.wait_ge(max_ready, p + 1)
                pool.tensor_tensor(pr, pr, rmax[:, p % NP, :].unsqueeze(2).broadcast_to([P, NH, T]),
                                   ALU.subtract).then_inc(shifted, 1)

            def norm(p):
                pr = probs[:, p % NP, :, 0:T]
                pool.wait_ge(sum_ready, p + 1)
                pool.tensor_tensor(pr, pr, rsum[:, p % 2, :].unsqueeze(2).broadcast_to([P, NH, T]),
                                   ALU.mult).then_inc(normed, 1)

            for p in range(3):
                shift(p)
            norm(0)
            for p in range(PAIRS):
                if p + 1 < PAIRS:
                    norm(p + 1)
                if p + 3 < PAIRS:
                    shift(p + 3)
                if p == 5:
                    pool.wait_ge(x_loaded, 32)
                if p >= 5:
                    for n in ((0, 1, 2), (3, 4), (5, 6))[p - 5]:
                        pool.tensor_tensor(x_nat[:, n, :], x_nat[:, n, :], bo[:, :], ALU.add).then_inc(xb_ready, 1)

        @block.scalar
        def _(act):
            act.dma_start(bias[:, :, :], a.sa_bias).then_inc(bias_loaded, 16)
            act.dma_start(parity[:, :], a.parity).then_inc(bias_loaded, 16)
            act.dma_start(causal[:, :], a.causal).then_inc(bias_loaded, 16)
            act.dma_start(ident[:, :], a.ident).then_inc(ident_loaded, 16)
            act.dma_start(gains[:, :], a.gains).then_inc(ident_loaded, 16)
            act.preload_act_table_set(TABLES)
            act.wait_ge(bias_loaded, 48)
            for m in range(4):
                i, n = divmod(m, 2)
                act.wait_ge(qT_mm, m + 1)
                act.activation(qT[:, i, n * UW:(n + 1) * UW], ps[:, m, 0:UW], ACT.Identity,
                               bias=bias[:, 0, i:i + 1]).then_inc(qT_ready, 1)

            def take_v(m):
                act.wait_ge(v_mm, m + 1)
                if m == 0:
                    act.wait_ge(cleared, 2)
                act.activation(vbd[0:T, 4 * m:4 * m + 4, :, 0:HD],
                               ps[0:T, m, :].rearrange("p (b g d) -> p b g d", b=4, d=HD),
                               ACT.Copy).then_inc(v_low, 1)

            def exp(p):
                pr = probs[:, p % NP, :, 0:T]
                act.wait_ge(shifted, p + 1)
                act.activation(pr, pr, ACT.Exp).then_inc(exped, 1)

            def take_pT(p):
                act.wait_ge(pT_mm, p + 1)
                if p >= 2:
                    act.wait_ge(y_mm, p - 1)
                act.activation(pT[:, p % 2, :, :], ps[:, 0:2, :].rearrange("p k (g q) -> p (k g) q", q=P),
                               ACT.Copy).then_inc(pT_ready, 1)

            def take_y(p):
                act.wait_ge(y_mm, p + 1)
                for i in range(EC):
                    act.activation(yT[:, i, 2 * p * T:2 * (p + 1) * T], ps[:, 2 + p % 2, i * 128:i * 128 + 2 * T],
                                   ACT.Identity, bias=bias[:, 2, i:i + 1]).then_inc(yT_ready, 1)

            def take_vo(m):
                act.wait_ge(vo_mm, m + 1)
                act.activation(vo[:, m * 2 * E:(m + 1) * 2 * E], ps[:, 6 + m % 2, :], ACT.Copy).then_inc(vo_ready, 1)

            def table(g):
                tiles = slice(*GROUPS[g])
                act.wait_ge(ln_table, g + 1)
                act.activation(lnl[:, tiles], lna[:, tiles], ACT.Ln).then_inc(ln_log, 1)
                act.wait_ge(ln_log, g + 1)
                act.activation(lny[:, tiles], lnl[:, tiles], ACT.Exp, scale=-0.5).then_inc(ln_est, 1)

            def x1T_high(n):
                act.wait_ge(x1T_mm, n + 1)
                act.activation(x1T_hi[:, :, n * P:(n + 1) * P],
                               ps[:, n % 4, 0:EC * P].rearrange("p (k t) -> p k t", k=EC),
                               ACT.Copy).then_inc(hi_ready, 1)

            for m in range(4):
                take_v(m)
                if m < 3:
                    exp(m)
            act.wait_ge(xwq_loaded, 16)
            for p in range(PAIRS):
                take_pT(p)
                if p >= 1:
                    take_y(p - 1)
                if p + 3 < PAIRS:
                    exp(p + 3)
                part = slice(p * WQ_PART, (p + 1) * WQ_PART)
                act.activation(xq_hi[:, part], xwq[:, part], ACT.Copy).then_inc(xq_hi_ready, 1)
                for m in VO_BESIDE.get(p, ()):
                    take_vo(m)
            table(0)
            take_y(PAIRS - 1)
            take_vo(4)
            take_vo(5)
            x1T_high(0)
            x1T_high(1)
            table(1)
            x1T_high(2)
            x1T_high(3)
            take_vo(6)
            take_vo(7)
            for n in range(*GROUPS[1]):
                x1T_high(n)

        @block.vector
        def _(dve):
            link = linker(dve, dve_chain)
            dve.memset(pT[:, 0, 0:4, :], 0.0).then_inc(warm_set, 1)
            dve.wait_ge(bias_loaded, 48)
            for m in range(4):
                i, n = divmod(m, 2)
                dve.wait_ge(kT_mm, m + 1)
                for par in range(2):
                    dve.tensor_scalar(kT2[:, i, par, n * UW:(n + 1) * UW], ps[:, 4 + m, 0:UW],
                                      bias[:, 1, i:i + 1], parity[:, par:par + 1],
                                      ALU.add, ALU.mult).then_inc(kT_ready, 1)

            def take_v(m):
                dve.wait_ge(v_mm, m + 1)
                if m == 0:
                    dve.wait_ge(cleared, 2)
                dve.tensor_copy(vbd[64:64 + T, 4 * m:4 * m + 4, :, HD:2 * HD],
                                ps[64:64 + T, m, :].rearrange("p (b g d) -> p b g d", b=4, d=HD)
                                ).then_inc(v_high, 1)

            def head_rows(p):
                dve.wait_ge(s_mm, p + 1)
                if p == 0:
                    dve.wait_ge(cleared, 3)
                if p >= NP:
                    dve.wait_ge(pT_mm, p - NP + 1)
                for i in range(EC):
                    for o in range(2):
                        col = 2 * T * i + T * o
                        dve.scalar_tensor_tensor(
                            probs[:, p % NP, 8 * i + o:8 * i + 8:2, 0:T], ps[:, 4:8, col:col + T], HD ** -0.5,
                            causal[:, :].unsqueeze(1).broadcast_to([P, 4, T]), ALU.mult, ALU.add
                        ).then_inc(s_masked, 1)
                dve.wait_ge(s_masked, 4 * (p + 1))
                dve.tensor_reduce(rmax[:, p % NP, :], probs[:, p % NP, :, 0:T], AX.X, ALU.max).then_inc(max_ready, 1)

            def row_sums(p):
                dve.wait_ge(exped, p + 1)
                if p >= 2:
                    dve.wait_ge(normed, p - 1)
                link(dve.tensor_reduce(rsum[:, p % 2, :], probs[:, p % NP, :, 0:T], AX.X, ALU.add))
                dve.reciprocal(rsum[:, p % 2, :], rsum[:, p % 2, :]).then_inc(sum_ready, 1)

            def stats(n):
                dve.wait_ge(o_mm, n + 1)
                dve.wait_ge(xb_ready, n + 1)
                link(dve.tensor_tensor(z[:, n, :], ps[:, 4 + n % 2, 0:E], z[:, n, :], ALU.add))
                link(dve.bn_stats(stat[:, n, :], z[:, n, :]))
                dve.bn_aggr(mv[:, n, :], stat[:, n, :]).then_inc(stat_ready, 1)

            def variances(g):
                tiles = slice(*GROUPS[g])
                dve.wait_ge(stat_ready, tiles.stop)
                dve.tensor_scalar(lna[:, tiles], mv[:, tiles, 1], LN_EPS, None, ALU.add).then_inc(ln_table, 1)

            def normalise(g):
                tiles = slice(*GROUPS[g])
                dve.wait_ge(ln_table, g + 1)
                dve.wait_ge(ln_est, g + 1)
                link(rsqrt_refine(dve, link, lny[:, tiles], lna[:, tiles], lnt[:, tiles]))
                for n in range(*GROUPS[g]):
                    dve.tensor_scalar(z[:, n, :], z[:, n, :], mv[:, n, 0:1], lny[:, n:n + 1],
                                      ALU.subtract, ALU.mult).then_inc(x1_ready, 1)

            def x1T_low(n):
                dve.wait_ge(hi_ready, n + 1)
                dve.tensor_tensor(x1T_lo[:, :, n * P:(n + 1) * P],
                                  ps[:, n % 4, 0:EC * P].rearrange("p (k t) -> p k t", k=EC),
                                  x1T_hi[:, :, n * P:(n + 1) * P].bitcast(F32), ALU.subtract).then_inc(lo_ready, 1)

            for p in range(3):
                head_rows(p)
                take_v(p)
            row_sums(0)
            take_v(3)
            for p in range(PAIRS):
                if p + 1 < PAIRS:
                    row_sums(p + 1)
                if p + 3 < PAIRS:
                    head_rows(p + 3)
                if p >= 1:
                    part = slice((p - 1) * WQ_PART, p * WQ_PART)
                    dve.wait_ge(xq_hi_ready, p)
                    dve.tensor_tensor(xq_lo[:, part], xwq[:, part], xq_hi[:, part].bitcast(F32), ALU.subtract
                                      ).then_inc(xq_lo_ready, 1)
                for n in OUT_BESIDE.get(p, ()):
                    stats(n)
            variances(0)
            stats(4)
            normalise(0)
            stats(5)
            stats(6)
            variances(1)
            x1T_low(0)
            x1T_low(1)
            part = slice((PAIRS - 1) * WQ_PART, PAIRS * WQ_PART)
            dve.wait_ge(xq_hi_ready, PAIRS)
            dve.tensor_tensor(xq_lo[:, part], xwq[:, part], xq_hi[:, part].bitcast(F32), ALU.subtract
                              ).then_inc(xq_lo_ready, 1)
            normalise(1)
            for n in range(2, NT):
                x1T_low(n)

        @block.tensor
        def _(pe):
            pe.wait_ge(warm_set, 1)
            for _ in range(WARM):
                pe.matmul(ps[:, 0, :], pT[:, 0, 0, :], pT[:, 0, 0:4, :], start=True, stop=True)
            pe.wait_ge(q_loaded, 48)
            for w, base, done in ((wq, 0, qT_mm), (wk, 4, kT_mm)):
                if w is wk:
                    pe.wait_ge(k_loaded, 16)
                for m in range(4):
                    i, n = divmod(m, 2)
                    for k in range(EC):
                        mm = pe.matmul(ps[:, base + m, 0:UW], w[:, k, i * P:(i + 1) * P],
                                       xT[:, k, n * UW:(n + 1) * UW], start=(k == 0), stop=(k == EC - 1))
                    mm.then_inc(done, 1)

            def project_v(m):
                if m == 0:
                    pe.wait_ge(v_loaded, 16)
                pe.wait_ge(qT_ready, m + 1)
                for b in range(4 * m, 4 * m + 4):
                    for par in range(2):
                        for k in range(EC):
                            mm = pe.matmul(ps[64 * par:64 * par + T, m, (b % 4) * P:(b % 4 + 1) * P],
                                           xT[:, k, b * T:(b + 1) * T],
                                           wv[:, k, :].rearrange("p (g q d) -> p q g d", q=2, d=HD)[:, par],
                                           start=(k == 0), stop=(k == EC - 1))
                mm.then_inc(v_mm, 1)

            def scores(p):
                if p >= 1:
                    pe.wait_ge(s_masked, 4 * p)
                else:
                    pe.wait_ge(kT_ready, 8)
                    pe.wait_ge(qT_ready, 4)
                    pe.wait_ge(cleared, 1)
                for e in range(2):
                    b = 2 * p + e
                    for i in range(EC):
                        for r in range(4):
                            rows = slice(32 * r, 32 * r + 32)
                            col = 2 * T * i
                            mm = pe.matmul(ps[64 * e:64 * e + 64, 4 + r, col:col + 2 * T],
                                           qT[rows, i, b * T:b * T + 64], kT2[rows, i, :, b * T:(b + 1) * T],
                                           start=True, stop=True)
                mm.then_inc(s_mm, 1)

            def turn(p):
                pe.wait_ge(normed, p + 1)
                if p >= 1:
                    pe.wait_ge(pT_ready, p)
                else:
                    pe.wait_ge(v_low, 4)
                    pe.wait_ge(v_high, 4)
                    pe.wait_ge(ident_loaded, 32)
                for g in range(NH // 2):
                    mm = pe.transpose(ps[:, g // 4, (g % 4) * P:(g % 4 + 1) * P],
                                      probs[:, p % NP, 2 * g:2 * g + 2, :], ident[:, :])
                mm.then_inc(pT_mm, 1)

            def weigh(p):
                pe.wait_ge(pT_ready, p + 1)
                if p >= 2:
                    pe.wait_ge(yT_ready, 2 * (p - 1))
                for e in range(2):
                    for g in range(NH // 2):
                        r = 32 * (g % 4)
                        mm = pe.matmul(ps[r:r + 32, 2 + p % 2, (g // 4) * P + e * T:(g // 4) * P + (e + 1) * T],
                                       vbd[:, 2 * p + e, g, :], pT[:, p % 2, g, 64 * e:64 * e + T],
                                       start=True, stop=True)
                mm.then_inc(y_mm, 1)

            def project_out(n):
                if n == 0:
                    pe.wait_ge(o_loaded, 16)
                    pe.wait_ge(s_masked, 4 * PAIRS)
                pe.wait_ge(yT_ready, 2 * ((n * P + P - 1) // (2 * T) + 1))
                if n >= 2:
                    pe.wait_ge(stat_ready, n - 1)
                for k in range(EC):
                    mm = pe.matmul(ps[:, 4 + n % 2, 0:E], yT[:, k, n * P:(n + 1) * P], wo[:, k, :],
                                   start=(k == 0), stop=(k == EC - 1))
                mm.then_inc(o_mm, 1)

            def project_vo(m):
                if m == 0:
                    pe.wait_ge(xvo_loaded, 32)
                    pe.wait_ge(s_masked, 4 * PAIRS)
                if m >= 2:
                    pe.wait_ge(vo_ready, m - 1)
                for h in (2 * m, 2 * m + 1):
                    mm = pe.matmul(ps[:, 6 + m % 2, (h % 2) * E:(h % 2 + 1) * E], xwvT[:, h, :], xwo[:, h, :],
                                   start=True, stop=True)
                mm.then_inc(vo_mm, 1)

            def turn_x1(n):
                pe.wait_ge(x1_ready, n + 1)
                if n == 0:
                    pe.wait_ge(yT_ready, 2 * PAIRS)
                if n >= 4:
                    pe.wait_ge(lo_ready, n - 3)
                for k in range(EC):
                    mm = pe.transpose(ps[:, n % 4, k * P:(k + 1) * P], z[:, n, k * P:(k + 1) * P], ident[:, :])
                mm.then_inc(x1T_mm, 1)

            for p in range(3):
                scores(p)
                project_v(p)
            project_v(3)
            for p in range(PAIRS):
                if p + 3 < PAIRS:
                    scores(p + 3)
                turn(p)
                if p >= 1:
                    weigh(p - 1)
                for n in OUT_BESIDE.get(p, ()):
                    project_out(n)
                for m in VO_BESIDE.get(p, ()):
                    project_vo(m)
            weigh(PAIRS - 1)
            for n in range(4, NT):
                project_out(n)
            project_vo(4)
            project_vo(5)
            for n in range(*GROUPS[0]):
                turn_x1(n)
            project_vo(6)
            project_vo(7)
            for n in range(*GROUPS[1]):
                turn_x1(n)


def query_path(nc, a, ident, gains, x1T_hi, x1T_lo, qo, wk_parts, xq_lo, wk_in, ctxT_in, wk_loaded, ctxT_loaded,
               x_nat, vo_stored):
    ctx = ExitStack()
    with ctx:
        def sb(name, shape, dt=F32):
            return ctx.enter_context(nc.sbuf_tensor(name, shape, dt))

        def sem(name):
            return ctx.enter_context(nc.semaphore(name))

        QH = 4
        wq_hi = wk_parts
        wq_lo = xq_lo[:, :].rearrange("p (k n) -> p k n", k=EC)
        wkT = sb("xq_wkT", [P, XH, C])
        gqk = sb("xq_gqk", [P, 1])
        sq = sb("xq_sq", [P, 2, QH * XD])
        qn = sb("xq_qn", [P, 4, QH, XD])
        qhT = sb("xq_qhT", [P, 2, QH, P])
        ss = sb("xq_ss", [P, 2, QH])
        lg = sb("xq_lg", [P, 2, QH])
        rs = sb("xq_rs", [P, 2, QH])
        rt = sb("xq_rt", [P, 2, QH])
        ps = ctx.enter_context(nc.psum_tensor("xq_ps", [P, 8, 512], F32))
        wkT_loaded = [sem(f"xq_wkT_loaded{i}") for i in range(XH // QH)]
        x1_stored, gains_ready = sem("xq_x1_stored"), sem("xq_gains_ready")
        q_mm, squared, mean_ready, table_ready, qn_ready, dve_chain, act_chain = (
            sem("xq_q_mm"), sem("xq_squared"), sem("xq_mean_ready"), sem("xq_table_ready"), sem("xq_qn_ready"),
            sem("xq_dve_chain"), sem("xq_act_chain"))
        qT_mm, qhT_ready, qp_mm, qp_ready = (
            sem("xq_qT_mm"), sem("xq_qhT_ready"), sem("xq_qp_mm"), sem("xq_qp_ready"))
        block = ctx.enter_context(nc.Block())

        V = (XH // QH) * NT
        TURN_LAG, QP_LAG = 2, 3

        @block.sync
        def _(sp):
            for i in range(XH // QH):
                heads = slice(i * QH, (i + 1) * QH)
                sp.dma_start(wkT[:, heads, :], a.xk_wT.rearrange("(h d) c -> d h c", d=XD)[:, heads, :]
                             ).then_inc(wkT_loaded[i], 16)
            sp.dma_start(a.x1.rearrange("(n p) e -> p n e", p=P), x_nat[:, :, :]).then_inc(x1_stored, 16)
            sp.dma_start(wk_in, a.xk_w).then_inc(wk_loaded, 16)
            for b in range(2):
                sp.dma_start(ctxT_in[:, b, :, :].rearrange("c t p -> c (t p)"), a.ctxT[b]
                             ).then_inc(ctxT_loaded[b], 16)
            sp.wait_ge(x1_stored, 16)
            sp.wait_ge(vo_stored, 32)

        @block.tensor
        def _(pe):
            def project(v):
                n, quarter = divmod(v, XH // QH)
                if v >= 4:
                    pe.wait_ge(qn_ready, v - 3)
                out, rows, cols = ps[:, v % 4, :], slice(n * P, (n + 1) * P), slice(quarter * 512, (quarter + 1) * 512)
                for k in range(EC):
                    pe.matmul(out, x1T_hi[:, k, rows], wq_hi[:, k, cols], start=(k == 0), stop=False)
                    pe.matmul(out, x1T_hi[:, k, rows], wq_lo[:, k, cols], start=False, stop=False)
                    mm = pe.matmul(out, x1T_lo[:, k, rows], wq_hi[:, k, cols], start=False, stop=(k == EC - 1))
                mm.then_inc(q_mm, 1)

            def turn(v):
                pe.wait_ge(qn_ready, v + 1)
                if v >= 2:
                    pe.wait_ge(qhT_ready, v - 1)
                for g in range(QH):
                    mm = pe.transpose(ps[:, 4 + v % 2, g * P:(g + 1) * P], qn[:, v % 4, g, :], ident[:, :])
                mm.then_inc(qT_mm, 1)

            def project_to_ctx(v):
                if v < XH // QH:
                    pe.wait_ge(wkT_loaded[v], 16)
                pe.wait_ge(qhT_ready, v + 1)
                if v >= 2:
                    pe.wait_ge(qp_ready, v - 1)
                for g in range(QH):
                    mm = pe.matmul(ps[:, 6 + v % 2, g * P:(g + 1) * P], wkT[:, QH * (v % (XH // QH)) + g, :],
                                   qhT[:, v % 2, g, :], start=True, stop=True)
                mm.then_inc(qp_mm, 1)

            for v in range(V + QP_LAG):
                if v < V:
                    project(v)
                if TURN_LAG <= v < V + TURN_LAG:
                    turn(v - TURN_LAG)
                if v >= QP_LAG:
                    project_to_ctx(v - QP_LAG)

        @block.scalar
        def _(act):
            act.wait_ge(gains_ready, 1)
            for v in range(V + TURN_LAG):
                if v < V:
                    act.wait_ge(q_mm, v + 1)
                    if v >= 2:
                        act.wait_ge(mean_ready, v - 1)
                    act.activation(sq[:, v % 2, :], ps[:, v % 4, :], ACT.Square).then_inc(squared, 1)
                if v >= TURN_LAG:
                    w = v - TURN_LAG
                    act.wait_ge(qT_mm, w + 1)
                    if w >= 2:
                        act.wait_ge(qp_mm, w - 1)
                    act.activation(qhT[:, w % 2, :, :], ps[:, 4 + w % 2, :].rearrange("p (g t) -> p g t", g=QH),
                                   ACT.Copy, scale=gqk[:, 0:1]).then_inc(qhT_ready, 1)
                if v < V:
                    act.wait_ge(mean_ready, v + 1)
                    act.activation(lg[:, v % 2, :], ss[:, v % 2, :], ACT.Ln).then_inc(act_chain, 1)
                    act.wait_ge(act_chain, v + 1)
                    act.activation(rs[:, v % 2, :], lg[:, v % 2, :], ACT.Exp, scale=-0.5).then_inc(table_ready, 1)

        @block.vector
        def _(dve):
            link = linker(dve, dve_chain)
            dve.tensor_tensor(gqk[:, :], gains[:, 0:1], gains[:, 1:2], ALU.mult).then_inc(gains_ready, 1)
            for v in range(V + QP_LAG):
                i = v % 2
                if v < V:
                    dve.wait_ge(squared, v + 1)
                    link(dve.tensor_reduce(ss[:, i, :], sq[:, i, :].rearrange("p (h d) -> p h d", d=XD), AX.X, ALU.add))
                    dve.tensor_scalar(ss[:, i, :], ss[:, i, :], 1.0 / XD, RMS_EPS, ALU.mult, ALU.add
                                      ).then_inc(mean_ready, 1)
                if v >= QP_LAG:
                    w = v - QP_LAG
                    n, quarter = divmod(w, XH // QH)
                    dve.wait_ge(qp_mm, w + 1)
                    if w == 0:
                        dve.wait_ge(vo_stored, 32)
                    dve.tensor_copy(qo[:, QH * quarter:QH * (quarter + 1), n * P:(n + 1) * P],
                                    ps[:, 6 + w % 2, :].rearrange("p (g t) -> p g t", g=QH)).then_inc(qp_ready, 1)
                if v < V:
                    dve.wait_ge(table_ready, v + 1)
                    link(rsqrt_refine(dve, link, rs[:, i, :], ss[:, i, :], rt[:, i, :]))
                    if v >= 4:
                        dve.wait_ge(qT_mm, v - 3)
                    dve.tensor_tensor(qn[:, v % 4, :, :], ps[:, v % 4, :].rearrange("p (h d) -> p h d", d=XD),
                                      rs[:, i, :].unsqueeze(2).broadcast_to([P, QH, XD]), ALU.mult
                                      ).then_inc(qn_ready, 1)


class Phase:

    def __init__(self, b=None, pair=None, i=0):
        self.b, self.pair, self.i = b, pair, i

    def shift(self, n):
        return Phase(self.b + n) if self.pair is None else Phase(None, self.pair, self.i + n)

    def at(self, per_phase, const):
        if self.pair is None:
            return per_phase * self.b + const
        return self.pair * (2 * per_phase) + (per_phase * self.i + const)

    def parity(self):
        return (self.i if self.b is None else self.b) % 2

    def within(self, first, last):
        return self.b is None or first <= self.b <= last

    def tokens(self):
        start = self.at(T, 0)
        return slice(start, start + T) if self.pair is None else bass.ds(start, T)


def each_phase(eng, body, loop_end):
    for b in (-1, 0, 1):
        body(Phase(b))
    with eng.Fori(1, loop_end // 2) as pair:
        for i in range(2):
            body(Phase(None, pair, i))
    for b in range(loop_end, B + 1):
        body(Phase(b))


def wait(eng, s, value):
    if not isinstance(value, int) or value > 0:
        eng.wait_ge(s, value)


STEPS = 2 * KT
SHIFT_LAG = KT + 2
EXP_LAG = SHIFT_LAG + 1
DEN_LAG = EXP_LAG + 1
PV_LAG = EXP_LAG + 3
TD = 6
NPR = 6
EARLY = 3
NAT_LAG = 9
WH = 6


def pos_s(ph, j):
    h, t = divmod(j, KT)
    if ph.b is not None:
        u = 2 * ph.b + h
        return KT * u + t + (u - 2 + (t > TD) if u >= 2 else 0)
    return ph.at(2 * (KT + 1), (KT + 1) * h + t - 2 + (t > TD))


def pos_d(ph, h):
    if ph.b is not None:
        u = 2 * ph.b + h
        return min(KT * u + TD + 1, STEPS * B) + u - 2
    return ph.at(2 * (KT + 1), (KT + 1) * h + TD - 1)


def bank_s(ph, j):
    h, t = divmod(j, KT)
    return pos_s(ph, j) % 2 if ph.b is not None else (h + t + (t > TD)) % 2


def bank_d(ph, h):
    return pos_d(ph, h) % 2 if ph.b is not None else (h + TD + 1) % 2


def closes(ph, j):
    return j % KT == TD and (ph.b is None or 2 <= 2 * ph.b + j // KT <= 2 * B + 1)


def lagged(ph, j, lag):
    y = j - lag
    return y if ph.b is None or 0 <= STEPS * ph.b + y < STEPS * B else None


def in_parts(ph, y):
    of = ph.shift(y // STEPS)
    return y % 3 == 2 and of.within(0, B - 3)


def nat_split_at(ph, j):
    t = j - NAT_LAG
    return t if 0 <= t < KT and t % 3 == 2 and ph.within(0, B - 3) else None


def parts_count(ph, y):
    return ph.at(STEPS // 3, 4 * (y // KT) + y % KT // 3 + 1)


def vector_shifts(ph, y):
    after_max = (y + SHIFT_LAG) % KT == 1
    return ph.b is not None and (ph.b == B - 1 and (y % 4 != 3 or after_max) or ph.b == B)


def vector_adds(ph, y):
    return ph.b is not None and ph.b == B and (y % 2 == 1 or y + DEN_LAG < 3)


def early_products(ph, j):
    if ph.b == B - 1 and j >= 4:
        first, last = j - 4, j - 3
    elif ph.b == B and j < KT + TD:
        first, last = STEPS - 4 + j, STEPS - 3 + j
    elif ph.b == B and j == KT + TD:
        first, last = STEPS - 4 + j, EARLY * XH
    else:
        return []
    return [divmod(i, XH) for i in range(first, last)]


def vector_heads(ph):
    return UH if ph.b == -1 else WH


def split_at(ph, j):
    if j % 4 or not ph.within(-1, 14):
        return None
    if j == 20:
        return (2, 0) if ph.within(-1, 13) else None
    return (1, j // 4 + 1)


def cross_attention(nc, a, qo, wk_parts, ctxT_in, probs, wk_in, wk_loaded, ctxT_loaded, vo, vo_loaded,
                    early_ps):
    ctx = ExitStack()
    with ctx:
        def sb(name, shape, dt=F32):
            return ctx.enter_context(nc.sbuf_tensor(name, shape, dt))

        def sem(name):
            return ctx.enter_context(nc.semaphore(name))

        wk_hi, wk_lo = wk_parts[:, 0, :], wk_parts[:, 1, :]
        ctxT_hi = sb("xa_ctxT_hi", [P, 2, KT, KP], F32R)
        ctxT_lo = sb("xa_ctxT_lo", [P, 2, KT, KP], F32R)
        ctx_nat = sb("xa_ctx_nat", [KP, 2, KT, C])
        q_hi = sb("xa_q_hi", [P, 2, UH, T], F32R)
        q_lo = sb("xa_q_lo", [P, 2, UH, T], F32R)
        scores = sb("xa_scores", [P, STEPS, UH, T])
        p_hi = sb("xa_p_hi", [KP, UW], F32R)
        p_lo = sb("xa_p_lo", [KP, UW], F32R)
        nat_hi = sb("xa_nat_hi", [KP, KT // 3, C], F32R)
        nat_lo = sb("xa_nat_lo", [KP, KT // 3, C], F32R)
        sq = sb("xa_sq", [KP, 2, WH * XD])
        cmax = sb("xa_cmax", [P, 2, UW])
        gmax = sb("xa_gmax", [KP, 2, UW])
        den = sb("xa_den", [KP, 2, UW])
        rden = sb("xa_rden", [P, UW])
        ss = sb("xa_ss", [KP, KT, XH])
        lg = sb("xa_lg", [KP, KT // 2, XH])
        nt = lg
        rk = sb("xa_rk", [KP, 2, KT, XH])
        ones = sb("xa_ones", [KP, P])
        spare = sb("xa_spare", [KP, 1])
        k_ps = ctx.enter_context(nc.psum_tensor("xa_k_ps", [P, 2, 2, 512], F32))
        s_ps = ctx.enter_context(nc.psum_tensor("xa_s_ps", [P, 2, 512], F32))
        o_ps = ctx.enter_context(nc.psum_tensor("xa_o_ps", [P, 2, 512], F32))

        def score_slot(j):
            return scores[0:KP, j % STEPS, :, :].rearrange("p h q -> p (h q)")

        def squares(ph, j):
            if ph.b == -1:
                slot = KT + 4 * (j % 2)
                return scores[0:KP, slot:slot + 3, :, :].rearrange("p s h q -> p (s h q)")[:, 0:UH * XD]
            return sq[:, j % 2, :]

        wk_hi_ready, wk_lo_ready, ones_set = (
            sem("xa_wk_hi_ready"), sem("xa_wk_lo_ready"), sem("xa_ones_set"))
        nat_loaded = [sem(f"xa_nat_loaded{i}") for i in range(2)]
        hi_ready, lo_ready = sem("xa_hi_ready"), sem("xa_lo_ready")
        qhi_ready, qlo_ready = sem("xa_qhi_ready"), sem("xa_qlo_ready")
        k_done, squared, summed = sem("xa_k_done"), sem("xa_squared"), sem("xa_summed")
        mean_ready, ln_ready, table_ready, rk_ready = (
            sem("xa_mean_ready"), sem("xa_ln_ready"), sem("xa_table_ready"), sem("xa_rk_ready"))
        den_ln, den_table, den_step = (
            sem("xa_den_ln"), sem("xa_den_table"), sem("xa_den_step"))
        newton = sem("xa_newton")
        s_done, s_taken = sem("xa_s_done"), sem("xa_s_taken")
        max_done, gmax_ready = sem("xa_max_done"), sem("xa_gmax_ready")
        shift_done, exp_done, den_done, pv_done = (
            sem("xa_shift_done"), sem("xa_exp_done"), sem("xa_den_done"), sem("xa_pv_done"))
        p_hi_ready, p_lo_ready = sem("xa_p_hi_ready"), sem("xa_p_lo_ready")
        nat_hi_ready, nat_lo_ready = sem("xa_nat_hi_ready"), sem("xa_nat_lo_ready")
        o_taken = sem("xa_o_taken")
        block = ctx.enter_context(nc.Block())

        def nat_loads(ph):
            return 16 * (ph.b // 2 + 1) if ph.b is not None else ph.pair * 16 + 16 * (ph.i // 2 + 1)

        def add_den(eng, ph, y):
            hy = (y // KT) % 2
            wait(eng, exp_done, ph.at(STEPS, y + 1))
            if y % KT == 1:
                closing = ph if y > 0 else ph.shift(-1)
                if closing.b is None or 2 * closing.b + hy >= 2:
                    wait(eng, s_done, pos_d(closing, hy) + 1)
                eng.tensor_tensor(den[:, hy, :], probs[0:KP, y % NPR, :], probs[0:KP, (y - 1) % NPR, :], ALU.add
                                  ).then_inc(den_done, 2)
            else:
                wait(eng, den_done, ph.at(STEPS, y))
                eng.tensor_tensor(den[:, hy, :], probs[0:KP, y % NPR, :], den[:, hy, :], ALU.add
                                  ).then_inc(den_done, 1)

        @block.sync
        def _(sp):
            def load_ctxT(ph):
                src = a.ctxT[ph.b] if ph.b is not None else a.ctxT[bass.ds(ph.at(1, 0), 1)].rearrange("o c k -> (o c) k")
                sp.dma_start(ctxT_in[:, ph.parity(), :, :].rearrange("c t p -> c (t p)"), src
                             ).then_inc(ctxT_loaded[ph.parity()], 16)

            def load_nat(ph):
                src = a.ctx[ph.b].rearrange("(p t) c -> p (t c)", t=KT) if ph.b is not None else \
                    a.ctx[bass.ds(ph.at(1, 0), 1)].rearrange("o (p t) c -> (o p) (t c)", t=KT)
                sp.dma_start(ctx_nat[:, ph.parity(), :, :].rearrange("p t c -> p (t c)"), src
                             ).then_inc(nat_loaded[ph.parity()], 16)

            def body(ph):
                if ph.within(-1, 14):
                    wait(sp, pv_done, ph.at(STEPS, 0))
                    load_nat(ph.shift(1))
                if ph.within(-1, 12):
                    wait(sp, hi_ready, ph.at(KT // 2, KT))
                    wait(sp, lo_ready, ph.at(KT // 2, KT))
                    load_ctxT(ph.shift(3))
                if ph.b == B - 1:
                    sp.wait_ge(k_done, STEPS * B)
                    sp.dma_start(vo[:, :, :], a.vo).then_inc(vo_loaded, 16)

            each_phase(sp, body, 12)

        @block.gpsimd
        def _(pool):
            pool.memset(ones[:, :], 1.0).then_inc(ones_set, 1)
            pool.wait_ge(ones_set, 1)

            def q_low(ph, h):
                pool.wait_ge(qhi_ready, ph.at(2, h + 1))
                pool.tensor_tensor(q_lo[:, h, :, :], qo[:, UH * h:UH * h + UH, ph.tokens()],
                                   q_hi[:, h, :, :].bitcast(F32), ALU.subtract).then_inc(qlo_ready, 1)

            def body(ph):
                if ph.b == -1:
                    q_low(Phase(0), 0)
                    return
                for j in range(STEPS):
                    h, t = divmod(j, KT)
                    y = lagged(ph, j, SHIFT_LAG)
                    if y is not None and not vector_shifts(ph, y):
                        if y % KT == 0:
                            pool.wait_ge(gmax_ready, ph.at(2, y // KT + 1))
                        if ph.b == B - 1:
                            pool.wait_ge(shift_done, ph.at(STEPS, y))
                        pool.tensor_tensor(score_slot(y), score_slot(y), gmax[:, (y // KT) % 2, :],
                                           ALU.subtract).then_inc(shift_done, 1)
                    y = lagged(ph, j, DEN_LAG)
                    if y is not None and y % KT and not vector_adds(ph, y):
                        add_den(pool, ph, y)
                    if ph.within(0, 15) and t == KT - 1:
                        wait(pool, max_done, ph.at(2 * (KT - 1), (KT - 1) * (h + 1)))
                        wait(pool, shift_done, ph.at(STEPS, KT * (h - 1)))
                        pool.tensor_tensor(spare[:, :], ones[:, 0:1], ones[:, 1:2], ALU.mult)
                        pool.partition_all_reduce(gmax[:, h, :], cmax[0:KP, h, :], KP, bass_max
                                                  ).then_inc(gmax_ready, 1)
                    if t == 6 and ph.within(0, 15) and not (ph.b == 15 and h == 1):
                        q_low(ph.shift(h), 1 - h)

            each_phase(pool, body, 14)

        @block.scalar
        def _(act):
            def q_high(ph, h):
                act.activation(q_hi[:, h, :, :], qo[:, UH * h:UH * h + UH, ph.tokens()], ACT.Copy
                               ).then_inc(qhi_ready, 1)

            def split_high(ph, c):
                i = ph.parity()
                act.wait_ge(ctxT_loaded[i], 16 * (ph.b // 2 + 1) if ph.b is not None else
                            ph.pair * 16 + 16 * (ph.i // 2 + 1))
                if ph.within(2, B):
                    act.wait_ge(s_done, pos_s(ph.shift(-2), KT + 2 * c + 1) + 1)
                act.activation(ctxT_hi[:, i, 2 * c:2 * c + 2, :], ctxT_in[:, i, 2 * c:2 * c + 2, :],
                               ACT.Copy).then_inc(hi_ready, 1)

            def body(ph):
                for j in range(STEPS):
                    h, t = divmod(j, KT)
                    if split_at(ph, j):
                        ahead, c = split_at(ph, j)
                        split_high(ph.shift(ahead), c)
                    if ph.within(-1, 14):
                        wait(act, k_done, ph.at(STEPS, STEPS + j + 1))
                        wait(act, summed, ph.at(STEPS, STEPS + j - 1))
                        k_cols = k_ps[0:KP, j % 2, :, :].rearrange("p k n -> p (k n)")
                        for g in range(vector_heads(ph), UH):
                            head = UH * (j % 2) + g
                            own = k_cols[:, g * XD:(g + 1) * XD]
                            act.activation(own, own, ACT.Square,
                                           accum_out=ss[:, j // 2, head:head + 1])
                        act.activation(squares(ph, j), k_cols[:, 0:vector_heads(ph) * XD], ACT.Square
                                       ).then_inc(squared, 1)
                    if closes(ph, j):
                        n = ph.at(2, h - 1)
                        act.wait_ge(s_done, pos_d(ph, h) + 1)
                        wait(act, o_taken, ph.at(2, h - 2))
                        act.activation(rden[:, :], s_ps[:, bank_d(ph, h), 0:UW], ACT.Ln).then_inc(den_ln, 1)
                        act.wait_ge(den_ln, n)
                        act.activation(rden[:, :], rden[:, :], ACT.Exp, scale=-1.0).then_inc(den_table, 1)
                    y = lagged(ph, j, EXP_LAG)
                    if y is not None:
                        wait(act, shift_done, ph.at(STEPS, y + 1))
                        wait(act, pv_done, ph.at(STEPS, y - NPR + 1))
                        wait(act, den_done, ph.at(STEPS, y - NPR + 1))
                        if in_parts(ph, y - NPR):
                            wait(act, p_lo_ready, parts_count(ph, y - NPR))
                        act.activation(probs[0:KP, y % NPR, :], score_slot(y), ACT.Exp).then_inc(exp_done, 1)
                        if in_parts(ph, y):
                            wait(act, exp_done, ph.at(STEPS, y + 1))
                            wait(act, pv_done, ph.at(STEPS, y - 2))
                            act.activation(p_hi[:, :], probs[0:KP, y % NPR, :], ACT.Copy
                                           ).then_inc(p_hi_ready, 1)
                    if nat_split_at(ph, j) is not None:
                        tile = nat_split_at(ph, j)
                        if tile == 2:
                            act.wait_ge(nat_loaded[ph.parity()], nat_loads(ph))
                        wait(act, pv_done, ph.at(STEPS, tile + 1 - KT))
                        act.activation(nat_hi[:, tile // 3, :], ctx_nat[:, ph.parity(), tile, :], ACT.Copy
                                       ).then_inc(nat_hi_ready, 1)
                    for step, ahead, g in ((13, 1, slice(0, 6)), (1, 0, slice(6, 12))):
                        if j == step and ph.shift(ahead).within(0, 15):
                            n = ph.at(2, 3 if ahead else 2)
                            act.wait_ge(mean_ready, n)
                            act.activation(lg[:, :, :], ss[:, g, :], ACT.Ln).then_inc(ln_ready, 1)
                            act.wait_ge(ln_ready, n)
                            act.activation(rk[:, ph.shift(ahead).parity(), g, :], lg[:, :, :], ACT.Exp, scale=-0.5
                                           ).then_inc(table_ready, 1)
                    if t == 4 and ph.within(0, 15) and not (ph.b == 15 and h == 1):
                        if h == 1:
                            act.wait_ge(s_done, pos_s(ph, KT - 1) + 1)
                        elif ph.b != 0:
                            act.wait_ge(s_done, pos_s(ph.shift(-1), STEPS - 1) + 1)
                        q_high(ph.shift(h), 1 - h)

            act.wait_ge(wk_loaded, 16)
            split_high(Phase(0), 0)
            for c in range(4):
                part = slice(c * 512, (c + 1) * 512)
                act.activation(wk_hi[:, part], wk_in[:, part], ACT.Copy).then_inc(wk_hi_ready, 1)
            q_high(Phase(0), 0)
            each_phase(act, body, 14)

        @block.vector
        def _(dve):
            def split_low(ph, c):
                i = ph.parity()
                dve.wait_ge(hi_ready, ph.at(KT // 2, c + 1))
                dve.tensor_tensor(ctxT_lo[:, i, 2 * c:2 * c + 2, :], ctxT_in[:, i, 2 * c:2 * c + 2, :],
                                  ctxT_hi[:, i, 2 * c:2 * c + 2, :].bitcast(F32), ALU.subtract).then_inc(lo_ready, 1)

            def body(ph):
                for j in range(STEPS):
                    h, t = divmod(j, KT)
                    if ph.within(0, 15):
                        wait(dve, s_done, pos_s(ph, j) + 1)
                        if j in (0, 6):
                            dve.wait_ge(rk_ready, ph.at(2, 1 + j // 6))
                        wait(dve, exp_done, ph.at(STEPS, j - STEPS + 1))
                        dve.tensor_tensor(scores[0:KP, j, :, :],
                                          s_ps[0:KP, bank_s(ph, j), 0:UW].rearrange("p (g q) -> p g q", q=T),
                                          rk[:, ph.parity(), t, UH * h:UH * h + UH].unsqueeze(2)
                                          .broadcast_to([KP, UH, T]), ALU.mult).then_inc(s_taken, 1)
                    if (ph.within(-1, 14) and j >= 1) or (ph.within(0, 15) and j == 0):
                        i = (j - 1) % STEPS
                        of = ph if j >= 1 else ph.shift(-1)
                        dve.wait_ge(squared, ph.at(STEPS, STEPS + j))
                        dve.tensor_reduce(ss[:, i // 2, UH * (i % 2):UH * (i % 2) + vector_heads(of)],
                                          squares(of, i).rearrange("p (g d) -> p g d", d=XD), AX.X, ALU.add
                                          ).then_inc(summed, 1)
                    if ph.within(0, 15) and t >= 1:
                        dve.wait_ge(s_taken, pos_s(ph, j) + 1)
                        if t == 1:
                            wait(dve, gmax_ready, ph.at(2, h - 1))
                            dve.tensor_tensor(cmax[0:KP, h, :], score_slot(j), score_slot(j - 1), ALU.max
                                              ).then_inc(max_done, 1)
                        else:
                            wait(dve, max_done, ph.at(2 * (KT - 1), (KT - 1) * h + t - 1))
                            dve.tensor_tensor(cmax[0:KP, h, :], score_slot(j), cmax[0:KP, h, :], ALU.max
                                              ).then_inc(max_done, 1)
                    for step, ahead, g in ((13, 1, slice(0, 6)), (1, 0, slice(6, 12))):
                        if not ph.shift(ahead).within(0, 15):
                            continue
                        n = 3 if ahead else 2
                        if j == step:
                            dve.wait_ge(summed, ph.at(STEPS, STEPS + KT if ahead else STEPS))
                            dve.tensor_scalar(ss[:, g, :], ss[:, g, :], 1.0 / XD, RMS_EPS, ALU.mult, ALU.add
                                              ).then_inc(mean_ready, 1)
                        if j == step + 1:
                            dve.wait_ge(table_ready, ph.at(2, n))
                            count = [0]

                            def link(ins):
                                count[0] += 1
                                ins.then_inc(newton, 1)
                                dve.wait_ge(newton, ph.at(6, 3 * (n - 1) + count[0]))

                            rsqrt_refine(dve, link, rk[:, ph.shift(ahead).parity(), g, :], ss[:, g, :], nt[:, :, :],
                                         XD ** -0.5).then_inc(rk_ready, 1)
                    y = lagged(ph, j, SHIFT_LAG)
                    if y is not None and vector_shifts(ph, y):
                        if y % KT == 0:
                            dve.wait_ge(gmax_ready, ph.at(2, y // KT + 1))
                        dve.wait_ge(shift_done, ph.at(STEPS, y))
                        dve.tensor_tensor(score_slot(y), score_slot(y), gmax[:, (y // KT) % 2, :],
                                          ALU.subtract).then_inc(shift_done, 1)
                    y = lagged(ph, j, DEN_LAG)
                    if y is not None and y % KT and vector_adds(ph, y):
                        add_den(dve, ph, y)
                    y = lagged(ph, j, DEN_LAG)
                    if y is not None and in_parts(ph, y):
                        dve.wait_ge(p_hi_ready, parts_count(ph, y))
                        dve.tensor_tensor(p_lo[:, :], probs[0:KP, y % NPR, :], p_hi[:, :].bitcast(F32), ALU.subtract
                                          ).then_inc(p_lo_ready, 1)
                    if nat_split_at(ph, j) is not None:
                        tile = nat_split_at(ph, j)
                        dve.wait_ge(nat_hi_ready, ph.at(KT // 3, tile // 3 + 1))
                        dve.tensor_tensor(nat_lo[:, tile // 3, :], ctx_nat[:, ph.parity(), tile, :],
                                          nat_hi[:, tile // 3, :].bitcast(F32), ALU.subtract).then_inc(nat_lo_ready, 1)
                    if closes(ph, j):
                        rd = cmax[:, 1 - h, :]
                        dve.wait_ge(gmax_ready, ph.at(2, h) if ph.b is None else min(ph.at(2, h), 2 * B))
                        dve.wait_ge(den_table, ph.at(2, h - 1))
                        dve.tensor_tensor(rd, s_ps[:, bank_d(ph, h), 0:UW], rden[:, :], ALU.mult
                                          ).then_inc(s_taken, 1)
                        dve.wait_ge(s_taken, pos_d(ph, h) + 1)
                        dve.scalar_tensor_tensor(rden[:, :], rd, 2.0, rden[:, :], ALU.subtract, ALU.mult
                                                 ).then_inc(den_step, 1)
                        dve.wait_ge(den_step, ph.at(2, h - 1))
                        dve.wait_ge(pv_done, ph.at(STEPS, KT * (h - 1)))
                        dve.scalar_tensor_tensor(qo[:, UH * h:UH * h + UH, ph.shift(-1).tokens()],
                                                 o_ps[:, h, 0:UW].rearrange("p (g q) -> p g q", q=T), -1.0,
                                                 rden[:, :].rearrange("p (g q) -> p g q", q=T), ALU.mult, ALU.mult
                                                 ).then_inc(o_taken, 1)
                    if split_at(ph, j):
                        ahead, c = split_at(ph, j)
                        split_low(ph.shift(ahead), c)

            dve.wait_ge(wk_loaded, 16)
            split_low(Phase(0), 0)
            for c in range(4):
                part = slice(c * 512, (c + 1) * 512)
                dve.wait_ge(wk_hi_ready, c + 1)
                dve.tensor_tensor(wk_lo[:, part], wk_in[:, part], wk_hi[:, part].bitcast(F32), ALU.subtract
                                  ).then_inc(wk_lo_ready, 1)
            each_phase(dve, body, 14)

        @block.tensor
        def _(pe):
            def three(out, l_hi, l_lo, r_hi, r_lo):
                pe.matmul(out, l_hi, r_hi, start=True, stop=False)
                pe.matmul(out, l_hi, r_lo, start=False, stop=False)
                return pe.matmul(out, l_lo, r_hi, start=False, stop=True)

            def project_k(ph, j, c):
                if ph.b == -1 and j < 2:
                    pe.wait_ge(wk_lo_ready, 2 * j + c + 1)
                i, t, cols = ph.shift(1).parity(), j // 2, slice((2 * (j % 2) + c) * 512, (2 * (j % 2) + c + 1) * 512)
                return three(k_ps[0:KP, j % 2, c, :], ctxT_hi[:, i, t, :], ctxT_lo[:, i, t, :],
                             wk_hi[:, cols], wk_lo[:, cols])

            def body(ph):
                for j in range(STEPS):
                    h, t = divmod(j, KT)
                    if ph.within(-1, 14):
                        if j % 4 == 0:
                            pe.wait_ge(hi_ready, ph.at(KT // 2, KT // 2 + j // 4 + 1))
                            pe.wait_ge(lo_ready, ph.at(KT // 2, KT // 2 + j // 4 + 1))
                        wait(pe, squared, ph.at(STEPS, STEPS + j - 1))
                        project_k(ph, j, 0)
                    if ph.within(0, 15):
                        if t == 0:
                            pe.wait_ge(qhi_ready, ph.at(2, h + 1))
                            pe.wait_ge(qlo_ready, ph.at(2, h + 1))
                        wait(pe, s_taken, pos_s(ph, j) - 1)
                        i = ph.parity()
                        three(s_ps[0:KP, bank_s(ph, j), 0:UW], ctxT_hi[:, i, t, :], ctxT_lo[:, i, t, :],
                              q_hi[:, h, :, :].rearrange("p g q -> p (g q)"),
                              q_lo[:, h, :, :].rearrange("p g q -> p (g q)")).then_inc(s_done, 1)
                    if closes(ph, j):
                        pe.wait_ge(den_done, ph.at(STEPS, KT * (h - 1)))
                        wait(pe, s_taken, pos_d(ph, h) - 1)
                        pe.matmul(s_ps[:, bank_d(ph, h), 0:UW], ones[:, :], den[:, h, :], start=True, stop=True
                                  ).then_inc(s_done, 1)
                    if ph.within(-1, 14):
                        project_k(ph, j, 1).then_inc(k_done, 1)
                    y = lagged(ph, j, PV_LAG)
                    if y is not None:
                        ty, hy, of = y % KT, (y // KT) % 2, ph.shift(y // STEPS)
                        if ty == 0:
                            wait(pe, o_taken, ph.at(2, y // KT - 1))
                            if hy == 0:
                                pe.wait_ge(nat_loaded[of.parity()], nat_loads(of))
                        if in_parts(ph, y):
                            if hy == 0:
                                pe.wait_ge(nat_lo_ready, of.at(KT // 3, ty // 3 + 1))
                            pe.wait_ge(p_lo_ready, parts_count(ph, y))
                            out, c = o_ps[:, hy, 0:UW], ty // 3
                            pe.matmul(out, nat_hi[:, c, :], p_hi[:, :], start=False, stop=False)
                            pe.matmul(out, nat_hi[:, c, :], p_lo[:, :], start=False, stop=False)
                            pe.matmul(out, nat_lo[:, c, :], p_hi[:, :], start=False, stop=(ty == KT - 1)
                                      ).then_inc(pv_done, 1)
                        else:
                            wait(pe, exp_done, ph.at(STEPS, y + 1))
                            pe.matmul(o_ps[:, hy, 0:UW], ctx_nat[:, of.parity(), ty, :], probs[0:KP, y % NPR, :],
                                      start=(ty == 0), stop=(ty == KT - 1)).then_inc(pv_done, 1)
                    for n, head in early_products(ph, j):
                        if n == 0 and head == 0:
                            pe.wait_ge(vo_loaded, 16)
                            pe.wait_ge(squared, STEPS * B)
                        pe.matmul(early_ps[:, n, 0:E], qo[:, head, n * P:(n + 1) * P], vo[:, head, :],
                                  start=(head == 0), stop=(head == XH - 1))

            pe.wait_ge(ones_set, 1)
            each_phase(pe, body, 14)


def output_and_mlp(nc, a, qo, hT_hi, hT_lo, vo, vo_lo, early_ps):
    ctx = ExitStack()
    with ctx:
        def sb(name, shape, dt=F32):
            return ctx.enter_context(nc.sbuf_tensor(name, shape, dt))

        def sem(name):
            return ctx.enter_context(nc.semaphore(name))

        FC = FF // P
        NHB = 4
        vo_hi = sb("om_vo_hi", [P, XH, E], F32R)
        q_hi = sb("om_q_hi", [P, 4, UH, P], F32R)
        q_lo = sb("om_q_lo", [P, 4, UH, P], F32R)
        w1_hi = sb("om_w1_hi", [P, EC, FF], F32R)
        w1 = overlay(nc, "om_w1", [P, EC, FF])
        w1_lo = sb("om_w1_lo", [P, EC, FF], F32R)
        w2_hi = sb("om_w2_hi", [P, FC, E], F32R)
        w2 = overlay(nc, "om_w2", [P, FC, E])
        w2_lo = sb("om_w2_lo", [P, FC, E], F32R)
        b1 = sb("om_b1", [P, FC])
        b2 = sb("om_b2", [P, E])
        ident = sb("om_ident", [P, P])
        x1 = sb("om_x1", [P, NT, E])
        z = sb("om_z", [P, NT, E])
        x2T_hi = sb("om_x2T_hi", [P, EC, TOK], F32R)
        x2T_lo = sb("om_x2T_lo", [P, EC, TOK], F32R)
        xb = sb("om_xb", [P, NT, E])
        h_in = sb("om_h", [P, NHB, UW])
        stat = sb("om_stat", [P, NT, 6])
        mv = sb("om_mv", [P, NT, 2])
        lna = sb("om_lna", [P, 2, NT])
        lnl = sb("om_lnl", [P, 2, NT])
        lny = sb("om_lny", [P, 2, NT])
        lnt = sb("om_lnt", [P, 2, NT])
        ps = ctx.enter_context(nc.psum_tensor("om_ps", [P, 8, 512], F32))
        x1_loaded, w_loaded, b_loaded = sem("om_x1_loaded"), sem("om_w_loaded"), sem("om_b_loaded")
        vo_lo_ready = [sem("om_vo_lo_even"), sem("om_vo_lo_odd")]
        vo_hi_ready, q_hi_ready, q_lo_ready, w_hi_ready, w_lo_ready = (
            sem("om_vo_hi_ready"), sem("om_q_hi_ready"), sem("om_q_lo_ready"),
            sem("om_w_hi_ready"), sem("om_w_lo_ready"))
        z_mm, stat_ready, ln_a, ln_l, ln_y, x2_ready, xb_ready = (
            sem("om_z_mm"), sem("om_stat_ready"), sem("om_ln_a"),
            sem("om_ln_l"), sem("om_ln_y"), sem("om_x2_ready"), sem("om_xb_ready"))
        x2T_mm, x2T_hi_ready, x2T_lo_ready, h_mm, h_ready, h_hi_ready, h_lo_ready, y_mm, out_ready, stored, dve_chain = (
            sem("om_x2T_mm"), sem("om_x2T_hi_ready"), sem("om_x2T_lo_ready"), sem("om_h_mm"), sem("om_h_ready"),
            sem("om_h_hi_ready"), sem("om_h_lo_ready"), sem("om_y_mm"),
            sem("om_out_ready"), sem("om_stored"), sem("om_dve_chain"))
        GROUPS = ((0, 4), (4, 7)), ((0, 4), (4, 6), (6, 7))
        TURN_BEFORE = 3
        HALF_TILES = (4, NT)
        block = ctx.enter_context(nc.Block())

        def turn_bank(n):
            return n if n < 4 else (0, 1, 7)[n - 4]

        @block.sync
        def _(sp):
            sp.dma_start(x1[:, :, :], a.x1.rearrange("(n p) e -> p n e", p=P)).then_inc(x1_loaded, 16)
            sp.dma_start(ident[:, :], a.ident).then_inc(x1_loaded, 16)
            sp.dma_start(w1[:, :, :], a.w1T.rearrange("(k p) f -> p k f", p=P)).then_inc(w_loaded, 16)
            sp.dma_start(w2[:, :, :], a.w2T.rearrange("(k p) e -> p k e", p=P)).then_inc(w_loaded, 16)
            sp.dma_start(b1[:, :], a.b1).then_inc(b_loaded, 16)
            sp.dma_start(b2[:, :], a.b2.partition_broadcast(P)).then_inc(b_loaded, 16)
            for n in range(NT):
                sp.wait_ge(out_ready, n + 1)
                sp.dma_start(a.out[n * P:(n + 1) * P, :], z[:, n, :]).then_inc(stored, 16)
            sp.wait_ge(stored, 16 * NT)

        def q_pieces(n):
            heads = UH if n > EARLY else UH // 2
            out = []
            for piece in range(XH // heads):
                h = piece * heads
                m, g = (2 * n + h // UH) % 4, slice(h % UH, h % UH + heads)
                out.append((q_hi[:, m, g, :], q_lo[:, m, g, :], qo[:, h:h + heads, n * P:(n + 1) * P], piece))
            return out

        def q_piece_count(n, h):
            return 2 * (n - EARLY) + 3 + h // UH if n > EARLY else h // (UH // 2) + 1

        def vo_low(eng, c):
            eng.wait_ge(vo_hi_ready, c + 1)
            eng.tensor_tensor(vo_lo[:, 2 * c:2 * c + 2, :], vo[:, 2 * c:2 * c + 2, :],
                              vo_hi[:, 2 * c:2 * c + 2, :].bitcast(F32), ALU.subtract).then_inc(vo_lo_ready[c % 2], 1)

        @block.gpsimd
        def _(pool):
            for c in range(1, XH // 2, 2):
                vo_low(pool, c)
            for i, (w, hi, lo) in enumerate(((w1, w1_hi, w1_lo), (w2, w2_hi, w2_lo))):
                pool.wait_ge(w_hi_ready, i + 1)
                pool.tensor_tensor(lo[:, :, :], w[:, :, :], hi[:, :, :].bitcast(F32), ALU.subtract).then_inc(w_lo_ready, 1)
            pool.wait_ge(b_loaded, 32)
            for n in range(NT):
                pool.wait_ge(x2_ready, n + 1)
                pool.tensor_tensor(xb[:, n, :], z[:, n, :], b2[:, :], ALU.add).then_inc(xb_ready, 1)

        @block.scalar
        def _(act):
            def q_high(n):
                for hi, _, src, piece in q_pieces(n):
                    if n >= EARLY + 2:
                        act.wait_ge(z_mm, n - EARLY - 1)
                    act.activation(hi, src, ACT.Copy).then_inc(q_hi_ready, 1)
                    if n == EARLY:
                        for c in (2 * piece, 2 * piece + 1):
                            act.activation(vo_hi[:, 2 * c:2 * c + 2, :], vo[:, 2 * c:2 * c + 2, :],
                                           ACT.Copy).then_inc(vo_hi_ready, 1)

            def table(i, g, count):
                tiles = slice(*GROUPS[i][g])
                act.wait_ge(ln_a, count)
                act.activation(lnl[:, i, tiles], lna[:, i, tiles], ACT.Ln).then_inc(ln_l, 1)
                act.wait_ge(ln_l, count)
                act.activation(lny[:, i, tiles], lnl[:, i, tiles], ACT.Exp, scale=-0.5).then_inc(ln_y, 1)

            def x2T_high(n):
                act.wait_ge(x2T_mm, n + 1)
                act.activation(x2T_hi[:, :, n * P:(n + 1) * P],
                               ps[:, turn_bank(n), 0:EC * P].rearrange("p (k t) -> p k t", k=EC),
                               ACT.Copy).then_inc(x2T_hi_ready, 1)

            for n in range(EARLY, NT):
                q_high(n)
                if n in (EARLY + 2, EARLY + 3):
                    act.wait_ge(w_loaded, 32)
                    w, hi = ((w1, w1_hi), (w2, w2_hi))[n - EARLY - 2]
                    act.activation(hi[:, :, :], w[:, :, :], ACT.Copy).then_inc(w_hi_ready, 1)
            table(0, 0, 1)
            for n in range(0, 4):
                x2T_high(n)
            table(0, 1, 2)
            act.wait_ge(b_loaded, 32)
            for m in range(2 * FC):
                n, f = divmod(m, FC)
                if m == TURN_BEFORE:
                    for tile in range(4, NT):
                        x2T_high(tile)
                act.wait_ge(h_mm, m + 1)
                if m >= NHB:
                    act.wait_ge(h_lo_ready, m - NHB + 1)
                act.activation(h_in[:, m % NHB, :], ps[:, 2 + m % 4, 0:UW], ACT.Gelu,
                               bias=b1[:, f:f + 1]).then_inc(h_ready, 1)
                if m % 2:
                    continue
                act.wait_ge(h_ready, m + 1)
                if m == 0:
                    act.wait_ge(q_lo_ready, q_piece_count(NT - 1, XH - 1))
                act.activation(hT_hi[:, f, n * UW:(n + 1) * UW], h_in[:, m % NHB, :], ACT.Copy
                               ).then_inc(h_hi_ready, 1)
            act.preload_act_table_set(TABLES)
            for g in range(3):
                table(1, g, 3 + g)

        @block.vector
        def _(dve):
            link = linker(dve, dve_chain)

            def q_low(n):
                for hi, lo, src, piece in q_pieces(n):
                    dve.wait_ge(q_hi_ready, q_piece_count(n, 0) + piece)
                    dve.tensor_tensor(lo, src, hi.bitcast(F32), ALU.subtract).then_inc(q_lo_ready, 1)
                    if n == EARLY:
                        vo_low(dve, 2 * piece)

            def stats(i, n, sums, other):
                link(dve.tensor_tensor(z[:, n, :], sums, other[:, n, :], ALU.add))
                link(dve.bn_stats(stat[:, n, :], z[:, n, :]))
                dve.bn_aggr(mv[:, n, :], stat[:, n, :]).then_inc(stat_ready, 1)

            def variances(i, g):
                tiles = slice(*GROUPS[i][g])
                dve.wait_ge(stat_ready, NT * i + tiles.stop)
                dve.tensor_scalar(lna[:, i, tiles], mv[:, tiles, 1], LN_EPS, None, ALU.add).then_inc(ln_a, 1)

            def normalise(i, g, count):
                tiles = slice(*GROUPS[i][g])
                dve.wait_ge(ln_a, count)
                dve.wait_ge(ln_y, count)
                link(rsqrt_refine(dve, link, lny[:, i, tiles], lna[:, i, tiles], lnt[:, i, tiles]))
                for n in range(*GROUPS[i][g]):
                    dve.tensor_scalar(z[:, n, :], z[:, n, :], mv[:, n, 0:1], lny[:, i, n:n + 1],
                                      ALU.subtract, ALU.mult).then_inc(out_ready if i else x2_ready, 1)

            def x2T_low(n):
                dve.wait_ge(x2T_hi_ready, n + 1)
                dve.tensor_tensor(x2T_lo[:, :, n * P:(n + 1) * P],
                                  ps[:, turn_bank(n), 0:EC * P].rearrange("p (k t) -> p k t", k=EC),
                                  x2T_hi[:, :, n * P:(n + 1) * P].bitcast(F32), ALU.subtract).then_inc(x2T_lo_ready, 1)

            q_low(EARLY)
            q_low(EARLY + 1)
            dve.wait_ge(x1_loaded, 32)
            for n in range(EARLY):
                stats(0, n, early_ps[:, n, 0:E], x1)
            for n in range(EARLY, NT):
                if n + 2 < NT:
                    q_low(n + 2)
                dve.wait_ge(z_mm, n - EARLY + 1)
                stats(0, n, ps[:, 4 + n % 4, 0:E], x1)
                if n == 3:
                    variances(0, 0)
                if n == 4:
                    normalise(0, 0, 1)
                if n == 5:
                    for tile in range(0, 4):
                        x2T_low(tile)
            variances(0, 1)
            normalise(0, 1, 2)
            for m in range(2 * FC):
                n, f = divmod(m, FC)
                if m == TURN_BEFORE:
                    for tile in range(4, NT):
                        x2T_low(tile)
                if m % 2:
                    dve.wait_ge(h_ready, m + 1)
                    link(dve.tensor_copy(hT_hi[:, f, n * UW:(n + 1) * UW], h_in[:, m % NHB, :]))
                else:
                    dve.wait_ge(h_hi_ready, m // 2 + 1)
                dve.tensor_tensor(hT_lo[:, f, n * UW:(n + 1) * UW], h_in[:, m % NHB, :],
                                  hT_hi[:, f, n * UW:(n + 1) * UW].bitcast(F32), ALU.subtract).then_inc(h_lo_ready, 1)
            for n in range(NT):
                dve.wait_ge(xb_ready, n + 1)
                dve.wait_ge(y_mm, n + 1)
                stats(1, n, ps[:, (6, 7, 0, 1)[n % 4], 0:E], xb)
                for g in range(3):
                    if n == GROUPS[1][g][1] - 1:
                        variances(1, g)
                        normalise(1, g, 3 + g)

        @block.tensor
        def _(pe):
            def three(out, l_hi, l_lo, r_hi, r_lo, first, last):
                pe.matmul(out, l_hi, r_hi, start=first, stop=False)
                pe.matmul(out, l_hi, r_lo, start=False, stop=False)
                return pe.matmul(out, l_lo, r_hi, start=False, stop=last)

            def project_out(n):
                if n >= EARLY + 4:
                    pe.wait_ge(stat_ready, n - 3)
                for h in range(XH):
                    if h % (UH // 2) == 0:
                        pe.wait_ge(q_hi_ready, q_piece_count(n, h))
                        pe.wait_ge(q_lo_ready, q_piece_count(n, h))
                    if n == EARLY:
                        pe.wait_ge(vo_lo_ready[(h // 2) % 2], h // 4 + 1)
                    m = (2 * n + h // UH) % 4
                    mm = three(ps[:, 4 + n % 4, 0:E], q_hi[:, m, h % UH, :], q_lo[:, m, h % UH, :],
                               vo_hi[:, h, :], vo_lo[:, h, :], h == 0, h == XH - 1)
                mm.then_inc(z_mm, 1)

            def turn(n):
                pe.wait_ge(x2_ready, n + 1)
                if n == 4:
                    pe.wait_ge(x2T_lo_ready, 2)
                for k in range(EC):
                    mm = pe.transpose(ps[:, turn_bank(n), k * P:(k + 1) * P], z[:, n, k * P:(k + 1) * P], ident[:, :])
                mm.then_inc(x2T_mm, 1)

            def up(n):
                pe.wait_ge(x2T_lo_ready, HALF_TILES[n])
                if n == 0:
                    pe.wait_ge(stat_ready, 6)
                    pe.wait_ge(w_lo_ready, 2)
                for f in range(FC):
                    m = n * FC + f
                    if m == TURN_BEFORE:
                        for tile in range(4, NT):
                            turn(tile)
                    if m >= 4:
                        pe.wait_ge(h_ready, m - 3)
                    for k in range(EC):
                        cols = slice(n * UW, (n + 1) * UW)
                        mm = three(ps[:, 2 + m % 4, 0:UW], w1_hi[:, k, f * P:(f + 1) * P],
                                   w1_lo[:, k, f * P:(f + 1) * P], x2T_hi[:, k, cols], x2T_lo[:, k, cols],
                                   k == 0, k == EC - 1)
                    mm.then_inc(h_mm, 1)

            for n in range(EARLY, NT - 1):
                project_out(n)
            pe.wait_ge(x1_loaded, 32)
            for n in range(4):
                turn(n)
            project_out(NT - 1)
            up(0)
            up(1)
            for n in range(NT):
                pe.wait_ge(h_lo_ready, FC if n < 3 else 2 * FC)
                if n >= 4:
                    pe.wait_ge(stat_ready, NT + n - 3)
                rows = slice(n * P, (n + 1) * P)
                for f in range(FC):
                    mm = three(ps[:, (6, 7, 0, 1)[n % 4], 0:E], hT_hi[:, f, rows], hT_lo[:, f, rows],
                               w2_hi[:, f, :], w2_lo[:, f, :], f == 0, f == FC - 1)
                mm.then_inc(y_mm, 1)


class Arrays:
    pass


def program(nc, a):
    with nc.psum_tensor("early_ps", [P, EARLY, 512], F32) as early_ps:
        pass
    with ExitStack() as outer:
        vo_loaded = outer.enter_context(nc.semaphore("vo_loaded"))
        with ExitStack() as ctx:
            qo = ctx.enter_context(nc.sbuf_tensor("qo", [P, XH, TOK], F32))
            vo = overlay(nc, "vo", [P, XH, E])
            wk_parts = ctx.enter_context(nc.sbuf_tensor("wk_parts", [P, 2, XH * XD], F32R))
            ctxT_in = ctx.enter_context(nc.sbuf_tensor("ctxT_in", [P, 2, KT, KP], F32))
            probs = ctx.enter_context(nc.sbuf_tensor("probs", [P, NPR, UW], F32))
            wk_in = probs[:, :, :].rearrange("p n q -> p (n q)")[:, 0:XH * XD]
            wk_loaded = ctx.enter_context(nc.semaphore("wk_loaded"))
            ctxT_loaded = [ctx.enter_context(nc.semaphore(f"ctxT_loaded{i}")) for i in range(2)]
            vo_stored = ctx.enter_context(nc.semaphore("vo_stored"))
            xT = overlay(nc, "xT", [P, EC, TOK])
            with nc.sbuf_tensor("x1T_lo", [P, EC, TOK], F32R) as x1T_lo, \
                    nc.sbuf_tensor("x1T_hi", [P, EC, TOK], F32R) as x1T_hi, \
                    nc.sbuf_tensor("xq_lo", [P, EC * XH * XD], F32R) as xq_lo, \
                    nc.sbuf_tensor("x_nat", [P, NT, E], F32) as x_nat, \
                    nc.sbuf_tensor("ident", [P, P], F32) as ident, nc.sbuf_tensor("gains", [P, 2], F32) as gains:
                self_attention(nc, a, ident, gains, x_nat, xT, x1T_hi, x1T_lo, qo, wk_parts, xq_lo, vo_stored)
                query_path(nc, a, ident, gains, x1T_hi, x1T_lo, qo, wk_parts, xq_lo, wk_in, ctxT_in, wk_loaded,
                           ctxT_loaded, x_nat, vo_stored)
            cross_attention(nc, a, qo, wk_parts, ctxT_in, probs, wk_in, wk_loaded, ctxT_loaded, vo, vo_loaded,
                            early_ps)
        hT_hi = outer.enter_context(nc.sbuf_tensor("hT_hi", [P, FF // P, TOK], F32R))
        hT_lo = outer.enter_context(nc.sbuf_tensor("hT_lo", [P, FF // P, TOK], F32R))
        vo_lo = outer.enter_context(nc.sbuf_tensor("vo_lo", [P, XH, E], F32R))
        output_and_mlp(nc, a, qo, hT_hi, hT_lo, vo, vo_lo, early_ps)


def kernel(**inputs):
    import numpy as np
    import concourse.bacc as bacc
    from concourse.bass_utils import run_bass_kernel_spmd

    g = {k: np.asarray(v) for k, v in inputs.items()}

    def heads_in(w):
        return w.transpose(1, 0, 2).reshape(E, NH * HD)

    def columns(v):
        return v.reshape(-1, P).T

    rows = np.arange(P)
    queries, keys = np.meshgrid(rows % 64, np.arange(T), indexing="ij")
    x = g["x"].reshape(TOK, E)
    ctx = g["ctx_1024"]
    host = {
        "x": x,
        "xT": x.T,
        "ctx": ctx,
        "ctxT": ctx.reshape(B, KP, KT, C).transpose(0, 3, 2, 1).reshape(B, C, SK),
        "sa_wq": heads_in(g["L0_attn_Wq"]), "sa_wk": heads_in(g["L0_attn_Wk"]), "sa_wv": heads_in(g["L0_attn_Wv"]),
        "sa_wo": g["L0_attn_Wo"],
        "sa_bias": np.stack([columns(g["L0_attn_" + n].reshape(-1)) for n in ("bq", "bk", "bv")], axis=1),
        "sa_bo": g["L0_attn_bo"],
        "xq_w": g["L0_xattn_Wq"], "xk_w": g["L0_xattn_Wk"], "xk_wT": g["L0_xattn_Wk"].T,
        "xv_wT": g["L0_xattn_Wv"].T, "xo_w": g["L0_xattn_Wo"],
        "gains": np.stack([g["L0_xattn_gq"], g["L0_xattn_gk"]], axis=1),
        "w1T": g["L0_ffn_proj1"].T, "b1": columns(g["L0_ffn_proj1_bias"]),
        "w2T": g["L0_ffn_proj2"].T, "b2": g["L0_ffn_proj2_bias"],
        "ident": np.eye(P, dtype=np.float32),
        "causal": np.where((keys > queries) & (queries < T), np.finfo(np.float32).min, 0).astype(np.float32),
        "parity": np.stack([(rows // HD + 1) % 2, rows // HD % 2], axis=1).astype(np.float32),
    }
    nc = bacc.Bacc("TRN2", target_bir_lowering=False, num_devices=1)
    a, arrays = Arrays(), {}
    for name, v in host.items():
        v = np.ascontiguousarray(v)
        arrays["in_" + name] = v
        a.__dict__[name] = nc.dram_tensor("in_" + name, v.shape, mybir.dt.from_np(v.dtype), kind="ExternalInput").ap()
    a.out = nc.dram_tensor("out", (TOK, E), F32, kind="ExternalOutput").ap()
    a.x1 = nc.dram_tensor("x1_scratch", (TOK, E), F32, kind="Internal").ap()
    a.vo = nc.dram_tensor("vo_scratch", (P, XH, E), F32, kind="Internal").ap()
    program(nc, a)
    r = run_bass_kernel_spmd(nc, [arrays], core_ids=[0])
    return r.results[0]["out"].reshape(B, T, E)
```
